# Optimizing a Trainium2 kernel written in Bass

```python
import numpy as np
import jax
import jax.numpy as jnp

def _softmax(x, axis=-1):
    return jax.nn.softmax(x, axis=axis)

def _gelu(x):
    return jax.nn.gelu(x, approximate=True)

def _silu(x):
    return jax.nn.silu(x)

def _sigmoid(x):
    return jax.nn.sigmoid(x)

def _layernorm(x, axis=-1, eps=1e-05):
    m = jnp.mean(x, axis=axis, keepdims=True)
    v = jnp.var(x, axis=axis, keepdims=True)
    return (x - m) / jnp.sqrt(v + eps)

def _scatter_add(tgt, idx, src, axis=0):
    return tgt.at[idx].add(src)

def _segment_sum(src, seg, n):
    return jax.ops.segment_sum(src, seg, n)
kernel_name = 'mk_early_fusion_embed_d1_tok_img768_r4_81f7aa'

def setup_inputs(seed: int=0):
    np.random.seed(seed)
    _w = jnp.asarray

    def _rec_inputs():
        import jax
        import jax.numpy as jnp
        _rk = jax.random.key(seed)
        x = -0.000111679 + 0.999904 * jax.random.normal(jax.random.fold_in(_rk, 1), (32, 3, 96, 96), jnp.float32)
        x_txt = jax.random.randint(jax.random.fold_in(_rk, 51), (32, 77), 0, 40470, jnp.int32)
        pos_S = jnp.broadcast_to(jnp.arange(77, dtype=jnp.int32), (77,))
        mask_BS_f1_0 = jnp.where(jnp.ones((32, 77), dtype=bool), 1.0, 0.0).astype(jnp.float32)
        return (x, x_txt, pos_S, mask_BS_f1_0)
    x, x_txt, pos_S, mask_BS_f1_0 = _rec_inputs()

    def _L0_tok_setup():
        import jax, jax.numpy as jnp
        import numpy as np
        PATCH = 10
        N_EMBD = 192
        EPS = 1e-05

        def _patchify(x, p):
            B, C, H, Wd = x.shape
            h_p, w_p = (H // p, Wd // p)
            x = x[:, :, :h_p * p, :w_p * p]
            x = x.reshape(B, C, h_p, p, w_p, p)
            x = x.transpose(0, 2, 4, 1, 3, 5)
            return x.reshape(B, h_p * w_p, C * p * p)
        key = jax.random.key(seed)
        k1, k2, k3 = jax.random.split(key, 3)
        B, C, H, W_img = (32, 3, 160, 160)
        x = jax.random.normal(k1, (B, C, H, W_img), dtype=jnp.float32)
        d_in = C * PATCH * PATCH
        W = jax.random.normal(k2, (N_EMBD, d_in), dtype=jnp.float32) / np.sqrt(d_in)
        b = jax.random.normal(k3, (N_EMBD,), dtype=jnp.float32) * 0.01
        cls = jnp.zeros((1, 1, N_EMBD), dtype=jnp.float32)
        gamma = jnp.ones((N_EMBD,), dtype=jnp.float32)
        beta = jnp.zeros((N_EMBD,), dtype=jnp.float32)
        return {'x': x, 'W': W, 'b': b, 'cls': cls, 'gamma': gamma, 'beta': beta}
    _L0_tok_all = _L0_tok_setup()
    _L0_tok_in = {k: v for k, v in _L0_tok_all.items() if k in ('W', 'b', 'cls', 'gamma', 'beta')}
    del _L0_tok_all

    def _L0_txt_setup():
        import jax, jax.numpy as jnp
        import numpy as np
        N_LAYER, D, H, V, S_MAX = (5, 192, 12, 40478, 256)
        HD = D // H
        GELU_C = float(np.sqrt(2.0 / np.pi))

        def gelu(x):
            return 0.5 * x * (1.0 + jnp.tanh(GELU_C * (x + 0.044715 * x ** 3)))

        def layernorm(x, w, b, eps=1e-05):
            mu = jnp.mean(x, axis=-1, keepdims=True)
            var = jnp.mean((x - mu) ** 2, axis=-1, keepdims=True)
            return (x - mu) * jax.lax.rsqrt(var + eps) * w + b

        def forward(input_ids, position_ids, attention_mask, tok_emb, pos_emb, c_attn_w, c_attn_b, c_proj_w, c_proj_b, ln1_w, ln1_b, c_fc_w, c_fc_b, mlp_proj_w, mlp_proj_b, ln2_w, ln2_b):
            B, S = input_ids.shape
            h = tok_emb[input_ids] + pos_emb[position_ids][None]
            ext_mask = (1.0 - attention_mask)[:, None, None, :] * jnp.finfo(h.dtype).min
            causal = jnp.tril(jnp.ones((S, S), dtype=h.dtype))
            scale = 1.0 / jnp.sqrt(jnp.asarray(HD, h.dtype))
            for i in range(N_LAYER):
                qkv = h @ c_attn_w[i] + c_attn_b[i]
                q, k, v = jnp.split(qkv, 3, axis=-1)
                q = q.reshape(B, S, H, HD).transpose(0, 2, 1, 3)
                k = k.reshape(B, S, H, HD).transpose(0, 2, 1, 3)
                v = v.reshape(B, S, H, HD).transpose(0, 2, 1, 3)
                w = jnp.einsum('bhqd,bhkd->bhqk', q, k) * scale
                w = w * causal + -10000.0 * (1.0 - causal)
                w = w + ext_mask
                p = jax.nn.softmax(w, axis=-1)
                a = jnp.einsum('bhqk,bhkd->bhqd', p, v)
                a = a.transpose(0, 2, 1, 3).reshape(B, S, D)
                a = a @ c_proj_w[i] + c_proj_b[i]
                n = layernorm(h + a, ln1_w[i], ln1_b[i])
                m = gelu(n @ c_fc_w[i] + c_fc_b[i]) @ mlp_proj_w[i] + mlp_proj_b[i]
                h = layernorm(n + m, ln2_w[i], ln2_b[i])
            return h
        key = jax.random.key(seed)
        ks = jax.random.split(key, 8)
        B, S = (4, 256)
        w = 0.02
        return {'input_ids': jax.random.randint(ks[0], (B, S), 0, V), 'position_ids': jnp.arange(S, dtype=jnp.int64), 'attention_mask': jnp.ones((B, S), dtype=jnp.float32), 'tok_emb': jax.random.normal(ks[1], (V, D), jnp.float32) * w, 'pos_emb': jax.random.normal(ks[2], (S_MAX, D), jnp.float32) * w, 'c_attn_w': jax.random.normal(ks[3], (N_LAYER, D, 3 * D), jnp.float32) * w, 'c_attn_b': jnp.zeros((N_LAYER, 3 * D), jnp.float32), 'c_proj_w': jax.random.normal(ks[4], (N_LAYER, D, D), jnp.float32) * w, 'c_proj_b': jnp.zeros((N_LAYER, D), jnp.float32), 'ln1_w': jnp.ones((N_LAYER, D), jnp.float32), 'ln1_b': jnp.zeros((N_LAYER, D), jnp.float32), 'c_fc_w': jax.random.normal(ks[5], (N_LAYER, D, 4 * D), jnp.float32) * w, 'c_fc_b': jnp.zeros((N_LAYER, 4 * D), jnp.float32), 'mlp_proj_w': jax.random.normal(ks[6], (N_LAYER, 4 * D, D), jnp.float32) * w, 'mlp_proj_b': jnp.zeros((N_LAYER, D), jnp.float32), 'ln2_w': jnp.ones((N_LAYER, D), jnp.float32), 'ln2_b': jnp.zeros((N_LAYER, D), jnp.float32)}
    _L0_txt_all = _L0_txt_setup()
    _L0_txt_in = {k: v for k, v in _L0_txt_all.items() if k in ('tok_emb', 'pos_emb', 'c_attn_w', 'c_attn_b', 'c_proj_w', 'c_proj_b', 'ln1_w', 'ln1_b', 'c_fc_w', 'c_fc_b', 'mlp_proj_w', 'mlp_proj_b', 'ln2_w', 'ln2_b')}
    del _L0_txt_all

    def _L0_attn_setup():
        import jax, jax.numpy as jnp
        import numpy as np
        B, S, D_MODEL, N_HEAD, D_HEAD, GROUPS = (2, 256, 192, 12, 64, 4)
        EPS = 1e-09
        SCALE = 1.0 / np.sqrt(D_HEAD).astype(np.float32)

        def grouped_proj(x, W, b=None):
            g = W.shape[0]
            b_, s_, d = x.shape
            y = jnp.einsum('bsgi,gio->bsgo', x.reshape(b_, s_, g, d // g), W).reshape(b_, s_, -1)
            return y if b is None else y + b

        def rel_shift_gather(pos_attn, context_len, shift):
            b, n, s, m = pos_attn.shape
            pos_attn = pos_attn.reshape(b, n, m, s)[:, :, shift:, :]
            pos_attn = pos_attn.reshape(b, n, s, m - shift)[..., :context_len]
            return pos_attn
        key = jax.random.key(seed)
        ks = jax.random.split(key, 16)
        dg = D_MODEL // GROUPS
        og = N_HEAD * D_HEAD // GROUPS
        std = 0.02
        return {'query': jax.random.normal(ks[0], (B, S, D_MODEL), jnp.float32), 'position_embeds': jax.random.normal(ks[1], (2 * S - 1, D_MODEL), jnp.float32), 'Wq': jax.random.normal(ks[2], (GROUPS, dg, og), jnp.float32) * std, 'Wk': jax.random.normal(ks[3], (GROUPS, dg, og), jnp.float32) * std, 'bk': jnp.zeros((N_HEAD * D_HEAD,), jnp.float32), 'Wv': jax.random.normal(ks[4], (GROUPS, dg, dg), jnp.float32) * std, 'bv': jnp.zeros((D_MODEL,), jnp.float32), 'r_kernel': jax.random.normal(ks[5], (D_MODEL, N_HEAD, D_HEAD), jnp.float32) * std, 'r_w_bias': jax.random.normal(ks[6], (N_HEAD, D_HEAD), jnp.float32) * std, 'r_r_bias': jax.random.normal(ks[7], (N_HEAD, D_HEAD), jnp.float32) * std, 'Wo': jax.random.normal(ks[8], (D_MODEL, D_MODEL), jnp.float32) * std, 'bo': jnp.zeros((D_MODEL,), jnp.float32), 'gamma': jnp.ones((D_MODEL,), jnp.float32), 'beta': jnp.zeros((D_MODEL,), jnp.float32)}
    _L0_attn_all = _L0_attn_setup()
    _L0_attn_in = {k: v for k, v in _L0_attn_all.items() if k in ('position_embeds', 'Wq', 'Wk', 'bk', 'Wv', 'bv', 'r_kernel', 'r_w_bias', 'r_r_bias', 'Wo', 'bo', 'gamma', 'beta')}
    del _L0_attn_all

    def _L0_ffn_setup():
        import jax, jax.numpy as jnp
        import numpy as np
        B, S, D_IN, D_HID, D_OUT = (32, 128, 192, 768, 192)
        key = jax.random.key(seed)
        k1, k2, k3, k4 = jax.random.split(key, 4)
        init_k = float(np.sqrt(1.0 / D_IN))
        init_k2 = float(np.sqrt(1.0 / D_HID))
        x = jax.random.normal(k1, (B, S, D_IN), dtype=jnp.float32)
        in_weight = jax.random.uniform(k2, (D_HID, D_IN), dtype=jnp.float32, minval=-init_k, maxval=init_k)
        in_bias = jax.random.uniform(k3, (D_HID,), dtype=jnp.float32, minval=-init_k, maxval=init_k)
        out_weight = jax.random.uniform(k4, (D_HID, D_OUT), dtype=jnp.float32, minval=-init_k2, maxval=init_k2)
        return {'x': x, 'in_weight': in_weight, 'in_bias': in_bias, 'out_weight': out_weight}
    _L0_ffn_all = _L0_ffn_setup()
    _L0_ffn_in = {k: v for k, v in _L0_ffn_all.items() if k in ('in_weight', 'in_bias', 'out_weight')}
    del _L0_ffn_all
    return {'x': x, 'x_txt': x_txt, 'pos_S': pos_S, 'mask_BS_f1_0': mask_BS_f1_0, 'L0_tok_W': _L0_tok_in['W'], 'L0_tok_b': _L0_tok_in['b'], 'L0_tok_cls': _L0_tok_in['cls'], 'L0_tok_gamma': _L0_tok_in['gamma'], 'L0_tok_beta': _L0_tok_in['beta'], 'L0_txt_tok_emb': _L0_txt_in['tok_emb'], 'L0_txt_pos_emb': _L0_txt_in['pos_emb'], 'L0_txt_c_attn_w': _L0_txt_in['c_attn_w'], 'L0_txt_c_attn_b': _L0_txt_in['c_attn_b'], 'L0_txt_c_proj_w': _L0_txt_in['c_proj_w'], 'L0_txt_c_proj_b': _L0_txt_in['c_proj_b'], 'L0_txt_ln1_w': _L0_txt_in['ln1_w'], 'L0_txt_ln1_b': _L0_txt_in['ln1_b'], 'L0_txt_c_fc_w': _L0_txt_in['c_fc_w'], 'L0_txt_c_fc_b': _L0_txt_in['c_fc_b'], 'L0_txt_mlp_proj_w': _L0_txt_in['mlp_proj_w'], 'L0_txt_mlp_proj_b': _L0_txt_in['mlp_proj_b'], 'L0_txt_ln2_w': _L0_txt_in['ln2_w'], 'L0_txt_ln2_b': _L0_txt_in['ln2_b'], 'L0_attn_position_embeds': _L0_attn_in['position_embeds'], 'L0_attn_Wq': _L0_attn_in['Wq'], 'L0_attn_Wk': _L0_attn_in['Wk'], 'L0_attn_bk': _L0_attn_in['bk'], 'L0_attn_Wv': _L0_attn_in['Wv'], 'L0_attn_bv': _L0_attn_in['bv'], 'L0_attn_r_kernel': _L0_attn_in['r_kernel'], 'L0_attn_r_w_bias': _L0_attn_in['r_w_bias'], 'L0_attn_r_r_bias': _L0_attn_in['r_r_bias'], 'L0_attn_Wo': _L0_attn_in['Wo'], 'L0_attn_bo': _L0_attn_in['bo'], 'L0_attn_gamma': _L0_attn_in['gamma'], 'L0_attn_beta': _L0_attn_in['beta'], 'L0_ffn_in_weight': _L0_ffn_in['in_weight'], 'L0_ffn_in_bias': _L0_ffn_in['in_bias'], 'L0_ffn_out_weight': _L0_ffn_in['out_weight']}

def reference(x, x_txt, pos_S, mask_BS_f1_0, L0_tok_W, L0_tok_b, L0_tok_cls, L0_tok_gamma, L0_tok_beta, L0_txt_tok_emb, L0_txt_pos_emb, L0_txt_c_attn_w, L0_txt_c_attn_b, L0_txt_c_proj_w, L0_txt_c_proj_b, L0_txt_ln1_w, L0_txt_ln1_b, L0_txt_c_fc_w, L0_txt_c_fc_b, L0_txt_mlp_proj_w, L0_txt_mlp_proj_b, L0_txt_ln2_w, L0_txt_ln2_b, L0_attn_position_embeds, L0_attn_Wq, L0_attn_Wk, L0_attn_bk, L0_attn_Wv, L0_attn_bv, L0_attn_r_kernel, L0_attn_r_w_bias, L0_attn_r_r_bias, L0_attn_Wo, L0_attn_bo, L0_attn_gamma, L0_attn_beta, L0_ffn_in_weight, L0_ffn_in_bias, L0_ffn_out_weight):
    import jax
    import jax.numpy as jnp

    def _L0_tok_ref(x, W, b, cls, gamma, beta):
        import jax, jax.numpy as jnp
        import numpy as np
        PATCH = 10
        N_EMBD = 192
        EPS = 1e-05

        def _patchify(x, p):
            B, C, H, Wd = x.shape
            h_p, w_p = (H // p, Wd // p)
            x = x[:, :, :h_p * p, :w_p * p]
            x = x.reshape(B, C, h_p, p, w_p, p)
            x = x.transpose(0, 2, 4, 1, 3, 5)
            return x.reshape(B, h_p * w_p, C * p * p)
        B = x.shape[0]
        patches = _patchify(x, PATCH)
        tok = jnp.einsum('bnd,ed->bne', patches, W) + b
        cls_tok = jnp.broadcast_to(cls, (B, 1, N_EMBD))
        tok = jnp.concatenate([cls_tok, tok], axis=1)
        mean = tok.mean(-1, keepdims=True)
        var = tok.var(-1, keepdims=True)
        return (tok - mean) * jax.lax.rsqrt(var + EPS) * gamma + beta

    def _L0_txt_ref(input_ids, position_ids, attention_mask, tok_emb, pos_emb, c_attn_w, c_attn_b, c_proj_w, c_proj_b, ln1_w, ln1_b, c_fc_w, c_fc_b, mlp_proj_w, mlp_proj_b, ln2_w, ln2_b):
        import jax, jax.numpy as jnp
        import numpy as np
        N_LAYER, D, H, V, S_MAX = (5, 192, 12, 40478, 256)
        HD = D // H
        GELU_C = float(np.sqrt(2.0 / np.pi))

        def gelu(x):
            return 0.5 * x * (1.0 + jnp.tanh(GELU_C * (x + 0.044715 * x ** 3)))

        def layernorm(x, w, b, eps=1e-05):
            mu = jnp.mean(x, axis=-1, keepdims=True)
            var = jnp.mean((x - mu) ** 2, axis=-1, keepdims=True)
            return (x - mu) * jax.lax.rsqrt(var + eps) * w + b

        def forward(input_ids, position_ids, attention_mask, tok_emb, pos_emb, c_attn_w, c_attn_b, c_proj_w, c_proj_b, ln1_w, ln1_b, c_fc_w, c_fc_b, mlp_proj_w, mlp_proj_b, ln2_w, ln2_b):
            B, S = input_ids.shape
            h = tok_emb[input_ids] + pos_emb[position_ids][None]
            ext_mask = (1.0 - attention_mask)[:, None, None, :] * jnp.finfo(h.dtype).min
            causal = jnp.tril(jnp.ones((S, S), dtype=h.dtype))
            scale = 1.0 / jnp.sqrt(jnp.asarray(HD, h.dtype))
            for i in range(N_LAYER):
                qkv = h @ c_attn_w[i] + c_attn_b[i]
                q, k, v = jnp.split(qkv, 3, axis=-1)
                q = q.reshape(B, S, H, HD).transpose(0, 2, 1, 3)
                k = k.reshape(B, S, H, HD).transpose(0, 2, 1, 3)
                v = v.reshape(B, S, H, HD).transpose(0, 2, 1, 3)
                w = jnp.einsum('bhqd,bhkd->bhqk', q, k) * scale
                w = w * causal + -10000.0 * (1.0 - causal)
                w = w + ext_mask
                p = jax.nn.softmax(w, axis=-1)
                a = jnp.einsum('bhqk,bhkd->bhqd', p, v)
                a = a.transpose(0, 2, 1, 3).reshape(B, S, D)
                a = a @ c_proj_w[i] + c_proj_b[i]
                n = layernorm(h + a, ln1_w[i], ln1_b[i])
                m = gelu(n @ c_fc_w[i] + c_fc_b[i]) @ mlp_proj_w[i] + mlp_proj_b[i]
                h = layernorm(n + m, ln2_w[i], ln2_b[i])
            return h
        return forward(input_ids, position_ids, attention_mask, tok_emb, pos_emb, c_attn_w, c_attn_b, c_proj_w, c_proj_b, ln1_w, ln1_b, c_fc_w, c_fc_b, mlp_proj_w, mlp_proj_b, ln2_w, ln2_b)

    def _L0_attn_ref(query, position_embeds, Wq, Wk, bk, Wv, bv, r_kernel, r_w_bias, r_r_bias, Wo, bo, gamma, beta):
        import jax, jax.numpy as jnp
        import numpy as np
        B, S, D_MODEL, N_HEAD, D_HEAD, GROUPS = (2, 256, 192, 12, 64, 4)
        EPS = 1e-09
        SCALE = 1.0 / np.sqrt(D_HEAD).astype(np.float32)

        def grouped_proj(x, W, b=None):
            g = W.shape[0]
            b_, s_, d = x.shape
            y = jnp.einsum('bsgi,gio->bsgo', x.reshape(b_, s_, g, d // g), W).reshape(b_, s_, -1)
            return y if b is None else y + b

        def rel_shift_gather(pos_attn, context_len, shift):
            b, n, s, m = pos_attn.shape
            pos_attn = pos_attn.reshape(b, n, m, s)[:, :, shift:, :]
            pos_attn = pos_attn.reshape(b, n, s, m - shift)[..., :context_len]
            return pos_attn
        b, s, _ = query.shape
        q = grouped_proj(query, Wq).reshape(b, s, N_HEAD, D_HEAD) * SCALE
        k = grouped_proj(query, Wk, bk).reshape(b, s, N_HEAD, D_HEAD)
        v = grouped_proj(query, Wv, bv).reshape(b, s, N_HEAD, D_MODEL // N_HEAD)
        content_score = jnp.einsum('bind,bjnd->bnij', q + r_w_bias * SCALE, k)
        r_head = jnp.einsum('td,dnh->tnh', position_embeds, r_kernel)
        pos_score = jnp.einsum('bind,tnd->bnit', q + r_r_bias * SCALE, r_head)
        pos_score = rel_shift_gather(pos_score, s, shift=1)
        attn_prob = jax.nn.softmax(content_score + pos_score, axis=-1)
        attn_vec = jnp.einsum('bnij,bjnd->bind', attn_prob, v).reshape(b, s, D_MODEL)
        attn_out = attn_vec @ Wo + bo
        h = query + attn_out
        mu = jnp.mean(h, axis=-1, keepdims=True)
        var = jnp.mean(jnp.square(h - mu), axis=-1, keepdims=True)
        return (h - mu) * jax.lax.rsqrt(var + EPS) * gamma + beta

    def _L0_ffn_ref(x, in_weight, in_bias, out_weight):
        import jax, jax.numpy as jnp
        import numpy as np
        B, S, D_IN, D_HID, D_OUT = (32, 128, 192, 768, 192)
        lead = x.shape[:-1]
        xt = x.reshape(-1, in_weight.shape[1])
        h = jax.nn.gelu(jnp.einsum('td,hd->th', xt, in_weight) + in_bias, approximate=False)
        out = jnp.einsum('th,ho->to', h, out_weight)
        return out.reshape(*lead, out_weight.shape[1])
    h = _L0_tok_ref(x, L0_tok_W, L0_tok_b, L0_tok_cls, L0_tok_gamma, L0_tok_beta)
    h = jnp.concatenate([h, _L0_txt_ref(x_txt, pos_S, mask_BS_f1_0, L0_txt_tok_emb, L0_txt_pos_emb, L0_txt_c_attn_w, L0_txt_c_attn_b, L0_txt_c_proj_w, L0_txt_c_proj_b, L0_txt_ln1_w, L0_txt_ln1_b, L0_txt_c_fc_w, L0_txt_c_fc_b, L0_txt_mlp_proj_w, L0_txt_mlp_proj_b, L0_txt_ln2_w, L0_txt_ln2_b)], axis=1)
    h = h + _L0_attn_ref(_layernorm(h, axis=-1), L0_attn_position_embeds, L0_attn_Wq, L0_attn_Wk, L0_attn_bk, L0_attn_Wv, L0_attn_bv, L0_attn_r_kernel, L0_attn_r_w_bias, L0_attn_r_r_bias, L0_attn_Wo, L0_attn_bo, L0_attn_gamma, L0_attn_beta)
    h = h + _L0_ffn_ref(_layernorm(h, axis=-1), L0_ffn_in_weight, L0_ffn_in_bias, L0_ffn_out_weight)
    return h

_drawn_inputs = setup_inputs


def setup_inputs(seed=0):
    import zlib

    import numpy as np

    out = dict(_drawn_inputs(seed))
    spreads = {'L0_tok_cls': (0.0, 0.1),
     'L0_tok_gamma': (1.0, 0.2),
     'L0_tok_beta': (0.0, 0.1),
     'L0_txt_c_attn_b': (0.0, 0.1),
     'L0_txt_c_proj_b': (0.0, 0.1),
     'L0_txt_ln1_w': (1.0, 0.2),
     'L0_txt_ln1_b': (0.0, 0.1),
     'L0_txt_c_fc_b': (0.0, 0.1),
     'L0_txt_mlp_proj_b': (0.0, 0.1),
     'L0_txt_ln2_w': (1.0, 0.2),
     'L0_txt_ln2_b': (0.0, 0.1),
     'L0_attn_bk': (0.0, 2.0),
     'L0_attn_bv': (0.0, 0.592),
     'L0_attn_bo': (0.0, 0.1),
     'L0_attn_gamma': (1.0, 0.2),
     'L0_attn_beta': (0.0, 0.1)}
    factors = {'L0_tok_b': 7.729,
     'L0_attn_position_embeds': 8.0,
     'L0_attn_Wq': 8.0,
     'L0_attn_Wk': 8.0,
     'L0_attn_Wv': 6.461,
     'L0_attn_r_kernel': 8.0,
     'L0_attn_r_w_bias': 38.434,
     'L0_attn_r_r_bias': 8.0,
     'L0_attn_Wo': 3.428,
     'L0_ffn_in_bias': 7.489}
    for name, (base, spread) in spreads.items():
        noise = np.random.default_rng([zlib.crc32(name.encode()), seed]).standard_normal(out[name].shape)
        drawn = base * np.exp(spread * noise) if base else spread * noise
        out[name] = jnp.asarray(drawn.astype(out[name].dtype))
    for name, factor in factors.items():
        out[name] = (out[name] * factor).astype(out[name].dtype)
    return out
```

```python
import concourse.bass as bass
from concourse import mybir
from contextlib import ExitStack

F32 = mybir.dt.float32
I32 = mybir.dt.int32
U32 = mybir.dt.uint32
ALU = mybir.AluOpType
ACT = mybir.ActivationFunctionType
AX = mybir.AxisListType

B = 32
TXT = 77
IMG = 82
S = IMG + TXT
D = 192
HALF = D // 2
NH = 12
LAYERS = 5
G = 4
GROUPS = B // G
STEPS = LAYERS * GROUPS
GT = G * TXT
HD = D // NH
HA = HD + 1
DH = 64
HID = 768
MH = HID // 128
NT = 2 * S - 1
WIN = S + IMG - 1
ROWS = (IMG, TXT)
OFF = (0, IMG)
PK = 100
EPS = 1e-5
ATT_EPS = 1e-9
NEG = -10000.0
FMIN = -3.4028234663852886e38

A_QK, A_V, A_COL = 0, 2 * 2 * D, 2 * 2 * D + 2 * D
A_W = A_COL + 6
C_FC, C_COL = 0, 2 * HID
C_W = C_COL + 4
C2_COL = MH * D
C2_W = C2_COL + MH
J_Q, J_K, J_V, J_O, J_IN = 0, 768, 1536, 1728, 2112
J_POS = J_IN + 2 * HID
J_R = J_POS + 2 * NT
J_W = J_R + 2 * 768
K_OUT, K_INB, K_RW, K_RR, K_BK = 0, MH * D, MH * D + 6, MH * D + 12, MH * D + 18
K_W = MH * D + 24
CST_I, CST_CAUSAL, CST_NEG, CST_EVEN, CST_ODD, CST_PW = 0, 128, 128 + TXT, 128 + 2 * TXT, 129 + 2 * TXT, 130 + 2 * TXT
CST_W = CST_PW + 2


class Signal:

    def __init__(self, sem, per):
        self.sem, self.per = sem, per


class Item:

    def __init__(self, engine, base, lag=0, products=None):
        self.engine, self.base, self.lag = engine, base, lag
        self.products = {} if products is None else products

    def minus(self, n):
        return Item(self.engine, self.base, self.lag - n, self.products)

    def at(self, per, n):
        if isinstance(self.base, int):
            return (self.base + self.lag) * per + n
        if per not in self.products:
            self.products[per] = self.engine.snap(self.base * per)
        return self.products[per] + (self.lag * per + n)

    def value(self):
        return self.base + self.lag


def wait(engine, signal, item, n):
    value = item.at(signal.per, n)
    if isinstance(value, int) and value <= 0:
        return
    engine.wait_ge(signal.sem, value)


def early_fusion(nc, patches, ids, pos_ids, mask, tok_emb, pos_emb, w_a, r_a, w_b, r_b, w_c, w_c2, r_c,
                 w_tok, r_joint, w_joint, w_joint128, consts, out, h_text, pos_scratch):
    ctx = ExitStack()
    with ctx:
        def sb(name, shape, dt=F32):
            return ctx.enter_context(nc.sbuf_tensor(name, shape, dt))

        def sig(name, per=1):
            return Signal(ctx.enter_context(nc.semaphore(name)), per)

        bank = [ctx.enter_context(nc.psum_tensor(f"bank{i}", [128, 512], F32)) for i in range(8)]

        cst = sb("cst", [128, CST_W])
        ident = cst[:, CST_I:CST_I + 128]
        power = cst[:, CST_PW:CST_PW + 2]
        wtok = sb("wtok", [PK, 3, D])
        wj = sb("wj", [HALF, J_W])
        wk = sb("wk", [128, K_W])
        rj = sb("rj", [IMG, 7, D])
        rel = sb("rel", [128, 6, NT])
        rw8 = sb("rw8", [128, 6])
        rr8 = sb("rr8", [128, 6])

        text_ctx = ExitStack()

        def tb(name, shape, dt=F32):
            return text_ctx.enter_context(nc.sbuf_tensor(name, shape, dt))

        id_sb = tb("id_sb", [TXT, B], I32)
        pid_sb = tb("pid_sb", [TXT, 1], I32)
        emb = tb("emb", [TXT, B, D])
        pos_row = tb("pos_row", [TXT, D])
        ext = tb("ext", [TXT, B, TXT])
        wa = tb("wa", [HALF, A_W])
        wb = tb("wb", [HALF, 2 * D])
        wc = tb("wc", [HALF, C_W])
        wc2 = tb("wc2", [128, C2_W])
        ra = tb("ra", [TXT, 2, D])
        rb = tb("rb", [TXT, 3, D])
        rc = tb("rc", [TXT, 2, D])
        h_tok = tb("h_tok", [TXT, G, D])
        hT = tb("hT", [HALF, 2, GT])
        q_even = tb("q_even", [HALF, 2, GT])
        q_odd = tb("q_odd", [HALF, 2, GT])
        kT = tb("kT", [HALF, 2, GT])
        v_tok = tb("v_tok", [TXT, G, NH, HA])
        sc = tb("sc", [TXT, G, NH, TXT])
        mx = tb("mx", [TXT, G, NH])
        pT = tb("pT", [TXT, 2, 6 * TXT])
        rden = tb("rden", [TXT, NH])
        att = tb("att", [TXT, D])
        aT = tb("aT", [HALF, 2 * TXT])
        h_bias = tb("h_bias", [TXT, G, D])
        r1 = tb("r1", [TXT, D])
        st1 = tb("st1", [TXT, 6])
        mv1 = tb("mv1", [TXT, 2])
        rs1 = tb("rs1", [TXT, 1])
        x1 = tb("x1", [TXT, G, D])
        nb_tmp = tb("nb_tmp", [TXT, D])
        bias2 = tb("bias2", [TXT, D])
        n_bias = tb("n_bias", [TXT, G, D])
        nT = tb("nT", [HALF, 2, GT])
        gel = tb("gel", [128, MH, GT])
        r2 = tb("r2", [TXT, D])
        st2 = tb("st2", [TXT, 6])
        mv2 = tb("mv2", [TXT, 2])
        rs2 = tb("rs2", [TXT, 1])
        x2 = tb("x2", [TXT, D])
        ho_tmp = tb("ho_tmp", [TXT, D])
        h_out = tb("h_out", [TXT, G, D])

        consts_in = sig("consts_in")
        carried = {nc.sync.engine: sig("carried_sp"), nc.vector.engine: sig("carried_dve")}
        ids_in = sig("ids_in")
        mask_in = sig("mask_in")
        pos_row_in = sig("pos_row_in")
        emb_in = [sig(f"emb_in{g}") for g in range(GROUPS)]
        emb_done = sig("emb_done")
        emb_stored = [sig(f"emb_stored{g}") for g in range(GROUPS)]
        ones_set = sig("ones_set")
        ext_one = sig("ext_one")
        ext_scaled = sig("ext_scaled")
        ext_ready = sig("ext_ready")
        wa_in, wb_in, wc_in = sig("wa_in", 32), sig("wb_in", 32), sig("wc_in", 48)
        h_in = [sig(f"h_in{b}", 16) for b in range(G)]
        h_stored = [sig(f"h_stored{b}", 16) for b in range(G)]
        hT_ps, hT_sb = sig("hT_ps", G), sig("hT_sb", G)
        qk_ps, q_sb, k_sb = sig("qk_ps", 4), sig("q_sb", 4), sig("k_sb", 2)
        v_ps, v_sb = sig("v_ps", G), sig("v_sb", G)
        s_ps, masked, biased, maxed, shifted, expd = (sig("s_ps", G), sig("masked", 3 * G), sig("biased", G),
                                                      sig("maxed", G), sig("shifted", G), sig("expd", G))
        pT_ps, pT_sb, pv_ps = sig("pT_ps", 2 * G), sig("pT_sb", 2 * G), sig("pv_ps", G)
        rden_ok, att_ok, aT_ps, aT_sb, pj_ps = (sig("rden_ok", G), sig("att_ok", G), sig("aT_ps", G),
                                                sig("aT_sb", G), sig("pj_ps", G))
        hb_ok, r1_ok, st1_ok, mv1_ok, ve1_ok, rs1_ok, x1_ok = (sig("hb_ok", G), sig("r1_ok", G), sig("st1_ok", G),
                                                               sig("mv1_ok", G), sig("ve1_ok", G), sig("rs1_ok", G),
                                                               sig("x1_ok", G))
        bias2_ok, nbt_ok, nb_mid, nb_ok = sig("bias2_ok", 1), sig("nbt_ok", G), sig("nb_mid", G), sig("nb_ok", G)
        nT_ps, nT_sb, fc_ps, gelu_ok, ml_ps = (sig("nT_ps", G), sig("nT_sb", 2 * G), sig("fc_ps", MH),
                                               sig("gelu_ok", MH), sig("ml_ps", G))
        r2_ok, st2_ok, mv2_ok, ve2_ok, rs2_ok, x2_ok = (sig("r2_ok", G), sig("st2_ok", G), sig("mv2_ok", G),
                                                        sig("ve2_ok", G), sig("rs2_ok", G), sig("x2_ok", G))
        hot_ok, ho_ok = sig("hot_ok", G), sig("ho_ok", G)

        def wait_alone(engine, signal, item, n):
            wait(engine, signal, item, n)
            if not isinstance(item.base, int):
                engine.sem_inc(carried[engine.engine].sem)

        def text_steps(engine, step):
            fixed = lambda t: Item(engine, t)
            step(fixed(0), None, None)
            step(fixed(1), fixed(0), None)
            step(fixed(2), fixed(1), fixed(0))
            with engine.Fori(3, STEPS) as t:
                a = Item(engine, t)
                step(a, a.minus(1), a.minus(2))
            step(None, fixed(STEPS - 1), fixed(STEPS - 2))
            step(None, None, fixed(STEPS - 1))

        def layer_in(engine, signal, item):
            if isinstance(item.base, int):
                engine.wait_ge(signal.sem, (item.value() // GROUPS + 1) * signal.per)
            else:
                engine.wait_ge(signal.sem, (item.value() >> 3) * signal.per + signal.per)

        def text_over(engine):
            for b in range(G):
                wait(engine, h_stored[b], Item(engine, STEPS - 1), 16)

        text_ctx.close()
        pat = sb("pat", [PK, 2, 3 * IMG])
        e0 = sb("e0", [IMG, D])
        ste = sb("ste", [IMG, 6])
        mve = sb("mve", [IMG, 2])
        rse = sb("rse", [IMG, 1])
        e1 = sb("e1", [IMG, D])
        e2 = sb("e2", [IMG, D])
        hj = sb("hj", [IMG, 2, 2, D])
        stq = sb("stq", [IMG, 2, 6])
        mvq = sb("mvq", [IMG, 2, 2])
        rsq = sb("rsq", [IMG, 2])
        xq = sb("xq", [IMG, 2, D])
        xqb = sb("xqb", [IMG, 2, 2, D])
        xqT = sb("xqT", [HALF, 2, S])
        qc = sb("qc", [128, 2, 6, S])
        qr = sb("qr", [128, 6, S])
        kj = sb("kj", [128, 2, 6, S])
        vj = sb("vj", [IMG, 2, 2, NH, HA])
        pos_out = sb("pos_out", [IMG, 2, NH, WIN])
        pos_in = sb("pos_in", [IMG, 2, NH, S])
        scj = sb("scj", [IMG, 2, NH, S])
        mxj = sb("mxj", [IMG, 2, NH])
        nmj = sb("nmj", [IMG, 2, NH])
        pTj = sb("pTj", [IMG, 2, 2, 3 * S])
        rdj = sb("rdj", [IMG, 2, NH])
        atj = sb("atj", [IMG, 2, D])
        aTj = sb("aTj", [HALF, 2 * S])
        r3 = sb("r3", [IMG, 2, D])
        st3 = sb("st3", [IMG, 2, 6])
        mv3 = sb("mv3", [IMG, 2, 2])
        rs3 = sb("rs3", [IMG, 2])
        x3 = sb("x3", [IMG, 2, D])
        t3 = sb("t3", [IMG, 2, D])
        t4 = sb("t4", [IMG, 2, D])
        h2 = sb("h2", [IMG, 2, 2, D])
        st4 = sb("st4", [IMG, 2, 6])
        mv4 = sb("mv4", [IMG, 2, 2])
        rs4 = sb("rs4", [IMG, 2])
        x4 = sb("x4", [IMG, 2, D])
        x4T = sb("x4T", [HALF, 2, S])
        gj = sb("gj", [128, MH, S])
        yj = sb("yj", [IMG, 2, 2, D])

        jw_in, rel_ps, rel_ok, r8_ok, pads = sig("jw_in"), sig("rel_ps"), sig("rel_ok"), sig("r8_ok"), sig("pads")
        pat_in = [sig(f"pat_in{p}", 16) for p in range(2)]
        ht_in = [sig(f"ht_in{p}", 16) for p in range(2)]
        e_ps, e0_ok, ste_ok, mve_ok, vee_ok, rse_ok, e1_ok, e2_ok, e3_ok = (
            sig("e_ps"), sig("e0_ok"), sig("ste_ok"), sig("mve_ok"), sig("vee_ok"), sig("rse_ok"),
            sig("e1_ok"), sig("e2_ok"), sig("e3_ok"))
        stq_ok, mvq_ok, veq_ok, rsq_ok, xq_ok, xqb_ok = (sig("stq_ok", 2), sig("mvq_ok", 2), sig("veq_ok"),
                                                         sig("rsq_ok"), sig("xq_ok", 2), sig("xqb_ok", 2))
        xqT_ps, xqT_sb = sig("xqT_ps"), sig("xqT_sb")
        qj_ps, qc_ok, qr_ok, kj_ps, kj_ok = sig("qj_ps", 2), sig("qc_ok", 2), sig("qr_ok", 2), sig("kj_ps", 2), sig("kj_ok", 2)
        vj_ps, vj_ok = sig("vj_ps"), sig("vj_ok", 2)
        pos_ps, pos_sb = sig("pos_ps", 6), sig("pos_sb", 12)
        pos_written, pos_back = [sig(f"pos_written{i}", 16) for i in range(2)], [sig(f"pos_back{i}", 16) for i in range(2)]
        sj_ps, sj_sb, nm_ok, ej_ok = sig("sj_ps", 4), sig("sj_sb", 24), sig("nm_ok", 2), sig("ej_ok", 24)
        ptj_ps, ptj_sb, pvj_ps = sig("ptj_ps", 8), sig("ptj_sb", 8), sig("pvj_ps", 4)
        rdj_ok, atj_ok, atT_ps, atT_sb, wo_ps = sig("rdj_ok", 2), sig("atj_ok", 2), sig("atT_ps"), sig("atT_sb"), sig("wo_ps")
        r3_ok, st3_ok, mv3_ok, ve3_ok, rs3_ok, x3_ok = (sig("r3_ok", 2), sig("st3_ok", 2), sig("mv3_ok", 2),
                                                        sig("ve3_ok"), sig("rs3_ok"), sig("x3_ok", 2))
        t3_ok, t4_ok, h2_ok = sig("t3_ok", 2), sig("t4_ok", 2), sig("h2_ok", 2)
        st4_ok, mv4_ok, ve4_ok, rs4_ok, x4_ok = sig("st4_ok", 2), sig("mv4_ok", 2), sig("ve4_ok"), sig("rs4_ok"), sig("x4_ok", 2)
        x4T_ps, x4T_sb, fj_ps, gj_ok, mj_ps, yj_ok = (sig("x4T_ps"), sig("x4T_sb"), sig("fj_ps", 2), sig("gj_ok", 6),
                                                      sig("mj_ps"), sig("yj_ok", 2))
        y_stored = [sig(f"y_stored{i}", 32) for i in range(2)]

        def joint_steps(engine, step):
            fixed = lambda u: Item(engine, u)
            step(fixed(0), None, None, 0)
            step(fixed(1), fixed(0), None, 1)
            step(fixed(2), fixed(1), fixed(0), 0)
            step(fixed(3), fixed(2), fixed(1), 1)
            with engine.Fori(2, B // 2) as pair:
                even = Item(engine, engine.snap(pair * 2))
                for p in range(2):
                    d = even.minus(-p)
                    step(d, d.minus(1), d.minus(2), p)
            step(None, fixed(B - 1), fixed(B - 2), 0)
            step(None, None, fixed(B - 1), 1)

        def pair_wait(engine, signal, item, parity):
            if isinstance(item.base, int):
                u = item.value()
                if u >= 0:
                    engine.wait_ge(signal.sem, (u // 2 + 1) * signal.per)
            else:
                half = signal.per // 2
                engine.wait_ge(signal.sem, item.at(half, signal.per - parity * half))

        block = ctx.enter_context(nc.Block())

        @block.sync
        def _(sp):
            sp.dma_start(cst[:, :], consts).then_inc(consts_in.sem, 16)
            sp.dma_start(id_sb[:, :], ids).then_inc(ids_in.sem, 16)
            sp.dma_start(pid_sb[:, :], pos_ids).then_inc(ids_in.sem, 16)
            sp.dma_start(ext[:, :, :].rearrange("p b k -> p (b k)"), mask[0:1, :].broadcast_to([TXT, B * TXT])
                         ).then_inc(mask_in.sem, 16)

            def load_a(l):
                sp.dma_start(wa[:, :], w_a[bass.ds(l, 1), :, :].rearrange("l p n -> (l p) n")).then_inc(wa_in.sem, 16)
                sp.dma_start(ra[:, :, :].rearrange("p r d -> p (r d)"),
                             r_a[bass.ds(l, 1), :].broadcast_to([TXT, 2 * D])).then_inc(wa_in.sem, 16)

            def load_b(l):
                sp.dma_start(wb[:, :], w_b[bass.ds(l, 1), :, :].rearrange("l p n -> (l p) n")).then_inc(wb_in.sem, 16)
                sp.dma_start(rb[:, :, :].rearrange("p r d -> p (r d)"),
                             r_b[bass.ds(l, 1), :].broadcast_to([TXT, 3 * D])).then_inc(wb_in.sem, 16)

            def load_c(l):
                sp.dma_start(wc[:, :], w_c[bass.ds(l, 1), :, :].rearrange("l p n -> (l p) n")).then_inc(wc_in.sem, 16)
                sp.dma_start(wc2[:, :], w_c2[bass.ds(l, 1), :, :].rearrange("l p n -> (l p) n")).then_inc(wc_in.sem, 16)
                sp.dma_start(rc[:, :, :].rearrange("p r d -> p (r d)"),
                             r_c[bass.ds(l, 1), :].broadcast_to([TXT, 2 * D])).then_inc(wc_in.sem, 16)

            load_a(0)
            load_b(0)
            load_c(0)
            for g in range(GROUPS):
                sp.wait_ge(emb_done.sem, g + 1)
                for b in range(G):
                    sp.dma_start(h_text[g * G + b, :, :], emb[:, g * G + b, :]).then_inc(emb_stored[g].sem, 16)
            sp.dma_start(wtok[:, :, :], w_tok).then_inc(jw_in.sem, 16)
            sp.dma_start(wj[:, :], w_joint).then_inc(jw_in.sem, 16)
            sp.dma_start(wk[:, :], w_joint128).then_inc(jw_in.sem, 16)
            sp.dma_start(rj[0:1, 0, :], r_joint[0:1, 0:D]).then_inc(jw_in.sem, 16)
            sp.dma_start(rj[1:IMG, 0, :], r_joint[0:1, D:2 * D].broadcast_to([IMG - 1, D])).then_inc(jw_in.sem, 16)
            sp.dma_start(rj[:, 1:7, :].rearrange("p r d -> p (r d)"),
                         r_joint[0:1, 2 * D:8 * D].broadcast_to([IMG, 6 * D])).then_inc(jw_in.sem, 16)

            def load_h(a, g, b):
                wait_alone(sp, hT_ps, a.minus(1), b + 1)
                wait_alone(sp, hb_ok, a.minus(1), b + 1)
                if isinstance(a.base, int) and a.value() < GROUPS:
                    sp.wait_ge(emb_stored[a.value()].sem, 16 * G)
                else:
                    wait_alone(sp, h_stored[b], a.minus(GROUPS), 16)
                sp.dma_start(h_tok[:, b, :], h_text[g * G + b, :, :]).then_inc(h_in[b].sem, 16)

            def step(c, c_group, a_next, a_group, reload=None):
                for b in range(G):
                    if c is not None:
                        wait_alone(sp, ho_ok, c, b + 1)
                        sp.dma_start(h_text[c_group * G + b, :, :], h_out[:, b, :]).then_inc(h_stored[b].sem, 16)
                    if a_next is not None and b > 0:
                        load_h(a_next, a_group, b - 1)
                if a_next is not None:
                    load_h(a_next, a_group, G - 1)

            def reload_a(a, l):
                wait_alone(sp, v_sb, a, G)
                wait_alone(sp, q_sb, a, 4)
                wait_alone(sp, k_sb, a, 2)
                wait_alone(sp, hb_ok, a, G)
                load_a(l)

            def reload_b(b_, l):
                wait_alone(sp, r1_ok, b_, G)
                wait_alone(sp, nb_ok, b_, G)
                load_b(l)

            def reload_c(c, l):
                wait_alone(sp, ho_ok, c, G)
                load_c(l)

            for b in range(G):
                load_h(Item(sp, 0), 0, b)

            def fixed_step(t):
                c = Item(sp, t - 2) if t >= 2 else None
                a_next = Item(sp, t + 1) if t + 1 < STEPS else None
                step(c, (t - 2) % GROUPS, a_next, (t + 1) % GROUPS)

            def reloads(t, g, layer):
                if g == GROUPS - 1:
                    reload_a(t, layer + 1)
                if g == 0:
                    reload_b(t.minus(1), layer)
                if g == 1:
                    reload_c(t.minus(2), layer)

            for t in range(GROUPS):
                fixed_step(t)
                if t == GROUPS - 1:
                    reloads(Item(sp, t), t, 0)
            with sp.Fori(1, LAYERS - 1) as layer:
                t0 = Item(sp, sp.snap(layer * GROUPS))
                for g in range(GROUPS):
                    t = t0.minus(-g)
                    step(t.minus(2), (g - 2) % GROUPS, t.minus(-1), (g + 1) % GROUPS)
                    reloads(t, g, layer)
            for t in range(STEPS - GROUPS, STEPS + 2):
                fixed_step(t)
                if t - (STEPS - GROUPS) < 2:
                    reloads(Item(sp, t), t % GROUPS, LAYERS - 1)

            text_over(sp)

            def load_d(u, p):
                wait_alone(sp, e_ps, u.minus(2), 1)
                sp.dma_start(pat[:, p, :], patches[:, bass.ds(u.value(), 1), :].rearrange("k b n -> k (b n)")
                             ).then_inc(pat_in[p].sem, 16)
                wait_alone(sp, h2_ok, u.minus(2), 2)
                wait_alone(sp, stq_ok, u.minus(2), 2)
                wait_alone(sp, xq_ok, u.minus(2), 2)
                sp.dma_start(hj[0:TXT, p, 1, :], h_text[bass.ds(u.value(), 1), :, :].rearrange("b t d -> (b t) d")
                             ).then_inc(ht_in[p].sem, 16)

            load_d(Item(sp, 0), 0)

            def jstep(d, e, f, p):
                if f is not None:
                    for it in range(2):
                        wait_alone(sp, yj_ok, f, it + 1)
                        sp.dma_start(out[bass.ds(f.value(), 1), OFF[it]:OFF[it] + ROWS[it], :].rearrange("b t d -> (b t) d"),
                                     yj[0:ROWS[it], p, it, :]).then_inc(y_stored[p].sem, 16)
                if d is not None:
                    if not (isinstance(d.base, int) and d.value() == B - 1):
                        pass
                    for it in range(2):
                        n = ROWS[it]
                        wait_alone(sp, pos_sb, d, 6 * (it + 1))
                        if it == 0 or True:
                            wait_alone(sp, pos_back[it], d.minus(1), 16)
                        sp.dma_start(pos_scratch[it, 0:n, :], pos_out[0:n, it, :, :].rearrange("p h w -> p (h w)")
                                     ).then_inc(pos_written[it].sem, 16)
                    for it in range(2):
                        n = ROWS[it]
                        wait_alone(sp, pos_written[it], d, 16)
                        wait_alone(sp, sj_sb, d.minus(1), 12 * (it + 1))
                        skew = bass.AP(pos_scratch.tensor, pos_scratch.offset + it * IMG * NH * WIN + n - 1,
                                       [[NH * WIN - 1, n], [WIN, NH], [1, S]])
                        sp.dma_start(pos_in[0:n, it, :, :], skew).then_inc(pos_back[it].sem, 16)

            def jstep_all(d, e, f, p):
                if d is not None and isinstance(d.base, int):
                    load_d(d.minus(-1), 1 - p)
                elif d is not None and p == 0:
                    load_d(d.minus(-1), 1)
                elif d is not None:
                    load_d(d.minus(-1), 0)
                jstep(d, e, f, p)

            def jprog():
                fixed = lambda u: Item(sp, u)
                jstep_all(fixed(0), None, None, 0)
                jstep_all(fixed(1), fixed(0), None, 1)
                jstep_all(fixed(2), fixed(1), fixed(0), 0)
                jstep_all(fixed(3), fixed(2), fixed(1), 1)
                with sp.Fori(2, B // 2 - 1) as pair:
                    even = Item(sp, sp.snap(pair * 2))
                    for p in range(2):
                        d = even.minus(-p)
                        jstep_all(d, d.minus(1), d.minus(2), p)
                jstep_all(fixed(B - 2), fixed(B - 3), fixed(B - 4), 0)
                jstep(fixed(B - 1), fixed(B - 2), fixed(B - 3), 1)
                jstep(None, fixed(B - 1), fixed(B - 2), 0)
                jstep(None, None, fixed(B - 1), 1)

            jprog()
            for p in range(2):
                sp.wait_ge(y_stored[p].sem, B // 2 * 32)
            for it in range(2):
                sp.wait_ge(pos_back[it].sem, B * 16)

        @block.gpsimd
        def _(pool):
            pool.wait_ge(ids_in.sem, 32)
            pool.indirect_dma_start(pos_row[:, :], None, pos_emb,
                                    bass.IndirectOffsetOnAxis(pid_sb[:, 0:1].bitcast(U32), 0)).then_inc(pos_row_in.sem, 16)
            for i in range(B):
                pool.indirect_dma_start(emb[:, i, :], None, tok_emb,
                                        bass.IndirectOffsetOnAxis(id_sb[:, i:i + 1].bitcast(U32), 0)
                                        ).then_inc(emb_in[i // G].sem, 16)
            pool.memset(v_tok[:, :, :, HD:HA], 1.0).then_inc(ones_set.sem, 1)
            pool.wait_ge(consts_in.sem, 16)

            def rstd(out_, var, n, ready, item, count, done):
                wait(pool, ready, item, count)
                nc.gpsimd.tensor_tensor(out_, var, power[0:out_.shape[0], 0:n], ALU.pow).then_inc(done.sem, 1)

            def step(a, b_, c):
                if a is not None:
                    layer_in(pool, wa_in, a)
                if b_ is not None:
                    layer_in(pool, wb_in, b_)
                    wait(pool, nb_ok, b_.minus(1), G)
                    nc.gpsimd.tensor_tensor(bias2[:, :], rb[:, 1, :], rb[:, 2, :], ALU.add).then_inc(bias2_ok.sem, 1)
                if c is not None:
                    layer_in(pool, wc_in, c)

                def first_norm(b):
                    if b_ is not None:
                        wait(pool, x1_ok, b_, b)
                        rstd(rs1[:, :], mv1[:, 1:2], 1, ve1_ok, b_, b + 1, rs1_ok)
                    if a is not None:
                        wait(pool, h_in[b], a, 16)
                        if b_ is not None:
                            wait(pool, r1_ok, b_, b + 1)
                        nc.gpsimd.tensor_tensor(h_bias[:, b, :], h_tok[:, b, :], ra[:, 1, :], ALU.add).then_inc(hb_ok.sem, 1)
                    if b_ is not None:
                        if b == 0:
                            wait(pool, bias2_ok, b_, 1)
                        wait(pool, x1_ok, b_, b + 1)
                        wait(pool, nb_ok, b_, b)
                        nc.gpsimd.tensor_tensor(nb_tmp[:, :], x1[:, b, :], rb[:, 0, :], ALU.mult).then_inc(nbt_ok.sem, 1)
                        wait(pool, nbt_ok, b_, b + 1)
                        if c is not None:
                            wait(pool, r2_ok, c, b + 1)
                        nc.gpsimd.tensor_tensor(n_bias[:, b, :], nb_tmp[:, :], bias2[:, :], ALU.add).then_inc(nb_ok.sem, 1)

                for b in range(G):
                    if a is not None:
                        wait(pool, masked, a, 3 * (b + 1))
                        if isinstance(a.base, int):
                            e = ext[:, (a.value() % GROUPS) * G + b, :].unsqueeze(1)
                        else:
                            e = ext[:, bass.ds((a.value() % GROUPS) * G + b, 1), :]
                        if isinstance(a.base, int) and a.value() == 0:
                            pool.wait_ge(ext_ready.sem, B // G)
                        nc.gpsimd.tensor_tensor(sc[:, b, :, :], sc[:, b, :, :], e.broadcast_to([TXT, NH, TXT]),
                                                ALU.add).then_inc(biased.sem, 1)
                    if b > 0:
                        first_norm(b - 1)
                    if c is not None:
                        wait(pool, x2_ok, c, b)
                        rstd(rs2[:, :], mv2[:, 1:2], 1, ve2_ok, c, b + 1, rs2_ok)
                        wait(pool, x2_ok, c, b + 1)
                        wait(pool, ho_ok, c, b)
                        nc.gpsimd.tensor_tensor(ho_tmp[:, :], x2[:, :], rc[:, 0, :], ALU.mult).then_inc(hot_ok.sem, 1)
                        wait(pool, hot_ok, c, b + 1)
                        wait(pool, h_stored[b], c.minus(1), 16)
                        nc.gpsimd.tensor_tensor(h_out[:, b, :], ho_tmp[:, :], rc[:, 1, :], ALU.add).then_inc(ho_ok.sem, 1)
                first_norm(G - 1)

            text_steps(pool, step)

            text_over(pool)
            pool.memset(vj[:, :, :, :, HD:HA], 1.0).then_inc(pads.sem, 1)
            for m in (mve, mvq, mv3, mv4):
                pool.memset(m[:], 0.0).then_inc(pads.sem, 1)
            pool.wait_ge(jw_in.sem, 96)
            pool.wait_ge(pads.sem, 5)

            def jstep(d, e, f, p):
                if d is not None:
                    rstd(rse[:, :], mve[:, 1:2], 1, vee_ok, d, 1, rse_ok)
                    wait(pool, e1_ok, d, 1)
                    nc.gpsimd.tensor_tensor(e2[:, :], e1[:, :], rj[:, 1, :], ALU.mult).then_inc(e2_ok.sem, 1)
                    wait(pool, e2_ok, d, 1)
                    wait(pool, h2_ok, d.minus(2), 2)
                    nc.gpsimd.tensor_tensor(hj[:, p, 0, :], e2[:, :], rj[:, 2, :], ALU.add).then_inc(e3_ok.sem, 1)
                    rstd(rsq[:, :], mvq[:, :, 1], 2, veq_ok, d, 1, rsq_ok)
                    for it in range(2):
                        n = ROWS[it]
                        wait(pool, xq_ok, d, it + 1)
                        wait(pool, r3_ok, d.minus(2), 2)
                        nc.gpsimd.tensor_tensor(xqb[0:n, p, it, :], xq[0:n, it, :], rj[0:n, 4, :], ALU.add).then_inc(xqb_ok.sem, 1)
                if e is not None:
                    rstd(rs3[:, :], mv3[:, :, 1], 2, ve3_ok, e, 1, rs3_ok)
                    for it in range(2):
                        n = ROWS[it]
                        wait(pool, x3_ok, e, it + 1)
                        nc.gpsimd.tensor_tensor(t3[0:n, it, :], x3[0:n, it, :], rj[0:n, 5, :], ALU.mult).then_inc(t3_ok.sem, 1)
                    for it in range(2):
                        n = ROWS[it]
                        wait(pool, t3_ok, e, it + 1)
                        nc.gpsimd.tensor_tensor(t4[0:n, it, :], t3[0:n, it, :], rj[0:n, 6, :], ALU.add).then_inc(t4_ok.sem, 1)
                    for it in range(2):
                        n = ROWS[it]
                        wait(pool, t4_ok, e, it + 1)
                        wait(pool, yj_ok, e.minus(2), 2)
                        nc.gpsimd.tensor_tensor(h2[0:n, 1 - p, it, :], t4[0:n, it, :], hj[0:n, 1 - p, it, :], ALU.add).then_inc(h2_ok.sem, 1)
                    rstd(rs4[:, :], mv4[:, :, 1], 2, ve4_ok, e, 1, rs4_ok)

            joint_steps(pool, jstep)

        @block.scalar
        def _(act):
            act.wait_ge(consts_in.sem, 16)

            def step(a, b_, c):
                if a is not None:
                    for b in range(G):
                        wait(act, hT_ps, a, b + 1)
                        if b == 0:
                            wait(act, v_ps, a.minus(1), G)
                        nc.scalar.activation(hT[:, :, b * TXT:(b + 1) * TXT],
                                             bank[b % 2][0:HALF, 0:2 * TXT].rearrange("p (c t) -> p c t", c=2),
                                             ACT.Identity).then_inc(hT_sb.sem, 1)
                    layer_in(act, wa_in, a)
                if c is not None:
                    layer_in(act, wc_in, c)

                def gelus(m):
                    if c is not None:
                        wait(act, fc_ps, c, m + 1)
                        if m == 0:
                            wait(act, ml_ps, c.minus(1), G)
                        nc.scalar.activation(gel[:, m, :], bank[6 + m % 2][:, 0:GT], ACT.Gelu_apprx_tanh,
                                             bias=wc2[:, C2_COL + m:C2_COL + m + 1]).then_inc(gelu_ok.sem, 1)

                def queries(m):
                    if a is not None:
                        wait(act, qk_ps, a, 2 * m + 1)
                        if m == 0:
                            wait(act, s_ps, a.minus(1), G)
                        for par, dst in enumerate((q_even, q_odd)):
                            nc.scalar.activation(dst[:, m, :], bank[(2 * m) % 3][0:HALF, 0:GT], ACT.Identity,
                                                 bias=wa[:, A_COL + 2 * par + m:A_COL + 2 * par + m + 1],
                                                 scale=cst[0:HALF, CST_EVEN + par:CST_EVEN + par + 1]).then_inc(q_sb.sem, 1)

                gelus(0)
                gelus(1)
                queries(0)
                gelus(2)
                gelus(3)
                queries(1)
                gelus(4)
                gelus(5)

                def attended(b):
                    if b_ is not None:
                        wait(act, aT_ps, b_, b + 1)
                        wait(act, pj_ps, b_, b)
                        nc.scalar.activation(aT[:, :], bank[5][0:HALF, 0:2 * TXT], ACT.Identity).then_inc(aT_sb.sem, 1)

                for b in range(G):
                    if b > 0:
                        attended(b - 1)
                    if b_ is not None:
                        for half in range(2):
                            wait(act, pT_ps, b_, 2 * b + half + 1)
                            wait(act, pv_ps, b_, b)
                            nc.scalar.activation(pT[:, half, :], bank[3 + half][0:TXT, 0:6 * TXT], ACT.Identity).then_inc(pT_sb.sem, 1)
                    if a is not None:
                        wait(act, shifted, a, b + 1)
                        nc.scalar.activation(sc[:, b, :, :], sc[:, b, :, :], ACT.Exp).then_inc(expd.sem, 1)
                attended(G - 1)

            text_steps(act, step)

            text_over(act)
            act.wait_ge(jw_in.sem, 96)
            act.wait_ge(r8_ok.sem, 2)

            def jstep(d, e, f, p):
                if e is not None:
                    for it in range(2):
                        n = ROWS[it]
                        wait(act, nm_ok, e, it + 1)
                        for h in range(NH):
                            nc.scalar.activation(scj[0:n, it, h, :], scj[0:n, it, h, :], ACT.Exp,
                                                 bias=nmj[0:n, it, h:h + 1]).then_inc(ej_ok.sem, 1)
                if d is not None:
                    wait(act, xqT_ps, d, 1)
                    nc.scalar.activation(xqT[:, :, :], bank[0][0:HALF, 0:2 * S].rearrange("p (c t) -> p c t", c=2),
                                         ACT.Identity).then_inc(xqT_sb.sem, 1)
                if e is not None:
                    for tr in range(4):
                        for jt in range(2):
                            wait(act, ptj_ps, e, 2 * tr + jt + 1)
                            if tr >= 2:
                                wait(act, pvj_ps, e, tr - 1)
                            else:
                                wait(act, pvj_ps, e.minus(1), tr + 3)
                            nc.scalar.activation(pTj[0:ROWS[jt], tr % 2, jt, :], bank[4 + jt][0:ROWS[jt], 0:3 * S],
                                                 ACT.Identity).then_inc(ptj_sb.sem, 1)
                    wait(act, atT_ps, e, 1)
                    nc.scalar.activation(aTj[:, :], bank[6][0:HALF, 0:2 * S], ACT.Identity).then_inc(atT_sb.sem, 1)
                if f is not None:
                    for m in range(MH):
                        wait(act, fj_ps, f, m // 3 + 1)
                        if m == 0:
                            wait(act, mj_ps, f.minus(1), 1)
                        nc.scalar.activation(gj[:, m, :], bank[7][:, (m % 3) * S:(m % 3 + 1) * S], ACT.Gelu,
                                             bias=wk[:, K_INB + m:K_INB + m + 1]).then_inc(gj_ok.sem, 1)
                if d is not None:
                    for rnd in range(6):
                        for x in range(2):
                            if (rnd + x) % 2 == 0:
                                continue
                        it, q4 = rnd // 3, rnd % 3
                        n = ROWS[it]
                        wait(act, pos_ps, d, rnd + 1)
                        wait(act, pos_written[it], d.minus(1), 16)
                        nc.scalar.activation(pos_out[0:n, it, 4 * q4 + 1:4 * q4 + 4:2, :],
                                             bank[1][0:n, 0:2 * WIN].rearrange("p (h w) -> p h w", h=2),
                                             ACT.Identity).then_inc(pos_sb.sem, 1)

            joint_steps(act, jstep)

        @block.tensor
        def _(pe):
            pe.wait_ge(consts_in.sem, 16)
            mm = nc.tensor.matmul

            def step(a, b_, c):
                if c is not None:
                    for b in range(G):
                        wait(pe, x1_ok, c, b + 1)
                        if b < 2:
                            wait(pe, r2_ok, c.minus(1), b + 3)
                        else:
                            wait(pe, nT_sb, c, 2 * (b - 1))
                        for k in range(2):
                            last = nc.tensor.transpose(bank[6 + b % 2][0:HALF, k * TXT:(k + 1) * TXT],
                                                       x1[:, b, k * HALF:(k + 1) * HALF], ident[0:TXT, 0:TXT])
                        last.then_inc(nT_ps.sem, 1)
                if a is not None:
                    for b in range(G):
                        wait(pe, h_in[b], a, 16)
                        if b == 0:
                            wait(pe, v_sb, a.minus(1), G)
                        if b == 1:
                            wait(pe, masked, a.minus(1), 3 * G)
                        if b >= 2:
                            wait(pe, hT_sb, a, b - 1)
                        for k in range(2):
                            last = nc.tensor.transpose(bank[b % 2][0:HALF, k * TXT:(k + 1) * TXT],
                                                       h_tok[:, b, k * HALF:(k + 1) * HALF], ident[0:TXT, 0:TXT])
                        last.then_inc(hT_ps.sem, 1)
                    layer_in(pe, wa_in, a)
                if c is not None:
                    layer_in(pe, wc_in, c)
                    wait(pe, nT_sb, c, 2 * G)
                if b_ is not None:
                    layer_in(pe, wb_in, b_)

                def up(m):
                    if c is not None:
                        if m >= 2:
                            wait(pe, gelu_ok, c, m - 1)
                        for k in range(2):
                            last = mm(bank[6 + m % 2][:, 0:GT], wc[:, k * HID + m * 128:k * HID + (m + 1) * 128],
                                      nT[:, k, :], start=(k == 0), stop=(k == 1))
                        last.then_inc(fc_ps.sem, 1)

                def qk(m):
                    if a is not None:
                        if m == 0:
                            wait(pe, hT_sb, a, G)
                        if m == 3:
                            wait(pe, q_sb, a, 2)
                        col = (m % 2) * D + (m // 2) * HALF
                        for k in range(2):
                            last = mm(bank[m % 3][0:HALF, 0:GT], wa[:, k * 2 * D + col:k * 2 * D + col + HALF],
                                      hT[:, k, :], start=(k == 0), stop=(k == 1))
                        last.then_inc(qk_ps.sem, 1)

                up(0)
                up(1)
                qk(0)
                up(2)
                qk(1)
                up(3)
                qk(2)
                up(4)
                qk(3)
                up(5)

                def scores(b):
                    if b == 0:
                        wait(pe, q_sb, a, 4)
                        wait(pe, k_sb, a, 2)
                    else:
                        wait(pe, v_sb, a, b)
                        wait(pe, masked, a, 3 * b)
                    for half in range(2):
                        for par, q in enumerate((q_even, q_odd)):
                            for r in range(3):
                                col = (2 * half + par) * TXT
                                last = mm(bank[r][0:TXT, col:col + TXT],
                                          q[32 * r:32 * r + 32, half, b * TXT:(b + 1) * TXT],
                                          kT[32 * r:32 * r + 32, half, b * TXT:(b + 1) * TXT],
                                          start=True, stop=True, tile_position=(32 * r, 0))
                    last.then_inc(s_ps.sem, 1)

                def attended_t(b):
                    wait(pe, att_ok, b_, b + 1)
                    for k in range(2):
                        last = nc.tensor.transpose(bank[5][0:HALF, k * TXT:(k + 1) * TXT],
                                                   att[:, k * HALF:(k + 1) * HALF], ident[0:TXT, 0:TXT])
                    last.then_inc(aT_ps.sem, 1)

                def project(b):
                    wait(pe, aT_sb, b_, b + 1)
                    for k in range(2):
                        last = mm(bank[5][0:TXT, 0:D], aT[:, k * TXT:(k + 1) * TXT], wb[:, k * D:(k + 1) * D],
                                  start=(k == 0), stop=(k == 1))
                    last.then_inc(pj_ps.sem, 1)

                for b in range(G):
                    if a is not None:
                        scores(b)
                    if b_ is not None:
                        if b > 0:
                            attended_t(b - 1)
                        wait(pe, expd, b_, b + 1)
                        for half in range(2):
                            if b > 0:
                                wait(pe, pT_sb, b_, 2 * b - 1 + half)
                            else:
                                wait(pe, pT_sb, b_.minus(1), 2 * G - 1 + half)
                            for i in range(6):
                                last = nc.tensor.transpose(bank[3 + half][0:TXT, i * TXT:(i + 1) * TXT],
                                                           sc[:, b, 6 * half + i, :], ident[0:TXT, 0:TXT])
                            last.then_inc(pT_ps.sem, 1)
                        if b > 0:
                            project(b - 1)
                    if c is not None:
                        wait(pe, gelu_ok, c, MH)
                        if b >= 2:
                            wait(pe, r2_ok, c, b - 1)
                        for m in range(MH):
                            last = mm(bank[6 + b % 2][0:TXT, 0:D], gel[:, m, b * TXT:(b + 1) * TXT],
                                      wc2[:, m * D:(m + 1) * D], start=(m == 0), stop=(m == MH - 1))
                        last.then_inc(ml_ps.sem, 1)
                    if b_ is not None:
                        wait(pe, v_sb, b_, b + 1)
                        wait(pe, pT_sb, b_, 2 * b + 2)
                        if b > 0:
                            wait(pe, r1_ok, b_, b)
                        else:
                            wait(pe, r1_ok, b_.minus(1), G)
                        for h in range(NH):
                            last = mm(bank[5][0:TXT, h * HA:(h + 1) * HA], pT[:, h // 6, (h % 6) * TXT:(h % 6 + 1) * TXT],
                                      v_tok[:, b, h, :], start=True, stop=True)
                        last.then_inc(pv_ps.sem, 1)
                    if a is not None:
                        wait(pe, masked, a, 3 * b + 1)
                        for k in range(2):
                            last = mm(bank[0][0:TXT, 0:D], hT[:, k, b * TXT:(b + 1) * TXT],
                                      wa[:, A_V + k * D:A_V + (k + 1) * D], start=(k == 0), stop=(k == 1))
                        last.then_inc(v_ps.sem, 1)
                if b_ is not None:
                    attended_t(G - 1)
                    project(G - 1)

            text_steps(pe, step)

            text_over(pe)
            pe.wait_ge(jw_in.sem, 96)
            for g in ((v_sb, G), (masked, 3 * G), (pT_sb, 2 * G), (r1_ok, G), (r2_ok, G)):
                wait(pe, g[0], Item(pe, STEPS - 1), g[1])
            for m in range(6):
                if m >= 2:
                    pe.wait_ge(rel_ok.sem, m - 1)
                for k in range(2):
                    last = mm(bank[m % 2][:, 0:NT], wj[:, J_R + k * 768 + m * 128:J_R + k * 768 + (m + 1) * 128],
                              wj[:, J_POS + k * NT:J_POS + (k + 1) * NT], start=(k == 0), stop=(k == 1))
                last.then_inc(rel_ps.sem, 1)
            pe.wait_ge(rel_ok.sem, 6)

            def jstep(d, e, f, p):
                if d is not None:
                    pair_wait(pe, pat_in[p], d, p)
                    wait(pe, pos_sb, d.minus(1), 12)
                    for k in range(3):
                        last = mm(bank[0][0:IMG, 0:D], pat[:, p, k * IMG:(k + 1) * IMG], wtok[:, k, :],
                                  start=(k == 0), stop=(k == 2))
                    last.then_inc(e_ps.sem, 1)

                def content(rnd):
                    it, half = rnd // 2, rnd % 2
                    n = ROWS[it]
                    if rnd == 0:
                        wait(pe, qc_ok, e, 2)
                        wait(pe, kj_ok, e, 2)
                        wait(pe, sj_sb, e.minus(1), 24)
                    else:
                        wait(pe, sj_sb, e, 6 * rnd)
                    for i in range(3):
                        for par in range(2):
                            m = 3 * half + i
                            last = mm(bank[2 + par][0:n, i * S:(i + 1) * S],
                                      qc[64 * par:64 * par + 64, 1 - p, m, OFF[it]:OFF[it] + n],
                                      kj[64 * par:64 * par + 64, 1 - p, m, :],
                                      start=True, stop=True, tile_position=(64 * par, 0))
                    last.then_inc(sj_ps.sem, 1)

                if e is not None:
                    content(0)
                if f is not None:
                    for it in range(2):
                        wait(pe, x4_ok, f, it + 1)
                    wait(pe, yj_ok, f.minus(1), 2)
                    for it in range(2):
                        n = ROWS[it]
                        for k in range(2):
                            last = nc.tensor.transpose(bank[7][0:HALF, k * S + OFF[it]:k * S + OFF[it] + n],
                                                       x4[0:n, it, k * HALF:(k + 1) * HALF], ident[0:n, 0:n])
                    last.then_inc(x4T_ps.sem, 1)
                if e is not None:
                    content(1)
                    content(2)
                    content(3)
                if d is not None:
                    for it in range(2):
                        wait(pe, xq_ok, d, it + 1)
                    wait(pe, e0_ok, d, 1)
                    for it in range(2):
                        n = ROWS[it]
                        for k in range(2):
                            last = nc.tensor.transpose(bank[0][0:HALF, k * S + OFF[it]:k * S + OFF[it] + n],
                                                       xq[0:n, it, k * HALF:(k + 1) * HALF], ident[0:n, 0:n])
                    last.then_inc(xqT_ps.sem, 1)

                def triple(tr):
                    for it in range(2):
                        wait(pe, ej_ok, e, 12 * it + 3 * tr + 3)
                    for jt in range(2):
                        if tr == 0:
                            wait(pe, ptj_sb, e.minus(1), 7 + jt)
                        else:
                            wait(pe, ptj_sb, e, 2 * tr - 1 + jt)
                        for i in range(3):
                            for it in range(2):
                                n = ROWS[it]
                                last = nc.tensor.transpose(bank[4 + jt][0:ROWS[jt], i * S + OFF[it]:i * S + OFF[it] + n],
                                                           scj[0:n, it, 3 * tr + i, OFF[jt]:OFF[jt] + ROWS[jt]],
                                                           ident[0:n, 0:n])
                        last.then_inc(ptj_ps.sem, 1)

                def values(tr):
                    wait(pe, ptj_sb, e, 2 * tr + 2)
                    if tr == 0:
                        wait(pe, vj_ok, e, 2)
                        wait(pe, r3_ok, e.minus(1), 2)
                    for i in range(3):
                        for it in range(2):
                            n = ROWS[it]
                            h = 3 * tr + i
                            for jt in range(2):
                                last = mm(bank[6][0:n, it * NH * HA + h * HA:it * NH * HA + (h + 1) * HA],
                                          pTj[0:ROWS[jt], tr % 2, jt, i * S + OFF[it]:i * S + OFF[it] + n],
                                          vj[0:ROWS[jt], 1 - p, jt, h, :], start=(jt == 0), stop=(jt == 1))
                    last.then_inc(pvj_ps.sem, 1)

                if e is not None:
                    for tr in range(4):
                        triple(tr)
                        if tr > 0:
                            values(tr - 1)
                    values(3)
                if d is not None:
                    wait(pe, xqT_sb, d, 1)
                    wait(pe, pos_sb, d.minus(1), 12)
                    for half in range(2):
                        if half == 1:
                            pass
                        for i in range(3):
                            m = 3 * half + i
                            last = mm(bank[1 - half][:, i * S:(i + 1) * S], wj[:, J_Q + m * 128:J_Q + (m + 1) * 128],
                                      xqT[:, half, :], start=True, stop=True)
                        last.then_inc(qj_ps.sem, 1)
                if e is not None:
                    for it in range(2):
                        wait(pe, atj_ok, e, it + 1)
                    for it in range(2):
                        n = ROWS[it]
                        for k in range(2):
                            last = nc.tensor.transpose(bank[6][0:HALF, k * S + OFF[it]:k * S + OFF[it] + n],
                                                       atj[0:n, it, k * HALF:(k + 1) * HALF], ident[0:n, 0:n])
                    last.then_inc(atT_ps.sem, 1)
                if d is not None:
                    for half in range(2):
                        wait(pe, qc_ok, d, half + 1)
                        wait(pe, qr_ok, d, half + 1)
                        for i in range(3):
                            m = 3 * half + i
                            last = mm(bank[1 - half][:, i * S:(i + 1) * S], wj[:, J_K + m * 128:J_K + (m + 1) * 128],
                                      xqT[:, half, :], start=True, stop=True)
                        last.then_inc(kj_ps.sem, 1)
                if e is not None:
                    wait(pe, atT_sb, e, 1)
                    for it in range(2):
                        n = ROWS[it]
                        for k in range(2):
                            last = mm(bank[6][0:n, it * D:(it + 1) * D], aTj[:, k * S + OFF[it]:k * S + OFF[it] + n],
                                      wj[:, J_O + k * D:J_O + (k + 1) * D], start=(k == 0), stop=(k == 1))
                    last.then_inc(wo_ps.sem, 1)
                if f is not None:
                    wait(pe, x4T_sb, f, 1)
                    for half in range(2):
                        if half == 1:
                            wait(pe, gj_ok, f, 3)
                        for i in range(3):
                            m = 3 * half + i
                            for k in range(2):
                                last = mm(bank[7][:, i * S:(i + 1) * S],
                                          wj[:, J_IN + k * HID + m * 128:J_IN + k * HID + (m + 1) * 128],
                                          x4T[:, k, :], start=(k == 0), stop=(k == 1))
                        last.then_inc(fj_ps.sem, 1)
                if d is not None:
                    wait(pe, kj_ok, d, 1)
                    for it in range(2):
                        n = ROWS[it]
                        for k in range(2):
                            last = mm(bank[1][0:n, it * D + k * HALF:it * D + (k + 1) * HALF],
                                      xqT[:, k, OFF[it]:OFF[it] + n], wj[:, J_V + k * HALF:J_V + (k + 1) * HALF],
                                      start=True, stop=True)
                    last.then_inc(vj_ps.sem, 1)
                    for rnd in range(6):
                        it, q4 = rnd // 3, rnd % 3
                        n = ROWS[it]
                        if rnd == 0:
                            wait(pe, kj_ok, d, 2)
                            wait(pe, vj_ok, d, 2)
                        else:
                            wait(pe, pos_sb, d, 2 * rnd)
                        first = (S - 1) - (OFF[it] + n - 1)
                        w = S + n - 1
                        for i in range(2):
                            for par in range(2):
                                m = 2 * q4 + i
                                last = mm(bank[par][0:n, i * WIN:i * WIN + w],
                                          qr[64 * par:64 * par + 64, m, OFF[it]:OFF[it] + n],
                                          rel[64 * par:64 * par + 64, m, first:first + w],
                                          start=True, stop=True, tile_position=(64 * par, 0))
                        last.then_inc(pos_ps.sem, 1)
                if f is not None:
                    wait(pe, gj_ok, f, 6)
                    for it in range(2):
                        n = ROWS[it]
                        for m in range(MH):
                            last = mm(bank[7][0:n, it * D:(it + 1) * D], gj[:, m, OFF[it]:OFF[it] + n],
                                      wk[:, K_OUT + m * D:K_OUT + (m + 1) * D], start=(m == 0), stop=(m == MH - 1))
                    last.then_inc(mj_ps.sem, 1)

            joint_steps(pe, jstep)

        @block.vector
        def _(dve):
            V = nc.vector
            dve.wait_ge(mask_in.sem, 16)
            dve.wait_ge(consts_in.sem, 16)
            flat = ext[:, :, :].rearrange("p b k -> p (b k)")
            V.tensor_scalar(flat, flat, -1.0, 1.0, ALU.mult, ALU.add).then_inc(ext_one.sem, 1)
            dve.wait_ge(ext_one.sem, 1)
            V.tensor_scalar(flat, flat, FMIN, None, ALU.mult).then_inc(ext_scaled.sem, 1)
            dve.wait_ge(ext_scaled.sem, 1)
            neg = cst[0:TXT, CST_NEG:CST_NEG + TXT].unsqueeze(1).broadcast_to([TXT, G, TXT])
            for g in range(B // G):
                V.tensor_tensor(ext[:, g * G:(g + 1) * G, :], ext[:, g * G:(g + 1) * G, :], neg, ALU.add).then_inc(ext_ready.sem, 1)
            dve.wait_ge(pos_row_in.sem, 16)
            for g in range(GROUPS):
                dve.wait_ge(emb_in[g].sem, 16 * G)
                V.tensor_tensor(emb[:, g * G:(g + 1) * G, :], emb[:, g * G:(g + 1) * G, :],
                                pos_row[:, :].unsqueeze(1).broadcast_to([TXT, G, D]), ALU.add).then_inc(emb_done.sem, 1)
            dve.wait_ge(ones_set.sem, 1)
            causal = cst[0:TXT, CST_CAUSAL:CST_CAUSAL + TXT].unsqueeze(1).broadcast_to([TXT, 2, TXT])

            def step(a, b_, c):
                if c is not None:
                    layer_in(dve, wc_in, c)
                    for b in range(G):
                        wait(dve, nT_ps, c, b + 1)
                        if b == 0:
                            wait(dve, fc_ps, c.minus(1), MH)
                        for k in range(2):
                            V.tensor_scalar(nT[:, k, b * TXT:(b + 1) * TXT], bank[6 + b % 2][0:HALF, k * TXT:(k + 1) * TXT],
                                            wc[:, C_COL + k:C_COL + k + 1], wc[:, C_COL + 2 + k:C_COL + 3 + k],
                                            ALU.mult, ALU.add).then_inc(nT_sb.sem, 1)
                if a is not None:
                    layer_in(dve, wa_in, a)
                    for m in range(2):
                        wait(dve, qk_ps, a, 2 * m + 2)
                        if m == 0:
                            wait(dve, s_ps, a.minus(1), G)
                        V.tensor_scalar(kT[:, m, :], bank[(2 * m + 1) % 3][0:HALF, 0:GT],
                                        wa[:, A_COL + 4 + m:A_COL + 5 + m], HD ** -0.5, ALU.add, ALU.mult).then_inc(k_sb.sem, 1)

                def first_norm_stats(b):
                    wait(dve, pj_ps, b_, b + 1)
                    wait(dve, x1_ok, b_, b)
                    wait(dve, hb_ok, b_, b + 1)
                    V.tensor_tensor(r1[:, :], bank[5][0:TXT, 0:D], h_bias[:, b, :], ALU.add).then_inc(r1_ok.sem, 1)
                    wait(dve, r1_ok, b_, b + 1)
                    V.bn_stats(st1[:, :], r1[:, :]).then_inc(st1_ok.sem, 1)
                    wait_alone(dve, st1_ok, b_, b + 1)
                    V.bn_aggr(mv1[:, :], st1[:, :]).then_inc(mv1_ok.sem, 1)
                    wait(dve, mv1_ok, b_, b + 1)
                    V.tensor_scalar(mv1[:, 1:2], mv1[:, 1:2], EPS, None, ALU.add).then_inc(ve1_ok.sem, 1)

                def first_norm(b):
                    wait(dve, rs1_ok, b_, b + 1)
                    if c is not None:
                        wait(dve, nT_ps, c, b + 1)
                        wait(dve, nb_ok, c, b + 1)
                    V.tensor_scalar(x1[:, b, :], r1[:, :], mv1[:, 0:1], rs1[:, 0:1], ALU.subtract, ALU.mult).then_inc(x1_ok.sem, 1)

                for b in range(G):
                    if a is not None:
                        wait(dve, s_ps, a, b + 1)
                        if b_ is not None:
                            wait(dve, pT_ps, b_, 2 * b + 2)
                        for r in range(3):
                            dst = sc[:, b, :, :].rearrange("p (half r par) k -> p half r par k", half=2, r=3)[:, :, r]
                            src = bank[r][0:TXT, 0:4 * TXT].rearrange("p (half par k) -> p half par k", half=2, par=2)
                            msk = cst[0:TXT, CST_CAUSAL:CST_CAUSAL + TXT].unsqueeze(1).unsqueeze(1).broadcast_to([TXT, 2, 2, TXT])
                            V.tensor_tensor(dst, src, msk, ALU.mult).then_inc(masked.sem, 1)
                    if b_ is not None and b > 0:
                        first_norm_stats(b - 1)
                    if c is not None:
                        wait(dve, ml_ps, c, b + 1)
                        wait(dve, x2_ok, c, b)
                        wait(dve, nb_ok, c, b + 1)
                        V.tensor_tensor(r2[:, :], bank[6 + b % 2][0:TXT, 0:D], n_bias[:, b, :], ALU.add).then_inc(r2_ok.sem, 1)
                        wait(dve, r2_ok, c, b + 1)
                        V.bn_stats(st2[:, :], r2[:, :]).then_inc(st2_ok.sem, 1)
                        wait_alone(dve, st2_ok, c, b + 1)
                        V.bn_aggr(mv2[:, :], st2[:, :]).then_inc(mv2_ok.sem, 1)
                        wait(dve, mv2_ok, c, b + 1)
                        V.tensor_scalar(mv2[:, 1:2], mv2[:, 1:2], EPS, None, ALU.add).then_inc(ve2_ok.sem, 1)
                    if a is not None:
                        wait(dve, biased, a, b + 1)
                        V.tensor_reduce(mx[:, b, :], sc[:, b, :, :], AX.X, ALU.max).then_inc(maxed.sem, 1)
                        wait(dve, maxed, a, b + 1)
                        V.tensor_tensor(sc[:, b, :, :], sc[:, b, :, :], mx[:, b, :].unsqueeze(2).broadcast_to([TXT, NH, TXT]),
                                        ALU.subtract).then_inc(shifted.sem, 1)
                    if b_ is not None and b > 0:
                        first_norm(b - 1)
                    if c is not None:
                        wait(dve, rs2_ok, c, b + 1)
                        wait(dve, hot_ok, c, b)
                        V.tensor_scalar(x2[:, :], r2[:, :], mv2[:, 0:1], rs2[:, 0:1], ALU.subtract, ALU.mult).then_inc(x2_ok.sem, 1)
                    if b_ is not None:
                        wait(dve, pv_ps, b_, b + 1)
                        pv = bank[5][0:TXT, 0:NH * HA].rearrange("p (h e) -> p h e", h=NH)
                        V.reciprocal(rden[:, :], pv[:, :, HD]).then_inc(rden_ok.sem, 1)
                        wait(dve, rden_ok, b_, b + 1)
                        wait(dve, aT_ps, b_, b)
                        V.tensor_tensor(att[:, :].rearrange("p (h e) -> p h e", h=NH), pv[:, :, 0:HD],
                                        rden[:, :].unsqueeze(2).broadcast_to([TXT, NH, HD]), ALU.mult).then_inc(att_ok.sem, 1)
                    if a is not None:
                        wait(dve, v_ps, a, b + 1)
                        if b_ is not None:
                            wait(dve, pv_ps, b_, b + 1)
                        V.tensor_tensor(v_tok[:, b, :, 0:HD], bank[0][0:TXT, 0:D].rearrange("p (h e) -> p h e", h=NH),
                                        ra[:, 0, :].rearrange("p (h e) -> p h e", h=NH), ALU.add).then_inc(v_sb.sem, 1)
                if b_ is not None:
                    first_norm_stats(G - 1)
                    first_norm(G - 1)

            text_steps(dve, step)

            text_over(dve)
            dve.wait_ge(jw_in.sem, 96)
            dve.wait_ge(pads.sem, 5)
            V.tensor_scalar(rw8[:, :], wk[:, K_RW:K_RW + 6], DH ** -0.5, None, ALU.mult).then_inc(r8_ok.sem, 1)
            V.tensor_scalar(rr8[:, :], wk[:, K_RR:K_RR + 6], DH ** -0.5, None, ALU.mult).then_inc(r8_ok.sem, 1)
            dve.wait_ge(r8_ok.sem, 2)
            for m in range(6):
                dve.wait_ge(rel_ps.sem, m + 1)
                V.tensor_copy(rel[:, m, :], bank[m % 2][:, 0:NT]).then_inc(rel_ok.sem, 1)

            def norm_stats(src, stats, mv, stats_ok, mv_ok, ve_ok, item, eps, ready):
                for it in range(2):
                    n = ROWS[it]
                    ready(it)
                    V.bn_stats(stats[0:n, it, :], src[0:n, it, :]).then_inc(stats_ok.sem, 1)
                for it in range(2):
                    n = ROWS[it]
                    wait_alone(dve, stats_ok, item, it + 1)
                    V.bn_aggr(mv[0:n, it, :], stats[0:n, it, :]).then_inc(mv_ok.sem, 1)
                wait(dve, mv_ok, item, 2)
                V.tensor_scalar(mv[:, :, 1], mv[:, :, 1], eps, None, ALU.add).then_inc(ve_ok.sem, 1)

            def jstep(d, e, f, p):
                if d is not None:
                    wait(dve, e_ps, d, 1)
                    wait(dve, e1_ok, d.minus(1), 1)
                    V.tensor_tensor(e0[:, :], bank[0][0:IMG, 0:D], rj[:, 0, :], ALU.add).then_inc(e0_ok.sem, 1)
                    wait(dve, e0_ok, d, 1)
                    V.bn_stats(ste[:, :], e0[:, :]).then_inc(ste_ok.sem, 1)
                    wait_alone(dve, ste_ok, d, 1)
                    V.bn_aggr(mve[:, :], ste[:, :]).then_inc(mve_ok.sem, 1)
                    wait(dve, mve_ok, d, 1)
                    V.tensor_scalar(mve[:, 1:2], mve[:, 1:2], EPS, None, ALU.add).then_inc(vee_ok.sem, 1)
                    wait(dve, rse_ok, d, 1)
                    wait(dve, e2_ok, d.minus(1), 1)
                    V.tensor_scalar(e1[:, :], e0[:, :], mve[:, 0:1], rse[:, 0:1], ALU.subtract, ALU.mult).then_inc(e1_ok.sem, 1)

                def add_positions(rnd):
                    it, half = rnd // 2, rnd % 2
                    n = ROWS[it]
                    if half == 0:
                        wait_alone(dve, pos_back[it], e, 16)
                        wait_alone(dve, ptj_ps, e.minus(1), 8)
                    wait_alone(dve, sj_ps, e, rnd + 1)
                    for i in range(3):
                        for par in range(2):
                            h = 6 * half + 2 * i + par
                            V.tensor_tensor_reduce(scj[0:n, it, h, :], bank[2 + par][0:n, i * S:(i + 1) * S],
                                                   pos_in[0:n, it, h, :], 1.0, FMIN, ALU.add, ALU.max,
                                                   mxj[0:n, it, h:h + 1]).then_inc(sj_sb.sem, 1)
                    if half == 1:
                        wait(dve, sj_sb, e, 12 * (it + 1))
                        V.tensor_scalar(nmj[0:n, it, :], mxj[0:n, it, :], -1.0, None, ALU.mult).then_inc(nm_ok.sem, 1)

                if e is not None:
                    add_positions(0)
                    add_positions(1)
                if d is not None:
                    def ready(it):
                        if it == 0:
                            wait(dve, e3_ok, d, 1)
                        else:
                            pair_wait(dve, ht_in[p], d, p)
                    norm_stats(hj[:, p], stq, mvq, stq_ok, mvq_ok, veq_ok, d, EPS, ready)
                if e is not None:
                    add_positions(2)
                    add_positions(3)
                if d is not None:
                    wait(dve, rsq_ok, d, 1)
                    wait(dve, xqT_ps, d.minus(1), 1)
                    wait(dve, xqb_ok, d.minus(1), 2)
                    for it in range(2):
                        n = ROWS[it]
                        V.tensor_scalar(xq[0:n, it, :], hj[0:n, p, it, :], mvq[0:n, it, 0:1], rsq[0:n, it:it + 1],
                                        ALU.subtract, ALU.mult).then_inc(xq_ok.sem, 1)
                if f is not None:
                    wait(dve, x4T_ps, f, 1)
                    V.tensor_copy(x4T[:, :, :], bank[7][0:HALF, 0:2 * S].rearrange("p (c t) -> p c t", c=2)).then_inc(x4T_sb.sem, 1)
                if d is not None:
                    for half in range(2):
                        wait(dve, qj_ps, d, half + 1)
                        src = bank[1 - half][:, 0:3 * S].rearrange("p (m t) -> p m t", m=3)
                        ms = slice(3 * half, 3 * half + 3)
                        V.scalar_tensor_tensor(qc[:, p, ms, :], src, DH ** -0.5, rw8[:, ms].unsqueeze(2).broadcast_to([128, 3, S]),
                                               ALU.mult, ALU.add).then_inc(qc_ok.sem, 1)
                        wait(dve, pos_ps, d.minus(1), 6)
                        V.scalar_tensor_tensor(qr[:, ms, :], src, DH ** -0.5, rr8[:, ms].unsqueeze(2).broadcast_to([128, 3, S]),
                                               ALU.mult, ALU.add).then_inc(qr_ok.sem, 1)
                if e is not None:
                    wait(dve, pvj_ps, e, 4)
                    for it in range(2):
                        n = ROWS[it]
                        pv = bank[6][0:n, it * NH * HA:(it + 1) * NH * HA].rearrange("p (h e) -> p h e", h=NH)
                        V.reciprocal(rdj[0:n, it, :], pv[:, :, HD]).then_inc(rdj_ok.sem, 1)
                    for it in range(2):
                        n = ROWS[it]
                        pv = bank[6][0:n, it * NH * HA:(it + 1) * NH * HA].rearrange("p (h e) -> p h e", h=NH)
                        wait(dve, rdj_ok, e, it + 1)
                        V.tensor_tensor(atj[0:n, it, :].rearrange("p (h e) -> p h e", h=NH), pv[:, :, 0:HD],
                                        rdj[0:n, it, :].unsqueeze(2).broadcast_to([n, NH, HD]), ALU.mult).then_inc(atj_ok.sem, 1)
                if d is not None:
                    for half in range(2):
                        wait(dve, kj_ps, d, half + 1)
                        src = bank[1 - half][:, 0:3 * S].rearrange("p (m t) -> p m t", m=3)
                        ms = slice(3 * half, 3 * half + 3)
                        V.tensor_tensor(kj[:, p, ms, :], src, wk[:, K_BK + 3 * half:K_BK + 3 * half + 3].unsqueeze(2).broadcast_to([128, 3, S]),
                                        ALU.add).then_inc(kj_ok.sem, 1)
                    wait(dve, vj_ps, d, 1)
                    for it in range(2):
                        n = ROWS[it]
                        V.tensor_tensor(vj[0:n, p, it, :, 0:HD], bank[1][0:n, it * D:(it + 1) * D].rearrange("p (h e) -> p h e", h=NH),
                                        rj[0:n, 3, :].rearrange("p (h e) -> p h e", h=NH), ALU.add).then_inc(vj_ok.sem, 1)
                if e is not None:
                    wait(dve, wo_ps, e, 1)
                    wait(dve, x3_ok, e.minus(1), 2)
                    wait(dve, xqb_ok, e, 2)
                    for it in range(2):
                        n = ROWS[it]
                        V.tensor_tensor(r3[0:n, it, :], bank[6][0:n, it * D:(it + 1) * D], xqb[0:n, 1 - p, it, :], ALU.add).then_inc(r3_ok.sem, 1)
                    norm_stats(r3, st3, mv3, st3_ok, mv3_ok, ve3_ok, e, ATT_EPS, lambda it: wait(dve, r3_ok, e, it + 1))
                if d is not None:
                    for rnd in range(6):
                        it, q4 = rnd // 3, rnd % 3
                        n = ROWS[it]
                        wait(dve, pos_ps, d, rnd + 1)
                        wait(dve, pos_written[it], d.minus(1), 16)
                        V.tensor_copy(pos_out[0:n, it, 4 * q4:4 * q4 + 4:2, :],
                                      bank[0][0:n, 0:2 * WIN].rearrange("p (h w) -> p h w", h=2)).then_inc(pos_sb.sem, 1)
                if e is not None:
                    wait(dve, rs3_ok, e, 1)
                    wait(dve, t3_ok, e.minus(1), 2)
                    for it in range(2):
                        n = ROWS[it]
                        V.tensor_scalar(x3[0:n, it, :], r3[0:n, it, :], mv3[0:n, it, 0:1], rs3[0:n, it:it + 1],
                                        ALU.subtract, ALU.mult).then_inc(x3_ok.sem, 1)
                if f is not None:
                    wait(dve, mj_ps, f, 1)
                    pair_wait(dve, y_stored[p], f.minus(2), p)
                    for it in range(2):
                        n = ROWS[it]
                        V.tensor_tensor(yj[0:n, p, it, :], bank[7][0:n, it * D:(it + 1) * D], h2[0:n, p, it, :], ALU.add).then_inc(yj_ok.sem, 1)
                if e is not None:
                    norm_stats(h2[:, 1 - p], st4, mv4, st4_ok, mv4_ok, ve4_ok, e, EPS, lambda it: wait(dve, h2_ok, e, it + 1))
                    wait(dve, rs4_ok, e, 1)
                    wait(dve, x4T_ps, e.minus(1), 1)
                    for it in range(2):
                        n = ROWS[it]
                        V.tensor_scalar(x4[0:n, it, :], h2[0:n, 1 - p, it, :], mv4[0:n, it, 0:1], rs4[0:n, it:it + 1],
                                        ALU.subtract, ALU.mult).then_inc(x4_ok.sem, 1)

            joint_steps(dve, jstep)


def kernel(**inputs):
    import numpy as np
    import concourse.bacc as bacc
    from concourse.bass_utils import run_bass_kernel_spmd

    x = {k: np.asarray(v) for k, v in inputs.items()}

    def chunks(w):
        return np.concatenate([w[0:HALF], w[HALF:D]], axis=1)

    def columns(vec, rows):
        return vec.reshape(-1, rows).T

    img = x["x"][:, :, :90, :90].reshape(B, 3, 9, 10, 9, 10)
    patches = np.zeros((PK, B, 3, IMG), np.float32)
    patches[:, :, :, 1:] = img.transpose(3, 5, 0, 1, 2, 4).reshape(PK, B, 3, 81)

    wa, ra, wb, rb, wc, wc2, rc = [], [], [], [], [], [], []
    for l in range(LAYERS):
        w, bias = x["L0_txt_c_attn_w"][l], x["L0_txt_c_attn_b"][l]
        q_cols = columns(bias[0:D], HALF)
        even = np.zeros((HALF, 2), np.float32)
        odd = np.zeros((HALF, 2), np.float32)
        is_even = (np.arange(HALF) // HD) % 2 == 0
        even[is_even] = q_cols[is_even]
        odd[~is_even] = q_cols[~is_even]
        wa.append(np.concatenate([chunks(w[:, 0:2 * D]), chunks(w[:, 2 * D:]), even, odd, columns(bias[D:2 * D], HALF)], axis=1))
        ra.append(np.concatenate([bias[2 * D:], x["L0_txt_c_proj_b"][l]]))
        wb.append(chunks(x["L0_txt_c_proj_w"][l]))
        rb.append(np.concatenate([x["L0_txt_ln1_w"][l], x["L0_txt_ln1_b"][l], x["L0_txt_mlp_proj_b"][l]]))
        wc.append(np.concatenate([chunks(x["L0_txt_c_fc_w"][l]), columns(x["L0_txt_ln1_w"][l], HALF),
                                  columns(x["L0_txt_ln1_b"][l], HALF)], axis=1))
        wc2.append(np.concatenate([x["L0_txt_mlp_proj_w"][l].reshape(MH, 128, D).transpose(1, 0, 2).reshape(128, MH * D),
                                   columns(x["L0_txt_c_fc_b"][l], 128)], axis=1))
        rc.append(np.concatenate([x["L0_txt_ln2_w"][l], x["L0_txt_ln2_b"][l]]))

    def block_diagonal(w):
        n = w.shape[2]
        out = np.zeros((HALF, 2, 2, n), np.float32)
        for g in range(4):
            out[48 * (g % 2):48 * (g % 2) + 48, g // 2, g % 2] = w[g]
        return out.reshape(HALF, 4 * n)

    w_joint = np.concatenate([
        block_diagonal(x["L0_attn_Wq"]), block_diagonal(x["L0_attn_Wk"]), block_diagonal(x["L0_attn_Wv"]),
        chunks(x["L0_attn_Wo"]), chunks(x["L0_ffn_in_weight"].T),
        chunks(x["L0_attn_position_embeds"][1:NT + 1].T), chunks(x["L0_attn_r_kernel"].reshape(D, 768))], axis=1)
    w_joint128 = np.concatenate([
        x["L0_ffn_out_weight"].reshape(MH, 128, D).transpose(1, 0, 2).reshape(128, MH * D),
        columns(x["L0_ffn_in_bias"], 128), columns(x["L0_attn_r_w_bias"].reshape(-1), 128),
        columns(x["L0_attn_r_r_bias"].reshape(-1), 128), columns(x["L0_attn_bk"], 128)], axis=1)
    r_joint = np.concatenate([x["L0_tok_cls"].reshape(-1), x["L0_tok_b"], x["L0_tok_gamma"], x["L0_tok_beta"],
                              x["L0_attn_bv"], x["L0_attn_bo"], x["L0_attn_gamma"], x["L0_attn_beta"]])[None]

    consts = np.zeros((128, CST_W), np.float32)
    consts[:, CST_I:CST_I + 128] = np.eye(128)
    consts[0:TXT, CST_CAUSAL:CST_CAUSAL + TXT] = np.tril(np.ones((TXT, TXT)))
    consts[0:TXT, CST_NEG:CST_NEG + TXT] = NEG * (1 - np.tril(np.ones((TXT, TXT))))
    consts[:, CST_EVEN] = (np.arange(128) // HD) % 2 == 0
    consts[:, CST_ODD] = (np.arange(128) // HD) % 2 == 1
    consts[:, CST_PW:CST_PW + 2] = -0.5

    host = {
        "patches": patches.reshape(PK, B, 3 * IMG), "ids": x["x_txt"].T, "pos_ids": x["pos_S"][:, None],
        "mask": x["mask_BS_f1_0"].reshape(1, B * TXT), "tok_emb": x["L0_txt_tok_emb"], "pos_emb": x["L0_txt_pos_emb"],
        "w_a": np.stack(wa), "r_a": np.stack(ra), "w_b": np.stack(wb), "r_b": np.stack(rb),
        "w_c": np.stack(wc), "w_c2": np.stack(wc2), "r_c": np.stack(rc),
        "w_tok": x["L0_tok_W"].T.reshape(3, PK, D).transpose(1, 0, 2), "r_joint": r_joint,
        "w_joint": w_joint, "w_joint128": w_joint128, "consts": consts,
    }
    nc = bacc.Bacc("TRN2", target_bir_lowering=False, num_devices=1)
    arrays, args = {}, []
    for name, array in host.items():
        array = np.ascontiguousarray(array)
        arrays[f"in_{name}"] = array
        args.append(nc.dram_tensor(f"in_{name}", array.shape, mybir.dt.from_np(array.dtype), kind="ExternalInput").ap())
    args.append(nc.dram_tensor("out_0", (B, S, D), F32, kind="ExternalOutput").ap())
    args.append(nc.dram_tensor("h_text", (B, TXT, D), F32, kind="Internal").ap())
    args.append(nc.dram_tensor("pos_scratch", (2, IMG, NH * WIN), F32, kind="Internal").ap())
    early_fusion(nc, *args)
    result = run_bass_kernel_spmd(nc, [arrays], core_ids=[0])
    return result.results[0]["out_0"]
```

```python
import concourse.bass as bass
from concourse import mybir
from contextlib import ExitStack

F32 = mybir.dt.float32
I32 = mybir.dt.int32
U32 = mybir.dt.uint32
ALU = mybir.AluOpType
ACT = mybir.ActivationFunctionType
AX = mybir.AxisListType

B = 32
TXT = 77
IMG = 82
S = IMG + TXT
D = 192
HALF = D // 2
NH = 12
LAYERS = 5
G = 4
GROUPS = B // G
STEPS = LAYERS * GROUPS
GT = G * TXT
HD = D // NH
HA = HD + 1
DH = 64
HID = 768
MH = HID // 128
NT = 2 * S - 1
WIN = S + IMG - 1
ROWS = (IMG, TXT)
OFF = (0, IMG)
PK = 100
EPS = 1e-5
ATT_EPS = 1e-9
NEG = -10000.0
FMIN = -3.4028234663852886e38

A_QK, A_V, A_COL = 0, 2 * 2 * D, 2 * 2 * D + 2 * D
A_W = A_COL + 6
C_FC, C_COL = 0, 2 * HID
C_W = C_COL + 4
C2_COL = MH * D
C2_W = C2_COL + MH
J_Q, J_K, J_V, J_O, J_IN = 0, 768, 1536, 1728, 2112
J_POS = J_IN + 2 * HID
J_R = J_POS + 2 * NT
J_W = J_R + 2 * 768
K_OUT, K_INB, K_RW, K_RR, K_BK = 0, MH * D, MH * D + 6, MH * D + 12, MH * D + 18
K_W = MH * D + 24
CST_I, CST_CAUSAL, CST_NEG, CST_EVEN, CST_ODD, CST_PW = 0, 128, 128 + TXT, 128 + 2 * TXT, 129 + 2 * TXT, 130 + 2 * TXT
CST_W = CST_PW + 2


class Signal:

    def __init__(self, sem, per):
        self.sem, self.per = sem, per


class Item:

    def __init__(self, engine, base, lag=0, products=None):
        self.engine, self.base, self.lag = engine, base, lag
        self.products = {} if products is None else products

    def minus(self, n):
        return Item(self.engine, self.base, self.lag - n, self.products)

    def at(self, per, n):
        if isinstance(self.base, int):
            return (self.base + self.lag) * per + n
        if per not in self.products:
            self.products[per] = self.engine.snap(self.base * per)
        return self.products[per] + (self.lag * per + n)

    def value(self):
        return self.base + self.lag


def wait(engine, signal, item, n):
    value = item.at(signal.per, n)
    if isinstance(value, int) and value <= 0:
        return
    engine.wait_ge(signal.sem, value)


def early_fusion(nc, patches, ids, pos_ids, mask, tok_emb, pos_emb, w_a, r_a, w_b, r_b, w_c, w_c2, r_c,
                 w_tok, r_joint, w_joint, w_joint128, consts, out, h_text, pos_scratch):
    ctx = ExitStack()
    with ctx:
        def sb(name, shape, dt=F32):
            return ctx.enter_context(nc.sbuf_tensor(name, shape, dt))

        def sig(name, per=1):
            return Signal(ctx.enter_context(nc.semaphore(name)), per)

        bank = [ctx.enter_context(nc.psum_tensor(f"bank{i}", [128, 512], F32)) for i in range(8)]

        cst = sb("cst", [128, CST_W])
        ident = cst[:, CST_I:CST_I + 128]
        power = cst[:, CST_PW:CST_PW + 2]
        wtok = sb("wtok", [PK, 3, D])
        wj = sb("wj", [HALF, J_W])
        wk = sb("wk", [128, K_W])
        rj = sb("rj", [IMG, 7, D])
        rel = sb("rel", [128, 6, NT])
        rw8 = sb("rw8", [128, 6])
        rr8 = sb("rr8", [128, 6])

        text_ctx = ExitStack()

        def tb(name, shape, dt=F32):
            return text_ctx.enter_context(nc.sbuf_tensor(name, shape, dt))

        id_sb = tb("id_sb", [TXT, B], I32)
        pid_sb = tb("pid_sb", [TXT, 1], I32)
        emb = tb("emb", [TXT, B, D])
        pos_row = tb("pos_row", [TXT, D])
        ext = tb("ext", [TXT, B, TXT])
        wa = tb("wa", [HALF, A_W])
        wb = tb("wb", [HALF, 2 * D])
        wc = tb("wc", [HALF, C_W])
        wc2 = tb("wc2", [128, C2_W])
        ra = tb("ra", [TXT, 2, D])
        rb = tb("rb", [TXT, 3, D])
        rc = tb("rc", [TXT, 2, D])
        h_tok = tb("h_tok", [TXT, G, D])
        h_res = tb("h_res", [TXT, G, D])
        hT = tb("hT", [HALF, 2, GT])
        q_even = tb("q_even", [HALF, 2, GT])
        q_odd = tb("q_odd", [HALF, 2, GT])
        kT = tb("kT", [HALF, 2, GT])
        v_tok = tb("v_tok", [TXT, G, NH, HA])
        sc = tb("sc", [TXT, G, NH, TXT])
        mx = tb("mx", [TXT, G, NH])
        pT = tb("pT", [TXT, 2, 6 * TXT])
        rden = tb("rden", [TXT, NH])
        att = tb("att", [TXT, D])
        aT = tb("aT", [HALF, 2 * TXT])
        h_bias = tb("h_bias", [TXT, G, D])
        r1 = tb("r1", [TXT, D])
        st1 = tb("st1", [TXT, 6])
        mv1 = tb("mv1", [TXT, 2])
        rs1 = tb("rs1", [TXT, 1])
        x1 = tb("x1", [TXT, G, D])
        nb_tmp = tb("nb_tmp", [TXT, D])
        bias2 = tb("bias2", [TXT, D])
        n_bias = tb("n_bias", [TXT, G, D])
        nT = tb("nT", [HALF, 2, GT])
        gel = tb("gel", [128, MH, GT])
        r2 = tb("r2", [TXT, D])
        st2 = tb("st2", [TXT, 6])
        mv2 = tb("mv2", [TXT, 2])
        rs2 = tb("rs2", [TXT, 1])
        x2 = tb("x2", [TXT, D])
        ho_tmp = tb("ho_tmp", [TXT, D])
        h_out = tb("h_out", [TXT, G, D])

        consts_in = sig("consts_in")
        carried = {nc.sync.engine: sig("carried_sp"), nc.vector.engine: sig("carried_dve")}
        ids_in = sig("ids_in")
        mask_in = sig("mask_in")
        pos_row_in = sig("pos_row_in")
        emb_in = [sig(f"emb_in{g}") for g in range(GROUPS)]
        emb_done = sig("emb_done")
        emb_stored = [sig("emb_stored_first"), sig("emb_stored_rest")]
        ones_set = sig("ones_set")
        ext_one = sig("ext_one")
        ext_scaled = sig("ext_scaled")
        ext_ready = sig("ext_ready")
        wa_in, wb_in, wc_in = sig("wa_in", 32), sig("wb_in", 32), sig("wc_in", 48)
        h_in = sig("h_in", 16)
        res_in = [sig(f"res_in{b}", 16) for b in range(G)]
        h_stored = [sig(f"h_stored{b}", 16) for b in range(G)]
        hT_ps, hT_sb = sig("hT_ps", 2), sig("hT_sb", 2)
        qk_ps, q_sb, k_sb = sig("qk_ps", 4), sig("q_sb", 4), sig("k_sb", 2)
        v_ps, v_sb = sig("v_ps", G), sig("v_sb", G)
        s_ps, masked, biased, maxed, shifted, expd = (sig("s_ps", G), sig("masked", 3 * G), sig("biased", G),
                                                      sig("maxed", G), sig("shifted", G), sig("expd", G))
        pT_ps, pT_sb, pv_ps = sig("pT_ps", 2 * G), sig("pT_sb", 2 * G), sig("pv_ps", G)
        rden_ok, att_ok, aT_ps, aT_sb, pj_ps = (sig("rden_ok", G), sig("att_ok", G), sig("aT_ps", G),
                                                sig("aT_sb", G), sig("pj_ps", G))
        hb_ok, r1_ok, st1_ok, mv1_ok, ve1_ok, rs1_ok, x1_ok = (sig("hb_ok", G), sig("r1_ok", G), sig("st1_ok", G),
                                                               sig("mv1_ok", G), sig("ve1_ok", G), sig("rs1_ok", G),
                                                               sig("x1_ok", G))
        bias2_ok, nbt_ok, nb_mid, nb_ok = sig("bias2_ok", 1), sig("nbt_ok", G), sig("nb_mid", G), sig("nb_ok", G)
        nT_ps, nT_sb, fc_ps, gelu_ok, ml_ps = (sig("nT_ps", 2), sig("nT_sb", 4), sig("fc_ps", MH),
                                               sig("gelu_ok", MH), sig("ml_ps", G))
        r2_ok, st2_ok, mv2_ok, ve2_ok, rs2_ok, x2_ok = (sig("r2_ok", G), sig("st2_ok", G), sig("mv2_ok", G),
                                                        sig("ve2_ok", G), sig("rs2_ok", G), sig("x2_ok", G))
        hot_ok, ho_ok = sig("hot_ok", G), sig("ho_ok", G)

        def wait_alone(engine, signal, item, n):
            wait(engine, signal, item, n)
            if not isinstance(item.base, int):
                engine.sem_inc(carried[engine.engine].sem)

        def text_steps(engine, step):
            fixed = lambda t: Item(engine, t)
            step(fixed(0), None, None)
            step(fixed(1), fixed(0), None)
            step(fixed(2), fixed(1), fixed(0))
            with engine.Fori(3, STEPS) as t:
                a = Item(engine, t)
                step(a, a.minus(1), a.minus(2))
            step(None, fixed(STEPS - 1), fixed(STEPS - 2))
            step(None, None, fixed(STEPS - 1))

        def layer_in(engine, signal, item):
            if isinstance(item.base, int):
                engine.wait_ge(signal.sem, (item.value() // GROUPS + 1) * signal.per)
            else:
                engine.wait_ge(signal.sem, (item.value() >> 3) * signal.per + signal.per)

        def text_over(engine):
            for b in range(G):
                wait(engine, h_stored[b], Item(engine, STEPS - 1), 16)

        text_ctx.close()
        pat = sb("pat", [PK, 2, 3 * IMG])
        e0 = sb("e0", [IMG, D])
        ste = sb("ste", [IMG, 6])
        mve = sb("mve", [IMG, 2])
        rse = sb("rse", [IMG, 1])
        e1 = sb("e1", [IMG, D])
        e2 = sb("e2", [IMG, D])
        hj = sb("hj", [IMG, 2, D])
        hc = sb("hc", [IMG, 2, 2, D])
        stq = sb("stq", [IMG, 2, 6])
        mvq = sb("mvq", [IMG, 2, 2])
        rsq = sb("rsq", [IMG, 2])
        xq = sb("xq", [IMG, 2, D])
        xqb = sb("xqb", [IMG, 2, 2, D])
        xqT = sb("xqT", [HALF, 2, S])
        qc = sb("qc", [128, 2, 6, S])
        qr = sb("qr", [128, 6, S])
        kj = sb("kj", [128, 2, 6, S])
        vj = sb("vj", [IMG, 2, 2, NH, HA])
        pos_out = sb("pos_out", [IMG, 2, NH, WIN])
        pos_in = sb("pos_in", [IMG, 2, NH, S])
        scj = sb("scj", [IMG, 2, NH, S])
        mxj = sb("mxj", [IMG, 2, NH])
        nmj = sb("nmj", [IMG, 2, NH])
        pTj = sb("pTj", [IMG, 2, 2, 3 * S])
        rdj = sb("rdj", [IMG, 2, NH])
        atj = sb("atj", [IMG, 2, D])
        aTj = sb("aTj", [HALF, 2 * S])
        r3 = sb("r3", [IMG, 2, D])
        st3 = sb("st3", [IMG, 2, 6])
        mv3 = sb("mv3", [IMG, 2, 2])
        rs3 = sb("rs3", [IMG, 2])
        x3 = sb("x3", [IMG, 2, D])
        t3 = sb("t3", [IMG, 2, D])
        t4 = sb("t4", [IMG, 2, D])
        h2 = sb("h2", [IMG, 2, 2, D])
        st4 = sb("st4", [IMG, 2, 6])
        mv4 = sb("mv4", [IMG, 2, 2])
        rs4 = sb("rs4", [IMG, 2])
        x4 = sb("x4", [IMG, 2, D])
        x4T = sb("x4T", [HALF, 2, S])
        gj = sb("gj", [128, MH, S])
        yj = sb("yj", [IMG, 2, 2, D])

        jw_in, rel_ps, rel_ok, r8_ok, pads = sig("jw_in"), sig("rel_ps"), sig("rel_ok"), sig("r8_ok"), sig("pads")
        pat_in = [sig(f"pat_in{p}", 16) for p in range(2)]
        ht_in, hc_ok = sig("ht_in", 16), sig("hc_ok", 2)
        e_ps, e0_ok, ste_ok, mve_ok, vee_ok, rse_ok, e1_ok, e2_ok, e3_ok = (
            sig("e_ps"), sig("e0_ok"), sig("ste_ok"), sig("mve_ok"), sig("vee_ok"), sig("rse_ok"),
            sig("e1_ok"), sig("e2_ok"), sig("e3_ok"))
        stq_ok, mvq_ok, veq_ok, rsq_ok, xq_ok, xqb_ok = (sig("stq_ok", 2), sig("mvq_ok", 2), sig("veq_ok"),
                                                         sig("rsq_ok"), sig("xq_ok", 2), sig("xqb_ok", 2))
        xqT_ps, xqT_sb = sig("xqT_ps"), sig("xqT_sb")
        qj_ps, qc_ok, qr_ok, kj_ps, kj_ok = sig("qj_ps", 2), sig("qc_ok", 2), sig("qr_ok", 2), sig("kj_ps", 2), sig("kj_ok", 2)
        vj_ps, vj_ok = sig("vj_ps"), sig("vj_ok", 2)
        pos_ps, pos_even, pos_odd = sig("pos_ps", 12), sig("pos_even", 6), sig("pos_odd", 6)
        pos_written, pos_back = [sig(f"pos_written{i}", 16) for i in range(2)], [sig(f"pos_back{i}", 16) for i in range(2)]
        sj_ps, sj_sb, nm_ok, ej_ok = sig("sj_ps", 8), sig("sj_sb", 24), sig("nm_ok", 2), sig("ej_ok", 24)
        ptj_ps, ptj_sb, pvj_ps = sig("ptj_ps", 8), sig("ptj_sb", 8), sig("pvj_ps", 4)
        rdj_ok, atj_ok, atT_ps, atT_sb, wo_ps = sig("rdj_ok", 2), sig("atj_ok", 2), sig("atT_ps"), sig("atT_sb"), sig("wo_ps")
        r3_ok, st3_ok, mv3_ok, ve3_ok, rs3_ok, x3_ok = (sig("r3_ok", 2), sig("st3_ok", 2), sig("mv3_ok", 2),
                                                        sig("ve3_ok"), sig("rs3_ok"), sig("x3_ok", 2))
        t3_ok, t4_ok, h2_ok = sig("t3_ok", 2), sig("t4_ok", 2), sig("h2_ok", 2)
        st4_ok, mv4_ok, ve4_ok, rs4_ok, x4_ok = sig("st4_ok", 2), sig("mv4_ok", 2), sig("ve4_ok"), sig("rs4_ok"), sig("x4_ok", 2)
        x4T_ps, x4T_sb, fj_ps, gj_ok, mj_ps, yj_ok = (sig("x4T_ps"), sig("x4T_sb"), sig("fj_ps", 2), sig("gj_ok", 6),
                                                      sig("mj_ps"), sig("yj_ok", 2))
        y_stored = [sig(f"y_stored{i}", 32) for i in range(2)]

        def joint_steps(engine, step):
            def fixed_step(u):
                stage = lambda v: Item(engine, v) if 0 <= v < B else None
                step(stage(u + 1), stage(u), stage(u - 1), stage(u - 2), u % 2)

            for u in range(-1, 4):
                fixed_step(u)
            with engine.Fori(2, B // 2 - 1) as pair:
                even = Item(engine, engine.snap(pair * 2))
                for p in range(2):
                    d = even.minus(-p)
                    step(d.minus(-1), d, d.minus(1), d.minus(2), p)
            for u in range(B - 2, B + 2):
                fixed_step(u)

        def pair_wait(engine, signal, item, parity):
            if isinstance(item.base, int):
                u = item.value()
                if u >= 0:
                    engine.wait_ge(signal.sem, (u // 2 + 1) * signal.per)
            else:
                half = signal.per // 2
                engine.wait_ge(signal.sem, item.at(half, signal.per - parity * half))

        block = ctx.enter_context(nc.Block())

        @block.sync
        def _(sp):
            sp.dma_start(cst[:, :], consts).then_inc(consts_in.sem, 16)
            sp.dma_start(id_sb[:, :], ids).then_inc(ids_in.sem, 16)
            sp.dma_start(pid_sb[:, :], pos_ids).then_inc(ids_in.sem, 16)
            sp.dma_start(ext[:, :, :].rearrange("p b k -> p (b k)"), mask[0:1, :].broadcast_to([TXT, B * TXT])
                         ).then_inc(mask_in.sem, 16)

            def load_a(l):
                sp.dma_start(wa[:, :], w_a[bass.ds(l, 1), :, :].rearrange("l p n -> (l p) n")).then_inc(wa_in.sem, 16)
                sp.dma_start(ra[:, :, :].rearrange("p r d -> p (r d)"),
                             r_a[bass.ds(l, 1), :].broadcast_to([TXT, 2 * D])).then_inc(wa_in.sem, 16)

            def load_b(l):
                sp.dma_start(wb[:, :], w_b[bass.ds(l, 1), :, :].rearrange("l p n -> (l p) n")).then_inc(wb_in.sem, 16)
                sp.dma_start(rb[:, :, :].rearrange("p r d -> p (r d)"),
                             r_b[bass.ds(l, 1), :].broadcast_to([TXT, 3 * D])).then_inc(wb_in.sem, 16)

            def load_c(l):
                sp.dma_start(wc[:, :], w_c[bass.ds(l, 1), :, :].rearrange("l p n -> (l p) n")).then_inc(wc_in.sem, 16)
                sp.dma_start(wc2[:, :], w_c2[bass.ds(l, 1), :, :].rearrange("l p n -> (l p) n")).then_inc(wc_in.sem, 16)
                sp.dma_start(rc[:, :, :].rearrange("p r d -> p (r d)"),
                             r_c[bass.ds(l, 1), :].broadcast_to([TXT, 2 * D])).then_inc(wc_in.sem, 16)

            load_a(0)
            load_b(0)
            load_c(0)
            for g in range(GROUPS):
                sp.wait_ge(emb_done.sem, g + 1)
                for b in range(G):
                    sp.dma_start(h_text[g * G + b, :, :], emb[:, g * G + b, :]).then_inc(emb_stored[min(g, 1)].sem, 16)
            sp.dma_start(wtok[:, :, :], w_tok).then_inc(jw_in.sem, 16)
            sp.dma_start(wj[:, :], w_joint).then_inc(jw_in.sem, 16)
            sp.dma_start(wk[:, :], w_joint128).then_inc(jw_in.sem, 16)
            sp.dma_start(rj[0:1, 0, :], r_joint[0:1, 0:D]).then_inc(jw_in.sem, 16)
            sp.dma_start(rj[1:IMG, 0, :], r_joint[0:1, D:2 * D].broadcast_to([IMG - 1, D])).then_inc(jw_in.sem, 16)
            sp.dma_start(rj[:, 1:7, :].rearrange("p r d -> p (r d)"),
                         r_joint[0:1, 2 * D:8 * D].broadcast_to([IMG, 6 * D])).then_inc(jw_in.sem, 16)

            def load_h(a, g):
                wait_alone(sp, hT_ps, a.minus(1), 2)
                for b in range(G):
                    if isinstance(a.base, int) and a.value() < GROUPS:
                        first = a.value() == 0
                        sp.wait_ge(emb_stored[0 if first else 1].sem, 16 * G * (1 if first else GROUPS - 1))
                        break
                    wait_alone(sp, h_stored[b], a.minus(GROUPS), 16)
                sp.dma_start(h_tok[:, :, :], h_text[g * G:(g + 1) * G, :, :].rearrange("b t d -> t b d")
                             ).then_inc(h_in.sem, 16)

            def load_res(a, g, b):
                wait_alone(sp, hb_ok, a.minus(1), b + 1)
                sp.dma_start(h_res[:, b, :], h_text[g * G + b, :, :]).then_inc(res_in[b].sem, 16)

            def step(c, c_group, a_next, a_group, reload=None):
                if a_next is not None:
                    load_h(a_next, a_group)
                for b in range(G):
                    if c is not None:
                        wait_alone(sp, ho_ok, c, b + 1)
                        sp.dma_start(h_text[c_group * G + b, :, :], h_out[:, b, :]).then_inc(h_stored[b].sem, 16)
                    if a_next is not None and b > 0:
                        load_res(a_next, a_group, b - 1)
                if a_next is not None:
                    load_res(a_next, a_group, G - 1)

            def reload_a(a, l):
                wait_alone(sp, v_sb, a, G)
                wait_alone(sp, q_sb, a, 4)
                wait_alone(sp, k_sb, a, 2)
                wait_alone(sp, hb_ok, a, G)
                load_a(l)

            def reload_b(b_, l):
                wait_alone(sp, r1_ok, b_, G)
                wait_alone(sp, nb_ok, b_, G)
                load_b(l)

            def reload_c(c, l):
                wait_alone(sp, ho_ok, c, G)
                load_c(l)

            load_h(Item(sp, 0), 0)
            for b in range(G):
                load_res(Item(sp, 0), 0, b)

            def fixed_step(t):
                c = Item(sp, t - 2) if t >= 2 else None
                a_next = Item(sp, t + 1) if t + 1 < STEPS else None
                step(c, (t - 2) % GROUPS, a_next, (t + 1) % GROUPS)

            def reloads(t, g, layer):
                if g == GROUPS - 1:
                    reload_a(t, layer + 1)
                if g == 0:
                    reload_b(t.minus(1), layer)
                if g == 1:
                    reload_c(t.minus(2), layer)

            for t in range(GROUPS):
                fixed_step(t)
                if t == GROUPS - 1:
                    reloads(Item(sp, t), t, 0)
            with sp.Fori(1, LAYERS - 1) as layer:
                t0 = Item(sp, sp.snap(layer * GROUPS))
                for g in range(GROUPS):
                    t = t0.minus(-g)
                    step(t.minus(2), (g - 2) % GROUPS, t.minus(-1), (g + 1) % GROUPS)
                    reloads(t, g, layer)
            for t in range(STEPS - GROUPS, STEPS + 2):
                fixed_step(t)
                if t - (STEPS - GROUPS) < 2:
                    reloads(Item(sp, t), t % GROUPS, LAYERS - 1)

            text_over(sp)

            def load_patches(u, p):
                wait_alone(sp, e_ps, u.minus(2), 1)
                sp.dma_start(pat[:, p, :], patches[:, bass.ds(u.value(), 1), :].rearrange("k b n -> k (b n)")
                             ).then_inc(pat_in[p].sem, 16)

            load_patches(Item(sp, 0), 0)

            def jstep(n, d, e, f, p):
                if n is not None:
                    wait_alone(sp, hc_ok, n.minus(1), 2)
                    wait_alone(sp, xq_ok, n.minus(1), 2)
                    sp.dma_start(hj[0:TXT, 1, :], h_text[bass.ds(n.value(), 1), :, :].rearrange("b t d -> (b t) d")
                                 ).then_inc(ht_in.sem, 16)
                if n is not None and not (isinstance(n.base, int) and n.value() == B - 1):
                    load_patches(n.minus(-1), p)
                if d is not None:
                    for it in range(2):
                        m = ROWS[it]
                        wait_alone(sp, pos_even, d, 3 * (it + 1))
                        wait_alone(sp, pos_odd, d, 3 * (it + 1))
                        wait_alone(sp, pos_back[it], d.minus(1), 16)
                        sp.dma_start(pos_scratch[it, 0:m, :], pos_out[0:m, it, :, :].rearrange("p h w -> p (h w)")
                                     ).then_inc(pos_written[it].sem, 16)
                    for it in range(2):
                        m = ROWS[it]
                        wait_alone(sp, pos_written[it], d, 16)
                        wait_alone(sp, sj_sb, d.minus(1), 12 * (it + 1))
                        skew = bass.AP(pos_scratch.tensor, pos_scratch.offset + it * IMG * NH * WIN + m - 1,
                                       [[NH * WIN - 1, m], [WIN, NH], [1, S]])
                        sp.dma_start(pos_in[0:m, it, :, :], skew).then_inc(pos_back[it].sem, 16)
                if f is not None:
                    for it in range(2):
                        wait_alone(sp, yj_ok, f, it + 1)
                        sp.dma_start(out[bass.ds(f.value(), 1), OFF[it]:OFF[it] + ROWS[it], :].rearrange("b t d -> (b t) d"),
                                     yj[0:ROWS[it], p, it, :]).then_inc(y_stored[p].sem, 16)

            joint_steps(sp, jstep)
            for p in range(2):
                sp.wait_ge(y_stored[p].sem, B // 2 * 32)
            for it in range(2):
                sp.wait_ge(pos_back[it].sem, B * 16)

        @block.gpsimd
        def _(pool):
            pool.wait_ge(ids_in.sem, 32)
            pool.indirect_dma_start(pos_row[:, :], None, pos_emb,
                                    bass.IndirectOffsetOnAxis(pid_sb[:, 0:1].bitcast(U32), 0)).then_inc(pos_row_in.sem, 16)
            for i in range(B):
                pool.indirect_dma_start(emb[:, i, :], None, tok_emb,
                                        bass.IndirectOffsetOnAxis(id_sb[:, i:i + 1].bitcast(U32), 0)
                                        ).then_inc(emb_in[i // G].sem, 16)
            pool.memset(v_tok[:, :, :, HD:HA], 1.0).then_inc(ones_set.sem, 1)
            pool.wait_ge(consts_in.sem, 16)

            def rstd(out_, var, n, ready, item, count, done):
                wait(pool, ready, item, count)
                nc.gpsimd.tensor_tensor(out_, var, power[0:out_.shape[0], 0:n], ALU.pow).then_inc(done.sem, 1)

            def step(a, b_, c):
                if a is not None:
                    layer_in(pool, wa_in, a)
                if b_ is not None:
                    layer_in(pool, wb_in, b_)
                    wait(pool, nb_ok, b_.minus(1), G)
                    nc.gpsimd.tensor_tensor(bias2[:, :], rb[:, 1, :], rb[:, 2, :], ALU.add).then_inc(bias2_ok.sem, 1)
                if c is not None:
                    layer_in(pool, wc_in, c)

                def first_norm(b):
                    if b_ is not None:
                        wait(pool, x1_ok, b_, b)
                        rstd(rs1[:, :], mv1[:, 1:2], 1, ve1_ok, b_, b + 1, rs1_ok)
                    if a is not None:
                        wait(pool, res_in[b], a, 16)
                        if b_ is not None:
                            wait(pool, r1_ok, b_, b + 1)
                        nc.gpsimd.tensor_tensor(h_bias[:, b, :], h_res[:, b, :], ra[:, 1, :], ALU.add).then_inc(hb_ok.sem, 1)
                    if b_ is not None:
                        if b == 0:
                            wait(pool, bias2_ok, b_, 1)
                        wait(pool, x1_ok, b_, b + 1)
                        wait(pool, nb_ok, b_, b)
                        nc.gpsimd.tensor_tensor(nb_tmp[:, :], x1[:, b, :], rb[:, 0, :], ALU.mult).then_inc(nbt_ok.sem, 1)
                        wait(pool, nbt_ok, b_, b + 1)
                        if c is not None:
                            wait(pool, r2_ok, c, b + 1)
                        nc.gpsimd.tensor_tensor(n_bias[:, b, :], nb_tmp[:, :], bias2[:, :], ALU.add).then_inc(nb_ok.sem, 1)

                for b in range(G):
                    if a is not None:
                        wait(pool, masked, a, 3 * (b + 1))
                        if isinstance(a.base, int):
                            e = ext[:, (a.value() % GROUPS) * G + b, :].unsqueeze(1)
                        else:
                            e = ext[:, bass.ds((a.value() % GROUPS) * G + b, 1), :]
                        if isinstance(a.base, int) and a.value() == 0:
                            pool.wait_ge(ext_ready.sem, B // G)
                        nc.gpsimd.tensor_tensor(sc[:, b, :, :], sc[:, b, :, :], e.broadcast_to([TXT, NH, TXT]),
                                                ALU.add).then_inc(biased.sem, 1)
                    if b == G - 1:
                        first_norm(b - 1)
                    if c is not None:
                        wait(pool, x2_ok, c, b)
                        rstd(rs2[:, :], mv2[:, 1:2], 1, ve2_ok, c, b + 1, rs2_ok)
                    if 0 < b < G - 1:
                        first_norm(b - 1)
                    if c is not None:
                        wait(pool, x2_ok, c, b + 1)
                        wait(pool, ho_ok, c, b)
                        nc.gpsimd.tensor_tensor(ho_tmp[:, :], x2[:, :], rc[:, 0, :], ALU.mult).then_inc(hot_ok.sem, 1)
                        wait(pool, hot_ok, c, b + 1)
                        wait(pool, h_stored[b], c.minus(1), 16)
                        nc.gpsimd.tensor_tensor(h_out[:, b, :], ho_tmp[:, :], rc[:, 1, :], ALU.add).then_inc(ho_ok.sem, 1)
                first_norm(G - 1)

            text_steps(pool, step)

            text_over(pool)
            pool.memset(vj[:, :, :, :, HD:HA], 1.0).then_inc(pads.sem, 1)
            for m in (mve, mvq, mv3, mv4):
                pool.memset(m[:], 0.0).then_inc(pads.sem, 1)
            pool.wait_ge(jw_in.sem, 96)
            pool.wait_ge(pads.sem, 5)

            def jstep(n, d, e, f, p):
                if n is not None:
                    rstd(rse[:, :], mve[:, 1:2], 1, vee_ok, n, 1, rse_ok)
                if f is not None:
                    rstd(rs4[:, :], mv4[:, :, 1], 2, ve4_ok, f, 1, rs4_ok)
                if d is not None:
                    for it in range(2):
                        m = ROWS[it]
                        wait(pool, xq_ok, d, it + 1)
                        wait(pool, r3_ok, d.minus(2), 2)
                        nc.gpsimd.tensor_tensor(xqb[0:m, p, it, :], xq[0:m, it, :], rj[0:m, 4, :], ALU.add).then_inc(xqb_ok.sem, 1)
                if n is not None:
                    wait(pool, e1_ok, n, 1)
                    nc.gpsimd.tensor_tensor(e2[:, :], e1[:, :], rj[:, 1, :], ALU.mult).then_inc(e2_ok.sem, 1)
                    wait(pool, e2_ok, n, 1)
                    wait(pool, hc_ok, n.minus(1), 2)
                    wait(pool, xq_ok, n.minus(1), 2)
                    nc.gpsimd.tensor_tensor(hj[:, 0, :], e2[:, :], rj[:, 2, :], ALU.add).then_inc(e3_ok.sem, 1)
                    rstd(rsq[:, :], mvq[:, :, 1], 2, veq_ok, n, 1, rsq_ok)
                if e is not None:
                    rstd(rs3[:, :], mv3[:, :, 1], 2, ve3_ok, e, 1, rs3_ok)
                    for it in range(2):
                        m = ROWS[it]
                        wait(pool, x3_ok, e, it + 1)
                        nc.gpsimd.tensor_tensor(t3[0:m, it, :], x3[0:m, it, :], rj[0:m, 5, :], ALU.mult).then_inc(t3_ok.sem, 1)
                    for it in range(2):
                        m = ROWS[it]
                        wait(pool, t3_ok, e, it + 1)
                        nc.gpsimd.tensor_tensor(t4[0:m, it, :], t3[0:m, it, :], rj[0:m, 6, :], ALU.add).then_inc(t4_ok.sem, 1)
                    for it in range(2):
                        m = ROWS[it]
                        wait(pool, t4_ok, e, it + 1)
                        wait(pool, yj_ok, e.minus(2), 2)
                        nc.gpsimd.tensor_tensor(h2[0:m, 1 - p, it, :], t4[0:m, it, :], hc[0:m, 1 - p, it, :], ALU.add).then_inc(h2_ok.sem, 1)

            joint_steps(pool, jstep)

        @block.scalar
        def _(act):
            act.wait_ge(consts_in.sem, 16)

            def step(a, b_, c):
                if a is not None:
                    for pair in range(2):
                        wait(act, hT_ps, a, pair + 1)
                        if pair == 0:
                            wait(act, v_ps, a.minus(1), G)
                        nc.scalar.activation(hT[:, :, pair * 2 * TXT:(pair + 1) * 2 * TXT],
                                             bank[pair][0:HALF, 0:4 * TXT].rearrange("p (c t) -> p c t", c=2),
                                             ACT.Identity).then_inc(hT_sb.sem, 1)
                    layer_in(act, wa_in, a)
                if c is not None:
                    layer_in(act, wc_in, c)

                def gelus(m):
                    if c is not None:
                        wait(act, fc_ps, c, m + 1)
                        if m == 0:
                            wait(act, ml_ps, c.minus(1), G)
                        nc.scalar.activation(gel[:, m, :], bank[6 + m % 2][:, 0:GT], ACT.Gelu_apprx_tanh,
                                             bias=wc2[:, C2_COL + m:C2_COL + m + 1]).then_inc(gelu_ok.sem, 1)

                def queries(m):
                    if a is not None:
                        wait(act, qk_ps, a, 2 * m + 1)
                        if m == 0:
                            wait(act, s_ps, a.minus(1), G)
                        for par, dst in enumerate((q_even, q_odd)):
                            nc.scalar.activation(dst[:, m, :], bank[2 - m][0:HALF, 0:GT], ACT.Identity,
                                                 bias=wa[:, A_COL + 2 * par + m:A_COL + 2 * par + m + 1],
                                                 scale=cst[0:HALF, CST_EVEN + par:CST_EVEN + par + 1]).then_inc(q_sb.sem, 1)

                queries(0)
                queries(1)
                for m in range(MH):
                    gelus(m)

                def attended(b):
                    if b_ is not None:
                        wait(act, aT_ps, b_, b + 1)
                        wait(act, pj_ps, b_, b)
                        nc.scalar.activation(aT[:, :], bank[5][0:HALF, 0:2 * TXT], ACT.Identity).then_inc(aT_sb.sem, 1)

                def exponents(item, b):
                    if item is not None:
                        wait(act, shifted, item, b + 1)
                        nc.scalar.activation(sc[:, b, :, :], sc[:, b, :, :], ACT.Exp).then_inc(expd.sem, 1)

                for b in range(G):
                    if b > 0:
                        attended(b - 1)
                    if b_ is not None:
                        for half in range(2):
                            wait(act, pT_ps, b_, 2 * b + half + 1)
                            wait(act, pv_ps, b_, b)
                            nc.scalar.activation(pT[:, half, :], bank[3 + half][0:TXT, 0:6 * TXT], ACT.Identity).then_inc(pT_sb.sem, 1)
                    if b == 0:
                        exponents(b_, G - 1)
                    else:
                        exponents(a, b - 1)
                attended(G - 1)

            text_steps(act, step)

            text_over(act)
            act.wait_ge(jw_in.sem, 96)
            act.wait_ge(r8_ok.sem, 2)

            def exponents(e, it):
                m = ROWS[it]
                wait(act, nm_ok, e, it + 1)
                for h in range(NH):
                    nc.scalar.activation(scj[0:m, it, h, :], scj[0:m, it, h, :], ACT.Exp,
                                         bias=nmj[0:m, it, h:h + 1]).then_inc(ej_ok.sem, 1)

            def jstep(n, d, e, f, p):
                if d is not None:
                    for it in range(2):
                        m = ROWS[it]
                        wait(act, e3_ok, d, 1)
                        wait(act, ht_in, d, 16)
                        wait(act, h2_ok, d.minus(2), 2)
                        nc.scalar.activation(hc[0:m, p, it, :], hj[0:m, it, :], ACT.Identity).then_inc(hc_ok.sem, 1)
                    for unit in range(1, 12, 2):
                        it, q4 = unit // 6, unit % 6 // 2
                        m = ROWS[it]
                        wait(act, pos_ps, d, unit + 1)
                        wait(act, pos_written[it], d.minus(1), 16)
                        nc.scalar.activation(pos_out[0:m, it, 4 * q4 + 1:4 * q4 + 4:2, :],
                                             bank[unit % 4][0:m, 0:2 * WIN].rearrange("p (h w) -> p h w", h=2),
                                             ACT.Identity).then_inc(pos_odd.sem, 1)
                if e is not None:
                    exponents(e, 0)
                if f is not None:
                    for t in range(MH):
                        wait(act, fj_ps, f, t // 3 + 1)
                        if t == 0:
                            wait(act, mj_ps, f.minus(1), 1)
                        nc.scalar.activation(gj[:, t, :], bank[4 + t // 3][:, (t % 3) * S:(t % 3 + 1) * S], ACT.Gelu,
                                             bias=wk[:, K_INB + t:K_INB + t + 1]).then_inc(gj_ok.sem, 1)
                if e is not None:
                    exponents(e, 1)
                if n is not None:
                    wait(act, xqT_ps, n, 1)
                    wait(act, vj_ps, n.minus(1), 1)
                    nc.scalar.activation(xqT[:, :, :], bank[6][0:HALF, 0:2 * S].rearrange("p (c t) -> p c t", c=2),
                                         ACT.Identity).then_inc(xqT_sb.sem, 1)
                if e is not None:
                    for tr in range(4):
                        for jt in range(2):
                            wait(act, ptj_ps, e, 2 * tr + jt + 1)
                            if tr >= 2:
                                wait(act, pvj_ps, e, tr - 1)
                            else:
                                wait(act, pvj_ps, e.minus(1), tr + 3)
                            nc.scalar.activation(pTj[0:ROWS[jt], tr % 2, jt, :], bank[4 + jt][0:ROWS[jt], 0:3 * S],
                                                 ACT.Identity).then_inc(ptj_sb.sem, 1)
                    wait(act, atT_ps, e, 1)
                    nc.scalar.activation(aTj[:, :], bank[6][0:HALF, 0:2 * S], ACT.Identity).then_inc(atT_sb.sem, 1)

            joint_steps(act, jstep)

        @block.tensor
        def _(pe):
            pe.wait_ge(consts_in.sem, 16)
            mm = nc.tensor.matmul

            def step(a, b_, c):
                if a is not None:
                    wait(pe, h_in, a, 16)
                    wait(pe, masked, a.minus(1), 3 * G)
                    for pair in range(2):
                        for k in range(2):
                            for b in range(2 * pair, 2 * pair + 2):
                                col = (2 * k + b % 2) * TXT
                                last = nc.tensor.transpose(bank[pair][0:HALF, col:col + TXT],
                                                           h_tok[:, b, k * HALF:(k + 1) * HALF], ident[0:TXT, 0:TXT])
                        last.then_inc(hT_ps.sem, 1)
                    layer_in(pe, wa_in, a)
                    wait(pe, hT_sb, a, 2)
                    for m in range(4):
                        if m == 3:
                            wait(pe, q_sb, a, 2)
                        col = (m % 2) * D + (m // 2) * HALF
                        for k in range(2):
                            last = mm(bank[(2, 0, 1, 2)[m]][0:HALF, 0:GT], wa[:, k * 2 * D + col:k * 2 * D + col + HALF],
                                      hT[:, k, :], start=(k == 0), stop=(k == 1))
                        last.then_inc(qk_ps.sem, 1)
                if c is not None:
                    wait(pe, r2_ok, c.minus(1), G)
                    wait(pe, v_sb, b_ if b_ is not None else Item(pe, STEPS - 1), G)
                    for pair in range(2):
                        wait(pe, x1_ok, c, 2 * pair + 2)
                        for k in range(2):
                            for b in range(2 * pair, 2 * pair + 2):
                                col = (2 * k + b % 2) * TXT
                                last = nc.tensor.transpose(bank[6 + pair][0:HALF, col:col + TXT],
                                                           x1[:, b, k * HALF:(k + 1) * HALF], ident[0:TXT, 0:TXT])
                        last.then_inc(nT_ps.sem, 1)
                    layer_in(pe, wc_in, c)
                    wait(pe, nT_sb, c, 4)
                    for m in range(MH):
                        if m >= 2:
                            wait(pe, gelu_ok, c, m - 1)
                        for k in range(2):
                            last = mm(bank[6 + m % 2][:, 0:GT], wc[:, k * HID + m * 128:k * HID + (m + 1) * 128],
                                      nT[:, k, :], start=(k == 0), stop=(k == 1))
                        last.then_inc(fc_ps.sem, 1)
                if b_ is not None:
                    layer_in(pe, wb_in, b_)

                def scores(b):
                    if b == 0:
                        wait(pe, q_sb, a, 4)
                        wait(pe, k_sb, a, 2)
                    else:
                        wait(pe, masked, a, 3 * b)
                    for half in range(2):
                        for par, q in enumerate((q_even, q_odd)):
                            for r in range(3):
                                col = (2 * half + par) * TXT
                                last = mm(bank[r][0:TXT, col:col + TXT],
                                          q[32 * r:32 * r + 32, half, b * TXT:(b + 1) * TXT],
                                          kT[32 * r:32 * r + 32, half, b * TXT:(b + 1) * TXT],
                                          start=True, stop=True, tile_position=(32 * r, 0))
                    last.then_inc(s_ps.sem, 1)

                def attended_t(b):
                    wait(pe, att_ok, b_, b + 1)
                    for k in range(2):
                        last = nc.tensor.transpose(bank[5][0:HALF, k * TXT:(k + 1) * TXT],
                                                   att[:, k * HALF:(k + 1) * HALF], ident[0:TXT, 0:TXT])
                    last.then_inc(aT_ps.sem, 1)

                def project(b):
                    wait(pe, aT_sb, b_, b + 1)
                    for k in range(2):
                        last = mm(bank[5][0:TXT, 0:D], aT[:, k * TXT:(k + 1) * TXT], wb[:, k * D:(k + 1) * D],
                                  start=(k == 0), stop=(k == 1))
                    last.then_inc(pj_ps.sem, 1)

                def transposes(b):
                    wait(pe, expd, b_, b + 1)
                    for half in range(2):
                        if b > 0:
                            wait(pe, pT_sb, b_, 2 * b - 1 + half)
                        else:
                            wait(pe, pT_sb, b_.minus(1), 2 * G - 1 + half)
                        for i in range(6):
                            last = nc.tensor.transpose(bank[3 + half][0:TXT, i * TXT:(i + 1) * TXT],
                                                       sc[:, b, 6 * half + i, :], ident[0:TXT, 0:TXT])
                        last.then_inc(pT_ps.sem, 1)

                def down(b):
                    wait(pe, gelu_ok, c, MH)
                    if b >= 2:
                        wait(pe, r2_ok, c, b - 1)
                        if a is not None:
                            wait(pe, v_sb, a, b - 1)
                    for m in range(MH):
                        last = mm(bank[6 + b % 2][0:TXT, 0:D], gel[:, m, b * TXT:(b + 1) * TXT],
                                  wc2[:, m * D:(m + 1) * D], start=(m == 0), stop=(m == MH - 1))
                    last.then_inc(ml_ps.sem, 1)

                def weighted(b):
                    wait(pe, v_sb, b_, b + 1)
                    wait(pe, pT_sb, b_, 2 * b + 2)
                    if b > 0:
                        wait(pe, r1_ok, b_, b)
                    else:
                        wait(pe, r1_ok, b_.minus(1), G)
                    for h in range(NH):
                        last = mm(bank[5][0:TXT, h * HA:(h + 1) * HA], pT[:, h // 6, (h % 6) * TXT:(h % 6 + 1) * TXT],
                                  v_tok[:, b, h, :], start=True, stop=True)
                    last.then_inc(pv_ps.sem, 1)

                def values(b):
                    if c is not None:
                        wait(pe, r2_ok, c, b + 1)
                    if b >= 2:
                        wait(pe, v_sb, a, b - 1)
                    elif c is None:
                        wait(pe, v_sb, a.minus(1), G)
                    for k in range(2):
                        last = mm(bank[6 + b % 2][0:TXT, 0:D], hT[:, k, b * TXT:(b + 1) * TXT],
                                  wa[:, A_V + k * D:A_V + (k + 1) * D], start=(k == 0), stop=(k == 1))
                    last.then_inc(v_ps.sem, 1)

                for b in range(G):
                    if a is not None:
                        scores(b)
                    if b_ is not None and b > 0:
                        attended_t(b - 1)
                    if b_ is not None:
                        transposes(b)
                    if b_ is not None and b > 0:
                        project(b - 1)
                    if a is not None and b > 0:
                        values(b - 1)
                    if c is not None and b < G - 1:
                        down(b)
                    if b_ is not None:
                        weighted(b)
                if c is not None:
                    down(G - 1)
                if b_ is not None:
                    attended_t(G - 1)
                if a is not None:
                    values(G - 1)
                if b_ is not None:
                    project(G - 1)

            text_steps(pe, step)

            text_over(pe)
            pe.wait_ge(jw_in.sem, 96)
            for g in ((v_sb, G), (masked, 3 * G), (pT_sb, 2 * G), (r1_ok, G), (r2_ok, G)):
                wait(pe, g[0], Item(pe, STEPS - 1), g[1])
            for m in range(6):
                if m >= 2:
                    pe.wait_ge(rel_ok.sem, m - 1)
                for k in range(2):
                    last = mm(bank[m % 2][:, 0:NT], wj[:, J_R + k * 768 + m * 128:J_R + k * 768 + (m + 1) * 128],
                              wj[:, J_POS + k * NT:J_POS + (k + 1) * NT], start=(k == 0), stop=(k == 1))
                last.then_inc(rel_ps.sem, 1)
            pe.wait_ge(rel_ok.sem, 6)

            def jstep(n, d, e, f, p):
                prev_e = f
                prev_d = d.minus(1) if d is not None else e
                if prev_d is not None:
                    wait(pe, pos_even, prev_d, 6)
                    wait(pe, pos_odd, prev_d, 6)
                if prev_e is not None:
                    wait(pe, sj_sb, prev_e, 24)
                    wait(pe, ptj_sb, prev_e, 8)
                    wait(pe, r3_ok, prev_e, 2)
                elif d is not None:
                    wait(pe, xqT_sb, d, 1)
                if n is not None:
                    pair_wait(pe, pat_in[1 - p], n, 1 - p)
                    for k in range(3):
                        last = mm(bank[6][0:IMG, 0:D], pat[:, 1 - p, k * IMG:(k + 1) * IMG], wtok[:, k, :],
                                  start=(k == 0), stop=(k == 2))
                    last.then_inc(e_ps.sem, 1)
                if d is not None:
                    wait(pe, xqT_sb, d, 1)
                    for half in range(2):
                        for i in range(3):
                            t = 3 * half + i
                            last = mm(bank[half][:, i * S:(i + 1) * S], wj[:, J_Q + t * 128:J_Q + (t + 1) * 128],
                                      xqT[:, half, :], start=True, stop=True)
                        last.then_inc(qj_ps.sem, 1)
                    for half in range(2):
                        for i in range(3):
                            t = 3 * half + i
                            last = mm(bank[2 + half][:, i * S:(i + 1) * S], wj[:, J_K + t * 128:J_K + (t + 1) * 128],
                                      xqT[:, half, :], start=True, stop=True)
                        last.then_inc(kj_ps.sem, 1)
                    for it in range(2):
                        m = ROWS[it]
                        for k in range(2):
                            last = mm(bank[4][0:m, it * D + k * HALF:it * D + (k + 1) * HALF],
                                      xqT[:, k, OFF[it]:OFF[it] + m], wj[:, J_V + k * HALF:J_V + (k + 1) * HALF],
                                      start=True, stop=True)
                    last.then_inc(vj_ps.sem, 1)
                    for unit in range(12):
                        it, q4, par = unit // 6, unit % 6 // 2, unit % 2
                        m = ROWS[it]
                        if unit < 2:
                            wait(pe, qc_ok, d, unit + 1)
                            wait(pe, qr_ok, d, 2)
                        elif unit < 4:
                            wait(pe, kj_ok, d, unit - 1)
                        else:
                            wait(pe, (pos_even, pos_odd)[par], d, (unit - 4) // 2 + 1)
                        first = (S - 1) - (OFF[it] + m - 1)
                        w = S + m - 1
                        for i in range(2):
                            t = 2 * q4 + i
                            last = mm(bank[unit % 4][0:m, i * WIN:i * WIN + w],
                                      qr[64 * par:64 * par + 64, t, OFF[it]:OFF[it] + m],
                                      rel[64 * par:64 * par + 64, t, first:first + w],
                                      start=True, stop=True, tile_position=(64 * par, 0))
                        last.then_inc(pos_ps.sem, 1)
                if f is not None:
                    for it in range(2):
                        wait(pe, x4_ok, f, it + 1)
                    wait(pe, yj_ok, f.minus(1), 2)
                    for it in range(2):
                        m = ROWS[it]
                        for k in range(2):
                            last = nc.tensor.transpose(bank[7][0:HALF, k * S + OFF[it]:k * S + OFF[it] + m],
                                                       x4[0:m, it, k * HALF:(k + 1) * HALF], ident[0:m, 0:m])
                    last.then_inc(x4T_ps.sem, 1)

                def content(it):
                    m = ROWS[it]
                    for i4 in range(4):
                        unit = 4 * it + i4
                        half, par = i4 // 2, i4 % 2
                        if it == 0:
                            if d is not None:
                                wait(pe, (pos_even, pos_odd)[par], d, 5 + i4 // 2)
                        else:
                            wait(pe, sj_sb, e, 3 * (unit - 4) + 3)
                        for i in range(3):
                            t = 3 * half + i
                            last = mm(bank[i4][0:m, i * S:(i + 1) * S],
                                      qc[64 * par:64 * par + 64, 1 - p, t, OFF[it]:OFF[it] + m],
                                      kj[64 * par:64 * par + 64, 1 - p, t, :],
                                      start=True, stop=True, tile_position=(64 * par, 0))
                        last.then_inc(sj_ps.sem, 1)

                if e is not None:
                    wait(pe, qc_ok, e, 2)
                    wait(pe, kj_ok, e, 2)
                    content(0)
                if f is not None:
                    wait(pe, x4T_sb, f, 1)
                    if d is not None:
                        wait(pe, vj_ok, d, 2)
                    for half in range(2):
                        for i in range(3):
                            t = 3 * half + i
                            for k in range(2):
                                last = mm(bank[4 + half][:, i * S:(i + 1) * S],
                                          wj[:, J_IN + k * HID + t * 128:J_IN + k * HID + (t + 1) * 128],
                                          x4T[:, k, :], start=(k == 0), stop=(k == 1))
                        last.then_inc(fj_ps.sem, 1)
                if e is not None:
                    content(1)
                if n is not None:
                    for it in range(2):
                        wait(pe, xq_ok, n, it + 1)
                    wait(pe, e0_ok, n, 1)
                    for it in range(2):
                        m = ROWS[it]
                        for k in range(2):
                            last = nc.tensor.transpose(bank[6][0:HALF, k * S + OFF[it]:k * S + OFF[it] + m],
                                                       xq[0:m, it, k * HALF:(k + 1) * HALF], ident[0:m, 0:m])
                    last.then_inc(xqT_ps.sem, 1)
                if f is not None:
                    wait(pe, gj_ok, f, 6)
                    for it in range(2):
                        m = ROWS[it]
                        for t in range(MH):
                            last = mm(bank[7][0:m, it * D:(it + 1) * D], gj[:, t, OFF[it]:OFF[it] + m],
                                      wk[:, K_OUT + t * D:K_OUT + (t + 1) * D], start=(t == 0), stop=(t == MH - 1))
                    last.then_inc(mj_ps.sem, 1)

                def triple(tr):
                    for it in range(2):
                        wait(pe, ej_ok, e, 12 * it + 3 * tr + 3)
                    for jt in range(2):
                        if tr == 0:
                            if d is not None:
                                wait(pe, vj_ok, d, 2)
                        else:
                            wait(pe, ptj_sb, e, 2 * tr - 1 + jt)
                        for i in range(3):
                            for it in range(2):
                                m = ROWS[it]
                                last = nc.tensor.transpose(bank[4 + jt][0:ROWS[jt], i * S + OFF[it]:i * S + OFF[it] + m],
                                                           scj[0:m, it, 3 * tr + i, OFF[jt]:OFF[jt] + ROWS[jt]],
                                                           ident[0:m, 0:m])
                        last.then_inc(ptj_ps.sem, 1)

                def weighted(tr):
                    wait(pe, ptj_sb, e, 2 * tr + 2)
                    if tr == 0:
                        wait(pe, vj_ok, e, 2)
                        if n is not None:
                            wait(pe, xqT_sb, n, 1)
                    for i in range(3):
                        for it in range(2):
                            m = ROWS[it]
                            h = 3 * tr + i
                            for jt in range(2):
                                last = mm(bank[6][0:m, it * NH * HA + h * HA:it * NH * HA + (h + 1) * HA],
                                          pTj[0:ROWS[jt], tr % 2, jt, i * S + OFF[it]:i * S + OFF[it] + m],
                                          vj[0:ROWS[jt], 1 - p, jt, h, :], start=(jt == 0), stop=(jt == 1))
                    last.then_inc(pvj_ps.sem, 1)

                if e is not None:
                    for tr in range(4):
                        triple(tr)
                        if tr > 0:
                            weighted(tr - 1)
                    weighted(3)
                    for it in range(2):
                        wait(pe, atj_ok, e, it + 1)
                    for it in range(2):
                        m = ROWS[it]
                        for k in range(2):
                            last = nc.tensor.transpose(bank[6][0:HALF, k * S + OFF[it]:k * S + OFF[it] + m],
                                                       atj[0:m, it, k * HALF:(k + 1) * HALF], ident[0:m, 0:m])
                    last.then_inc(atT_ps.sem, 1)
                    wait(pe, atT_sb, e, 1)
                    for it in range(2):
                        m = ROWS[it]
                        for k in range(2):
                            last = mm(bank[6][0:m, it * D:(it + 1) * D], aTj[:, k * S + OFF[it]:k * S + OFF[it] + m],
                                      wj[:, J_O + k * D:J_O + (k + 1) * D], start=(k == 0), stop=(k == 1))
                    last.then_inc(wo_ps.sem, 1)

            joint_steps(pe, jstep)

        @block.vector
        def _(dve):
            V = nc.vector
            dve.wait_ge(mask_in.sem, 16)
            dve.wait_ge(consts_in.sem, 16)
            flat = ext[:, :, :].rearrange("p b k -> p (b k)")
            V.tensor_scalar(flat, flat, -1.0, 1.0, ALU.mult, ALU.add).then_inc(ext_one.sem, 1)
            dve.wait_ge(ext_one.sem, 1)
            V.tensor_scalar(flat, flat, FMIN, None, ALU.mult).then_inc(ext_scaled.sem, 1)
            dve.wait_ge(ext_scaled.sem, 1)
            neg = cst[0:TXT, CST_NEG:CST_NEG + TXT].unsqueeze(1).broadcast_to([TXT, G, TXT])
            for g in range(B // G):
                V.tensor_tensor(ext[:, g * G:(g + 1) * G, :], ext[:, g * G:(g + 1) * G, :], neg, ALU.add).then_inc(ext_ready.sem, 1)
            dve.wait_ge(pos_row_in.sem, 16)
            for g in range(GROUPS):
                dve.wait_ge(emb_in[g].sem, 16 * G)
                V.tensor_tensor(emb[:, g * G:(g + 1) * G, :], emb[:, g * G:(g + 1) * G, :],
                                pos_row[:, :].unsqueeze(1).broadcast_to([TXT, G, D]), ALU.add).then_inc(emb_done.sem, 1)
            dve.wait_ge(ones_set.sem, 1)
            causal = cst[0:TXT, CST_CAUSAL:CST_CAUSAL + TXT].unsqueeze(1).broadcast_to([TXT, 2, TXT])

            def step(a, b_, c):
                if a is not None:
                    layer_in(dve, wa_in, a)
                    for m in range(2):
                        wait(dve, qk_ps, a, 2 * m + 2)
                        if m == 0:
                            wait(dve, s_ps, a.minus(1), G)
                        V.tensor_scalar(kT[:, m, :], bank[(0, 2)[m]][0:HALF, 0:GT],
                                        wa[:, A_COL + 4 + m:A_COL + 5 + m], HD ** -0.5, ALU.add, ALU.mult).then_inc(k_sb.sem, 1)
                if c is not None:
                    layer_in(dve, wc_in, c)
                    for pair in range(2):
                        wait(dve, nT_ps, c, pair + 1)
                        if pair == 0:
                            wait(dve, fc_ps, c.minus(1), MH)
                        for k in range(2):
                            V.tensor_scalar(nT[:, k, pair * 2 * TXT:(pair + 1) * 2 * TXT],
                                            bank[6 + pair][0:HALF, 2 * k * TXT:(2 * k + 2) * TXT],
                                            wc[:, C_COL + k:C_COL + k + 1], wc[:, C_COL + 2 + k:C_COL + 3 + k],
                                            ALU.mult, ALU.add).then_inc(nT_sb.sem, 1)

                def first_norm_stats(b):
                    wait(dve, pj_ps, b_, b + 1)
                    wait(dve, x1_ok, b_, b)
                    wait(dve, hb_ok, b_, b + 1)
                    V.tensor_tensor(r1[:, :], bank[5][0:TXT, 0:D], h_bias[:, b, :], ALU.add).then_inc(r1_ok.sem, 1)
                    wait(dve, r1_ok, b_, b + 1)
                    V.bn_stats(st1[:, :], r1[:, :]).then_inc(st1_ok.sem, 1)
                    wait_alone(dve, st1_ok, b_, b + 1)
                    V.bn_aggr(mv1[:, :], st1[:, :]).then_inc(mv1_ok.sem, 1)
                    wait(dve, mv1_ok, b_, b + 1)
                    V.tensor_scalar(mv1[:, 1:2], mv1[:, 1:2], EPS, None, ALU.add).then_inc(ve1_ok.sem, 1)

                def first_norm(b):
                    wait(dve, rs1_ok, b_, b + 1)
                    if c is not None:
                        wait(dve, nT_ps, c, b // 2 + 1)
                        wait(dve, nb_ok, c, b + 1)
                    V.tensor_scalar(x1[:, b, :], r1[:, :], mv1[:, 0:1], rs1[:, 0:1], ALU.subtract, ALU.mult).then_inc(x1_ok.sem, 1)

                def mask(b):
                    wait(dve, s_ps, a, b + 1)
                    if b_ is not None:
                        wait(dve, pT_ps, b_, 2 * b + 2)
                    for r in range(3):
                        dst = sc[:, b, :, :].rearrange("p (half r par) k -> p half r par k", half=2, r=3)[:, :, r]
                        src = bank[r][0:TXT, 0:4 * TXT].rearrange("p (half par k) -> p half par k", half=2, par=2)
                        msk = cst[0:TXT, CST_CAUSAL:CST_CAUSAL + TXT].unsqueeze(1).unsqueeze(1).broadcast_to([TXT, 2, 2, TXT])
                        V.tensor_tensor(dst, src, msk, ALU.mult).then_inc(masked.sem, 1)

                def shift(item, b):
                    if item is not None:
                        wait(dve, biased, item, b + 1)
                        V.tensor_reduce(mx[:, b, :], sc[:, b, :, :], AX.X, ALU.max).then_inc(maxed.sem, 1)
                        wait(dve, maxed, item, b + 1)
                        V.tensor_tensor(sc[:, b, :, :], sc[:, b, :, :], mx[:, b, :].unsqueeze(2).broadcast_to([TXT, NH, TXT]),
                                        ALU.subtract).then_inc(shifted.sem, 1)

                def second_norm_stats(b):
                    wait(dve, ml_ps, c, b + 1)
                    wait(dve, x2_ok, c, b)
                    wait(dve, nb_ok, c, b + 1)
                    V.tensor_tensor(r2[:, :], bank[6 + b % 2][0:TXT, 0:D], n_bias[:, b, :], ALU.add).then_inc(r2_ok.sem, 1)
                    wait(dve, r2_ok, c, b + 1)
                    V.bn_stats(st2[:, :], r2[:, :]).then_inc(st2_ok.sem, 1)
                    wait_alone(dve, st2_ok, c, b + 1)
                    V.bn_aggr(mv2[:, :], st2[:, :]).then_inc(mv2_ok.sem, 1)
                    wait(dve, mv2_ok, c, b + 1)
                    V.tensor_scalar(mv2[:, 1:2], mv2[:, 1:2], EPS, None, ALU.add).then_inc(ve2_ok.sem, 1)

                def second_norm(b):
                    wait(dve, rs2_ok, c, b + 1)
                    wait(dve, hot_ok, c, b)
                    V.tensor_scalar(x2[:, :], r2[:, :], mv2[:, 0:1], rs2[:, 0:1], ALU.subtract, ALU.mult).then_inc(x2_ok.sem, 1)

                def attend(b):
                    wait(dve, pv_ps, b_, b + 1)
                    pv = bank[5][0:TXT, 0:NH * HA].rearrange("p (h e) -> p h e", h=NH)
                    V.reciprocal(rden[:, :], pv[:, :, HD]).then_inc(rden_ok.sem, 1)
                    wait(dve, rden_ok, b_, b + 1)
                    wait(dve, aT_ps, b_, b)
                    V.tensor_tensor(att[:, :].rearrange("p (h e) -> p h e", h=NH), pv[:, :, 0:HD],
                                    rden[:, :].unsqueeze(2).broadcast_to([TXT, NH, HD]), ALU.mult).then_inc(att_ok.sem, 1)

                def value(b):
                    wait(dve, v_ps, a, b + 1)
                    if b_ is not None:
                        wait(dve, pv_ps, b_, b + 1)
                    V.tensor_tensor(v_tok[:, b, :, 0:HD], bank[6 + b % 2][0:TXT, 0:D].rearrange("p (h e) -> p h e", h=NH),
                                    ra[:, 0, :].rearrange("p (h e) -> p h e", h=NH), ALU.add).then_inc(v_sb.sem, 1)

                for b in range(G):
                    if b_ is not None and b > 0:
                        attend(b - 1)
                    if a is not None:
                        mask(b)
                    if b == 0:
                        shift(b_, G - 1)
                    else:
                        shift(a, b - 1)
                    if b_ is not None and b > 0:
                        first_norm_stats(b - 1)
                    if a is not None and b > 0:
                        value(b - 1)
                    if c is not None and b < G - 1:
                        second_norm_stats(b)
                    if b_ is not None and b > 0:
                        first_norm(b - 1)
                    if c is not None and b < G - 1:
                        second_norm(b)
                if b_ is not None:
                    attend(G - 1)
                if c is not None:
                    second_norm_stats(G - 1)
                    second_norm(G - 1)
                if a is not None:
                    value(G - 1)
                if b_ is not None:
                    first_norm_stats(G - 1)
                    first_norm(G - 1)

            text_steps(dve, step)

            text_over(dve)
            dve.wait_ge(jw_in.sem, 96)
            dve.wait_ge(pads.sem, 5)
            V.tensor_scalar(rw8[:, :], wk[:, K_RW:K_RW + 6], DH ** -0.5, None, ALU.mult).then_inc(r8_ok.sem, 1)
            V.tensor_scalar(rr8[:, :], wk[:, K_RR:K_RR + 6], DH ** -0.5, None, ALU.mult).then_inc(r8_ok.sem, 1)
            dve.wait_ge(r8_ok.sem, 2)
            for m in range(6):
                dve.wait_ge(rel_ps.sem, m + 1)
                V.tensor_copy(rel[:, m, :], bank[m % 2][:, 0:NT]).then_inc(rel_ok.sem, 1)

            def norm_stats(src, stats, mv, stats_ok, mv_ok, ve_ok, item, eps, ready):
                for it in range(2):
                    n = ROWS[it]
                    ready(it)
                    V.bn_stats(stats[0:n, it, :], src[0:n, it, :]).then_inc(stats_ok.sem, 1)
                for it in range(2):
                    n = ROWS[it]
                    wait_alone(dve, stats_ok, item, it + 1)
                    V.bn_aggr(mv[0:n, it, :], stats[0:n, it, :]).then_inc(mv_ok.sem, 1)
                wait(dve, mv_ok, item, 2)
                V.tensor_scalar(mv[:, :, 1], mv[:, :, 1], eps, None, ALU.add).then_inc(ve_ok.sem, 1)

            def jstep(n, d, e, f, p):
                if n is not None:
                    wait(dve, e_ps, n, 1)
                    wait(dve, e1_ok, n.minus(1), 1)
                    V.tensor_tensor(e0[:, :], bank[6][0:IMG, 0:D], rj[:, 0, :], ALU.add).then_inc(e0_ok.sem, 1)
                    wait(dve, e0_ok, n, 1)
                    V.bn_stats(ste[:, :], e0[:, :]).then_inc(ste_ok.sem, 1)
                    wait_alone(dve, ste_ok, n, 1)
                    V.bn_aggr(mve[:, :], ste[:, :]).then_inc(mve_ok.sem, 1)
                    wait(dve, mve_ok, n, 1)
                    V.tensor_scalar(mve[:, 1:2], mve[:, 1:2], EPS, None, ALU.add).then_inc(vee_ok.sem, 1)
                if f is not None:
                    norm_stats(h2[:, p], st4, mv4, st4_ok, mv4_ok, ve4_ok, f, EPS, lambda it: wait(dve, h2_ok, f, it + 1))
                if d is not None:
                    for half in range(2):
                        wait(dve, qj_ps, d, half + 1)
                        src = bank[half][:, 0:3 * S].rearrange("p (m t) -> p m t", m=3)
                        ms = slice(3 * half, 3 * half + 3)
                        wait(dve, pos_ps, d.minus(1), 12)
                        V.scalar_tensor_tensor(qr[:, ms, :], src, DH ** -0.5, rr8[:, ms].unsqueeze(2).broadcast_to([128, 3, S]),
                                               ALU.mult, ALU.add).then_inc(qr_ok.sem, 1)
                        V.scalar_tensor_tensor(qc[:, p, ms, :], src, DH ** -0.5, rw8[:, ms].unsqueeze(2).broadcast_to([128, 3, S]),
                                               ALU.mult, ALU.add).then_inc(qc_ok.sem, 1)
                if n is not None:
                    wait(dve, rse_ok, n, 1)
                    wait(dve, e2_ok, n.minus(1), 1)
                    V.tensor_scalar(e1[:, :], e0[:, :], mve[:, 0:1], rse[:, 0:1], ALU.subtract, ALU.mult).then_inc(e1_ok.sem, 1)
                if d is not None:
                    for half in range(2):
                        wait(dve, kj_ps, d, half + 1)
                        src = bank[2 + half][:, 0:3 * S].rearrange("p (m t) -> p m t", m=3)
                        ms = slice(3 * half, 3 * half + 3)
                        V.tensor_tensor(kj[:, p, ms, :], src, wk[:, K_BK + 3 * half:K_BK + 3 * half + 3].unsqueeze(2).broadcast_to([128, 3, S]),
                                        ALU.add).then_inc(kj_ok.sem, 1)
                    wait(dve, vj_ps, d, 1)
                    for it in range(2):
                        m = ROWS[it]
                        V.tensor_tensor(vj[0:m, p, it, :, 0:HD], bank[4][0:m, it * D:(it + 1) * D].rearrange("p (h e) -> p h e", h=NH),
                                        rj[0:m, 3, :].rearrange("p (h e) -> p h e", h=NH), ALU.add).then_inc(vj_ok.sem, 1)
                if f is not None:
                    wait(dve, rs4_ok, f, 1)
                    wait(dve, x4T_ps, f.minus(1), 1)
                    for it in range(2):
                        m = ROWS[it]
                        V.tensor_scalar(x4[0:m, it, :], h2[0:m, p, it, :], mv4[0:m, it, 0:1], rs4[0:m, it:it + 1],
                                        ALU.subtract, ALU.mult).then_inc(x4_ok.sem, 1)
                if n is not None:
                    norm_stats(hj, stq, mvq, stq_ok, mvq_ok, veq_ok, n, EPS,
                               lambda it: wait(dve, (e3_ok, ht_in)[it], n, (1, 16)[it]))
                if d is not None:
                    for unit in range(0, 12, 2):
                        it, q4 = unit // 6, unit % 6 // 2
                        m = ROWS[it]
                        wait(dve, pos_ps, d, unit + 1)
                        wait(dve, pos_written[it], d.minus(1), 16)
                        V.tensor_copy(pos_out[0:m, it, 4 * q4:4 * q4 + 4:2, :],
                                      bank[unit % 4][0:m, 0:2 * WIN].rearrange("p (h w) -> p h w", h=2)).then_inc(pos_even.sem, 1)
                if f is not None:
                    wait(dve, x4T_ps, f, 1)
                    V.tensor_copy(x4T[:, :, :], bank[7][0:HALF, 0:2 * S].rearrange("p (c t) -> p c t", c=2)).then_inc(x4T_sb.sem, 1)

                def add_positions(it):
                    m = ROWS[it]
                    wait_alone(dve, pos_back[it], e, 16)
                    wait_alone(dve, ptj_ps, e.minus(1), 8)
                    for i4 in range(4):
                        half, par = i4 // 2, i4 % 2
                        wait_alone(dve, sj_ps, e, 4 * it + i4 + 1)
                        for i in range(3):
                            h = 6 * half + 2 * i + par
                            V.tensor_tensor_reduce(scj[0:m, it, h, :], bank[i4][0:m, i * S:(i + 1) * S],
                                                   pos_in[0:m, it, h, :], 1.0, FMIN, ALU.add, ALU.max,
                                                   mxj[0:m, it, h:h + 1]).then_inc(sj_sb.sem, 1)
                    wait(dve, sj_sb, e, 12 * (it + 1))
                    V.tensor_scalar(nmj[0:m, it, :], mxj[0:m, it, :], -1.0, None, ALU.mult).then_inc(nm_ok.sem, 1)

                if e is not None:
                    add_positions(0)
                if n is not None:
                    wait(dve, rsq_ok, n, 1)
                    wait(dve, xqT_ps, n.minus(1), 1)
                    wait(dve, xqb_ok, n.minus(1), 2)
                    for it in range(2):
                        m = ROWS[it]
                        V.tensor_scalar(xq[0:m, it, :], hj[0:m, it, :], mvq[0:m, it, 0:1], rsq[0:m, it:it + 1],
                                        ALU.subtract, ALU.mult).then_inc(xq_ok.sem, 1)
                if e is not None:
                    add_positions(1)
                if f is not None:
                    wait(dve, mj_ps, f, 1)
                    pair_wait(dve, y_stored[p], f.minus(2), p)
                    for it in range(2):
                        m = ROWS[it]
                        V.tensor_tensor(yj[0:m, p, it, :], bank[7][0:m, it * D:(it + 1) * D], h2[0:m, p, it, :], ALU.add).then_inc(yj_ok.sem, 1)
                if e is not None:
                    wait(dve, pvj_ps, e, 4)
                    pv = [bank[6][0:ROWS[it], it * NH * HA:(it + 1) * NH * HA].rearrange("p (h e) -> p h e", h=NH) for it in range(2)]
                    for it in range(2):
                        V.reciprocal(rdj[0:ROWS[it], it, :], pv[it][:, :, HD]).then_inc(rdj_ok.sem, 1)
                    for it in range(2):
                        m = ROWS[it]
                        wait(dve, rdj_ok, e, it + 1)
                        V.tensor_tensor(atj[0:m, it, :].rearrange("p (h e) -> p h e", h=NH), pv[it][:, :, 0:HD],
                                        rdj[0:m, it, :].unsqueeze(2).broadcast_to([m, NH, HD]), ALU.mult).then_inc(atj_ok.sem, 1)
                    wait(dve, wo_ps, e, 1)
                    wait(dve, x3_ok, e.minus(1), 2)
                    wait(dve, xqb_ok, e, 2)
                    for it in range(2):
                        m = ROWS[it]
                        V.tensor_tensor(r3[0:m, it, :], bank[6][0:m, it * D:(it + 1) * D], xqb[0:m, 1 - p, it, :], ALU.add).then_inc(r3_ok.sem, 1)
                    norm_stats(r3, st3, mv3, st3_ok, mv3_ok, ve3_ok, e, ATT_EPS, lambda it: wait(dve, r3_ok, e, it + 1))
                    wait(dve, rs3_ok, e, 1)
                    wait(dve, t3_ok, e.minus(1), 2)
                    for it in range(2):
                        m = ROWS[it]
                        V.tensor_scalar(x3[0:m, it, :], r3[0:m, it, :], mv3[0:m, it, 0:1], rs3[0:m, it:it + 1],
                                        ALU.subtract, ALU.mult).then_inc(x3_ok.sem, 1)

            joint_steps(dve, jstep)


def kernel(**inputs):
    import numpy as np
    import concourse.bacc as bacc
    from concourse.bass_utils import run_bass_kernel_spmd

    x = {k: np.asarray(v) for k, v in inputs.items()}

    def chunks(w):
        return np.concatenate([w[0:HALF], w[HALF:D]], axis=1)

    def columns(vec, rows):
        return vec.reshape(-1, rows).T

    img = x["x"][:, :, :90, :90].reshape(B, 3, 9, 10, 9, 10)
    patches = np.zeros((PK, B, 3, IMG), np.float32)
    patches[:, :, :, 1:] = img.transpose(3, 5, 0, 1, 2, 4).reshape(PK, B, 3, 81)

    wa, ra, wb, rb, wc, wc2, rc = [], [], [], [], [], [], []
    for l in range(LAYERS):
        w, bias = x["L0_txt_c_attn_w"][l], x["L0_txt_c_attn_b"][l]
        q_cols = columns(bias[0:D], HALF)
        even = np.zeros((HALF, 2), np.float32)
        odd = np.zeros((HALF, 2), np.float32)
        is_even = (np.arange(HALF) // HD) % 2 == 0
        even[is_even] = q_cols[is_even]
        odd[~is_even] = q_cols[~is_even]
        wa.append(np.concatenate([chunks(w[:, 0:2 * D]), chunks(w[:, 2 * D:]), even, odd, columns(bias[D:2 * D], HALF)], axis=1))
        ra.append(np.concatenate([bias[2 * D:], x["L0_txt_c_proj_b"][l]]))
        wb.append(chunks(x["L0_txt_c_proj_w"][l]))
        rb.append(np.concatenate([x["L0_txt_ln1_w"][l], x["L0_txt_ln1_b"][l], x["L0_txt_mlp_proj_b"][l]]))
        wc.append(np.concatenate([chunks(x["L0_txt_c_fc_w"][l]), columns(x["L0_txt_ln1_w"][l], HALF),
                                  columns(x["L0_txt_ln1_b"][l], HALF)], axis=1))
        wc2.append(np.concatenate([x["L0_txt_mlp_proj_w"][l].reshape(MH, 128, D).transpose(1, 0, 2).reshape(128, MH * D),
                                   columns(x["L0_txt_c_fc_b"][l], 128)], axis=1))
        rc.append(np.concatenate([x["L0_txt_ln2_w"][l], x["L0_txt_ln2_b"][l]]))

    def block_diagonal(w):
        n = w.shape[2]
        out = np.zeros((HALF, 2, 2, n), np.float32)
        for g in range(4):
            out[48 * (g % 2):48 * (g % 2) + 48, g // 2, g % 2] = w[g]
        return out.reshape(HALF, 4 * n)

    w_joint = np.concatenate([
        block_diagonal(x["L0_attn_Wq"]), block_diagonal(x["L0_attn_Wk"]), block_diagonal(x["L0_attn_Wv"]),
        chunks(x["L0_attn_Wo"]), chunks(x["L0_ffn_in_weight"].T),
        chunks(x["L0_attn_position_embeds"][1:NT + 1].T), chunks(x["L0_attn_r_kernel"].reshape(D, 768))], axis=1)
    w_joint128 = np.concatenate([
        x["L0_ffn_out_weight"].reshape(MH, 128, D).transpose(1, 0, 2).reshape(128, MH * D),
        columns(x["L0_ffn_in_bias"], 128), columns(x["L0_attn_r_w_bias"].reshape(-1), 128),
        columns(x["L0_attn_r_r_bias"].reshape(-1), 128), columns(x["L0_attn_bk"], 128)], axis=1)
    r_joint = np.concatenate([x["L0_tok_cls"].reshape(-1), x["L0_tok_b"], x["L0_tok_gamma"], x["L0_tok_beta"],
                              x["L0_attn_bv"], x["L0_attn_bo"], x["L0_attn_gamma"], x["L0_attn_beta"]])[None]

    consts = np.zeros((128, CST_W), np.float32)
    consts[:, CST_I:CST_I + 128] = np.eye(128)
    consts[0:TXT, CST_CAUSAL:CST_CAUSAL + TXT] = np.tril(np.ones((TXT, TXT)))
    consts[0:TXT, CST_NEG:CST_NEG + TXT] = NEG * (1 - np.tril(np.ones((TXT, TXT))))
    consts[:, CST_EVEN] = (np.arange(128) // HD) % 2 == 0
    consts[:, CST_ODD] = (np.arange(128) // HD) % 2 == 1
    consts[:, CST_PW:CST_PW + 2] = -0.5

    host = {
        "patches": patches.reshape(PK, B, 3 * IMG), "ids": x["x_txt"].T, "pos_ids": x["pos_S"][:, None],
        "mask": x["mask_BS_f1_0"].reshape(1, B * TXT), "tok_emb": x["L0_txt_tok_emb"], "pos_emb": x["L0_txt_pos_emb"],
        "w_a": np.stack(wa), "r_a": np.stack(ra), "w_b": np.stack(wb), "r_b": np.stack(rb),
        "w_c": np.stack(wc), "w_c2": np.stack(wc2), "r_c": np.stack(rc),
        "w_tok": x["L0_tok_W"].T.reshape(3, PK, D).transpose(1, 0, 2), "r_joint": r_joint,
        "w_joint": w_joint, "w_joint128": w_joint128, "consts": consts,
    }
    nc = bacc.Bacc("TRN2", target_bir_lowering=False, num_devices=1)
    arrays, args = {}, []
    for name, array in host.items():
        array = np.ascontiguousarray(array)
        arrays[f"in_{name}"] = array
        args.append(nc.dram_tensor(f"in_{name}", array.shape, mybir.dt.from_np(array.dtype), kind="ExternalInput").ap())
    args.append(nc.dram_tensor("out_0", (B, S, D), F32, kind="ExternalOutput").ap())
    args.append(nc.dram_tensor("h_text", (B, TXT, D), F32, kind="Internal").ap())
    args.append(nc.dram_tensor("pos_scratch", (2, IMG, NH * WIN), F32, kind="Internal").ap())
    early_fusion(nc, *args)
    result = run_bass_kernel_spmd(nc, [arrays], core_ids=[0])
    return result.results[0]["out_0"]
```

```python
import concourse.bass as bass
from concourse import mybir
from contextlib import ExitStack

F32 = mybir.dt.float32
I32 = mybir.dt.int32
U32 = mybir.dt.uint32
ALU = mybir.AluOpType
ACT = mybir.ActivationFunctionType
AX = mybir.AxisListType

B = 32
TXT = 77
IMG = 82
S = IMG + TXT
D = 192
HALF = D // 2
NH = 12
LAYERS = 5
G = 4
GROUPS = B // G
STEPS = LAYERS * GROUPS
GT = G * TXT
HD = D // NH
HA = HD + 1
VW = HALF + HD
DH = 64
HID = 768
MH = HID // 128
NT = 2 * S - 1
WIN = S + IMG - 1
ROWS = (IMG, TXT)
OFF = (0, IMG)
KEYS = (128, S - 128)
KOFF = (0, 128)
KR = 32
PK = 100
EPS = 1e-5
ATT_EPS = 1e-9
NEG = -10000.0
FMIN = -3.4028234663852886e38

A_QK, A_COL, A_V = 0, 2 * 2 * D, 2 * 2 * D + 6
A_W = A_V + 2 * D
C_FC, C_COL = 0, 2 * HID
C_W = C_COL + 4
C2_COL = MH * D
C2_W = C2_COL + MH
J_Q, J_K, J_V, J_O, J_IN = 0, 768, 1536, 1728, 2112
J_POS = J_IN + 2 * HID
J_R = J_POS + 2 * NT
J_W = J_R + 2 * 768
K_OUT, K_INB, K_RW, K_RR, K_BK = 0, MH * D, MH * D + 6, MH * D + 12, MH * D + 18
K_W = MH * D + 24
POS_DVE, POS_ACT = (0, 1, 2, 4, 6, 8, 10), (3, 5, 7, 9, 11)
CST_I, CST_CAUSAL, CST_NEG, CST_EVEN, CST_ODD, CST_PW = 0, 128, 128 + TXT, 128 + 2 * TXT, 129 + 2 * TXT, 130 + 2 * TXT
CST_W = CST_PW + 2


class Signal:

    def __init__(self, sem, per):
        self.sem, self.per = sem, per

    def after(self, item, n):
        return item.at(self.per, n)


class Item:

    def __init__(self, engine, base, lag=0, products=None):
        self.engine, self.base, self.lag = engine, base, lag
        self.products = {} if products is None else products

    def minus(self, n):
        return Item(self.engine, self.base, self.lag - n, self.products)

    def at(self, per, n):
        if isinstance(self.base, int):
            return (self.base + self.lag) * per + n
        if per not in self.products:
            self.products[per] = self.engine.snap(self.base * per)
        return self.products[per] + (self.lag * per + n)

    def value(self):
        return self.base + self.lag


def wait(engine, signal, item, n):
    value = item.at(signal.per, n)
    if isinstance(value, int) and value <= 0:
        return
    engine.wait_ge(signal.sem, value)


def early_fusion(nc, patches, ids, pos_ids, mask, tok_emb, pos_emb, w_a, r_a, w_b, r_b, w_c, w_c2, r_c,
                 w_tok, r_joint, w_joint, w_joint128, consts, out, h_text, pos_scratch):
    ctx = ExitStack()
    with ctx:
        def sb(name, shape, dt=F32):
            return ctx.enter_context(nc.sbuf_tensor(name, shape, dt))

        def sig(name, per=1):
            return Signal(ctx.enter_context(nc.semaphore(name)), per)

        bank = [ctx.enter_context(nc.psum_tensor(f"bank{i}", [128, 512], F32)) for i in range(8)]

        cst = sb("cst", [128, CST_W])
        ident = cst[:, CST_I:CST_I + 128]
        power = cst[:, CST_PW:CST_PW + 2]
        wtok = sb("wtok", [PK, 3, D])
        wj = sb("wj", [HALF, J_W])
        wk = sb("wk", [128, K_W])
        rj = sb("rj", [IMG, 7, D])
        v_bias = sb("v_bias", [128, D])
        rel = sb("rel", [128, 6, NT])
        rw8 = sb("rw8", [128, 6])
        rr8 = sb("rr8", [128, 6])

        text_ctx = ExitStack()

        def tb(name, shape, dt=F32):
            return text_ctx.enter_context(nc.sbuf_tensor(name, shape, dt))

        id_sb = tb("id_sb", [TXT, B], I32)
        pid_sb = tb("pid_sb", [TXT, 1], I32)
        emb = tb("emb", [TXT, B, D])
        pos_row = tb("pos_row", [TXT, D])
        ext = tb("ext", [TXT, B, TXT])
        wa = tb("wa", [HALF, A_W])
        wb = tb("wb", [HALF, 2 * D])
        wc = tb("wc", [HALF, C_W])
        wc2 = tb("wc2", [128, C2_W])
        ra = tb("ra", [TXT, 2, D])
        rb = tb("rb", [TXT, 3, D])
        rc = tb("rc", [TXT, 2, D])
        h_tok = tb("h_tok", [TXT, G, D])
        h_res = tb("h_res", [TXT, G, D])
        hT = tb("hT", [HALF, 2, GT])
        q_even = tb("q_even", [HALF, 2, GT])
        q_odd = tb("q_odd", [HALF, 2, GT])
        kT = tb("kT", [HALF, 2, GT])
        v_tok = tb("v_tok", [TXT, G, NH, HA])
        sc = tb("sc", [TXT, G, NH, TXT])
        mx = tb("mx", [TXT, G, NH])
        pT = tb("pT", [TXT, 2, 6 * TXT])
        rden = tb("rden", [TXT, NH])
        att = tb("att", [TXT, D])
        aT = tb("aT", [HALF, 2 * TXT])
        h_bias = tb("h_bias", [TXT, G, D])
        r1 = tb("r1", [TXT, D])
        st1 = tb("st1", [TXT, 6])
        mv1 = tb("mv1", [TXT, 2])
        rs1 = tb("rs1", [TXT, 1])
        x1 = tb("x1", [TXT, G, D])
        nb_tmp = tb("nb_tmp", [TXT, D])
        bias2 = tb("bias2", [TXT, D])
        n_bias = tb("n_bias", [TXT, G, D])
        nT = tb("nT", [HALF, 2, GT])
        gel = tb("gel", [128, MH, GT])
        primer = tb("primer", [1, 1])
        r2 = tb("r2", [TXT, D])
        st2 = tb("st2", [TXT, 6])
        mv2 = tb("mv2", [TXT, 2])
        rs2 = tb("rs2", [TXT, 1])
        x2 = tb("x2", [TXT, D])
        ho_tmp = tb("ho_tmp", [TXT, D])
        h_out = tb("h_out", [TXT, G, D])

        consts_in = sig("consts_in")
        carried = {nc.sync.engine: sig("carried_sp"), nc.vector.engine: sig("carried_dve")}
        ids_in = sig("ids_in")
        mask_in = sig("mask_in")
        pos_row_in = sig("pos_row_in")
        emb_in = [sig(f"emb_in{g}") for g in range(GROUPS)]
        emb_done = sig("emb_done")
        emb_stored = [sig("emb_stored_first"), sig("emb_stored_second"), sig("emb_stored_rest")]
        ones_set = sig("ones_set")
        ext_one = sig("ext_one")
        ext_scaled = sig("ext_scaled")
        ext_ready = sig("ext_ready")
        wa_in, wv_in, wb_in, wc_in, wc2_in = (sig("wa_in", 16), sig("wv_in", 32), sig("wb_in", 32), sig("wc_in", 32),
                                              sig("wc2_in", 32))
        h_in = sig("h_in", 16)
        res_in = [sig(f"res_in{b}", 16) for b in range(G)]
        h_stored = [sig(f"h_stored{b}", 16) for b in range(G)]
        hT_ps, hT_sb = sig("hT_ps", 2), sig("hT_sb", 2)
        qk_ps, q_sb, k_sb = sig("qk_ps", 4), sig("q_sb", 4), sig("k_sb", 2)
        v_ps, v_sb = sig("v_ps", G), sig("v_sb", G)
        s_ps, masked, biased, maxed, shifted, expd = (sig("s_ps", G), sig("masked", 3 * G), sig("biased", G),
                                                      sig("maxed", G), sig("shifted", G), sig("expd", G))
        pT_ps, pT_sb, pv_ps = sig("pT_ps", 2 * G), sig("pT_sb", 2 * G), sig("pv_ps", G)
        rden_ok, att_ok, aT_ps, aT_sb, pj_ps = (sig("rden_ok", G), sig("att_ok", G), sig("aT_ps", G),
                                                sig("aT_sb", G), sig("pj_ps", G))
        hb_ok, r1_ok, st1_ok, mv1_ok, ve1_ok, rs1_ok, x1_ok = (sig("hb_ok", G), sig("r1_ok", G), sig("st1_ok", G),
                                                               sig("mv1_ok", G), sig("ve1_ok", G), sig("rs1_ok", G),
                                                               sig("x1_ok", G))
        bias2_ok, nbt_ok, nb_mid, nb_ok = sig("bias2_ok", 1), sig("nbt_ok", G), sig("nb_mid", G), sig("nb_ok", G)
        nT_ps, nT_sb, fc_ps, gelu_ok, ml_ps = (sig("nT_ps", 2), sig("nT_sb", 4), sig("fc_ps", MH),
                                               sig("gelu_ok", MH), sig("ml_ps", G))
        r2_ok, st2_ok, mv2_ok, ve2_ok, rs2_ok, x2_ok = (sig("r2_ok", G), sig("st2_ok", G), sig("mv2_ok", G),
                                                        sig("ve2_ok", G), sig("rs2_ok", G), sig("x2_ok", G))
        hot_ok, ho_ok = sig("hot_ok", G), sig("ho_ok", G)

        def wait_alone(engine, signal, item, n):
            wait(engine, signal, item, n)
            if not isinstance(item.base, int):
                engine.sem_inc(carried[engine.engine].sem)

        def text_steps(engine, step):
            fixed = lambda t: Item(engine, t)
            step(fixed(0), None, None)
            step(fixed(1), fixed(0), None)
            step(fixed(2), fixed(1), fixed(0))
            with engine.Fori(3, STEPS) as t:
                a = Item(engine, t)
                step(a, a.minus(1), a.minus(2))
            step(None, fixed(STEPS - 1), fixed(STEPS - 2))
            step(None, None, fixed(STEPS - 1))

        def first_step(item):
            return isinstance(item.base, int) and item.value() == 0

        def layer_in(engine, signal, item):
            if isinstance(item.base, int):
                engine.wait_ge(signal.sem, (item.value() // GROUPS + 1) * signal.per)
            else:
                engine.wait_ge(signal.sem, (item.value() >> 3) * signal.per + signal.per)

        def text_over(engine):
            for b in range(G):
                wait(engine, h_stored[b], Item(engine, STEPS - 1), 16)

        text_ctx.close()
        pat = sb("pat", [PK, 2, 3 * IMG])
        e0 = sb("e0", [IMG, D])
        ste = sb("ste", [IMG, 6])
        mve = sb("mve", [IMG, 2])
        rse = sb("rse", [IMG, 1])
        e1 = sb("e1", [IMG, D])
        e2 = sb("e2", [IMG, D])
        hj = sb("hj", [IMG, 2, D])
        hc = sb("hc", [IMG, 2, 2, D])
        stq = sb("stq", [IMG, 2, 6])
        mvq = sb("mvq", [IMG, 2, 2])
        rsq = sb("rsq", [IMG, 2])
        xq = sb("xq", [IMG, 2, D])
        xqb = sb("xqb", [IMG, 2, 2, D])
        xqT = sb("xqT", [HALF, 2, S])
        qc = sb("qc", [128, 2, 6, S])
        qr = sb("qr", [128, 6, S])
        kj = sb("kj", [128, 2, 6, S])
        vj = sb("vj", [128, 2, 2, 6 * VW])
        vk = sb("vk", [3 * KR, 2, 4, HALF])
        pos_out = sb("pos_out", [IMG, 2, NH, WIN])
        pos_in = sb("pos_in", [IMG, 2, NH, S])
        scj = sb("scj", [IMG, 2, NH, S + 1])
        pk = sb("pk", [IMG, 2, NH, KR])
        mxj = sb("mxj", [IMG, 2, NH])
        nmj = sb("nmj", [IMG, 2, NH])
        pTj = sb("pTj", [128, 2, 3 * S])
        pTk = sb("pTk", [3 * KR, 2, S])
        dnj = sb("dnj", [IMG, 2, NH])
        rdj = sb("rdj", [IMG, 2, NH])
        aTj = sb("aTj", [HALF, 2 * S])
        primer_j = sb("primer_j", [1, 1])
        r3 = sb("r3", [IMG, 2, D])
        st3 = sb("st3", [IMG, 2, 6])
        mv3 = sb("mv3", [IMG, 2, 2])
        rs3 = sb("rs3", [IMG, 2])
        x3 = sb("x3", [IMG, 2, D])
        t3 = sb("t3", [IMG, 2, D])
        t4 = sb("t4", [IMG, 2, D])
        h2 = sb("h2", [IMG, 2, 2, D])
        st4 = sb("st4", [IMG, 2, 6])
        mv4 = sb("mv4", [IMG, 2, 2])
        rs4 = sb("rs4", [IMG, 2])
        x4 = sb("x4", [IMG, 2, D])
        x4T = sb("x4T", [HALF, 2, S])
        gj = sb("gj", [128, MH, S])
        yj = sb("yj", [IMG, 2, 2, D])

        jw_in, rel_ps, rel_ok, r8_ok, pads = sig("jw_in"), sig("rel_ps"), sig("rel_ok"), sig("r8_ok"), sig("pads")
        pat_in = [sig(f"pat_in{p}", 16) for p in range(2)]
        ht_in, hc_ok = sig("ht_in", 16), sig("hc_ok", 2)
        e_ps, e0_ok, ste_ok, mve_ok, vee_ok, rse_ok, e1_ok, e2_ok, e3_ok = (
            sig("e_ps"), sig("e0_ok"), sig("ste_ok"), sig("mve_ok"), sig("vee_ok"), sig("rse_ok"),
            sig("e1_ok"), sig("e2_ok"), sig("e3_ok"))
        stq_ok, mvq_ok, veq_ok, rsq_ok, xq_ok, xqb_ok = (sig("stq_ok", 2), sig("mvq_ok", 2), sig("veq_ok"),
                                                         sig("rsq_ok"), sig("xq_ok", 2), sig("xqb_ok", 2))
        xqT_ps, xqT_sb = sig("xqT_ps"), sig("xqT_sb")
        qj_ps, qc_ok, qr_ok, kj_ps, kj_ok = sig("qj_ps", 2), sig("qc_ok", 2), sig("qr_ok", 2), sig("kj_ps", 2), sig("kj_ok", 2)
        vj_ps, vj_ok = sig("vj_ps"), sig("vj_ok", 7)
        pos_ps, pos_dve, pos_act = sig("pos_ps", 12), sig("pos_dve", len(POS_DVE)), sig("pos_act", len(POS_ACT))
        pos_written, pos_back = [sig(f"pos_written{i}", 16) for i in range(2)], [sig(f"pos_back{i}", 16) for i in range(2)]
        sj_ps, sj_sb, nm_ok, ej_ok = sig("sj_ps", 8), sig("sj_sb", 24), sig("nm_ok", 2), sig("ej_ok", 24)
        rdj_ok, pn_ok = sig("rdj_ok", 2), sig("pn_ok", 8)
        ptj_ps, ptj_sb, pvj_ps = sig("ptj_ps", 8), [sig(f"ptj_sb{jt}", 4) for jt in range(2)], sig("pvj_ps", 4)
        atT_sb, wo_ps = sig("atT_sb"), sig("wo_ps")
        r3_ok, st3_ok, mv3_ok, ve3_ok, rs3_ok, x3_ok = (sig("r3_ok", 2), sig("st3_ok", 2), sig("mv3_ok", 2),
                                                        sig("ve3_ok"), sig("rs3_ok"), sig("x3_ok", 2))
        t3_ok, t4_ok, h2_ok = sig("t3_ok", 2), sig("t4_ok", 2), sig("h2_ok", 2)
        st4_ok, mv4_ok, ve4_ok, rs4_ok, x4_ok = sig("st4_ok", 2), sig("mv4_ok", 2), sig("ve4_ok"), sig("rs4_ok"), sig("x4_ok", 2)
        x4T_ps, x4T_sb, fj_ps, gj_ok, mj_ps, yj_ok = (sig("x4T_ps"), sig("x4T_sb"), sig("fj_ps", 2), sig("gj_ok", 6),
                                                      sig("mj_ps"), sig("yj_ok", 2))
        y_stored = [sig(f"y_stored{i}", 32) for i in range(2)]

        def joint_steps(engine, step):
            def fixed_step(u):
                stage = lambda v: Item(engine, v) if 0 <= v < B else None
                step(stage(u + 1), stage(u), stage(u - 1), stage(u - 2), u % 2)

            for u in range(-1, 4):
                fixed_step(u)
            with engine.Fori(2, B // 2 - 1) as pair:
                even = Item(engine, engine.snap(pair * 2))
                for p in range(2):
                    d = even.minus(-p)
                    step(d.minus(-1), d, d.minus(1), d.minus(2), p)
            for u in range(B - 2, B + 2):
                fixed_step(u)

        def pair_wait(engine, signal, item, parity):
            if isinstance(item.base, int):
                u = item.value()
                if u >= 0:
                    engine.wait_ge(signal.sem, (u // 2 + 1) * signal.per)
            else:
                half = signal.per // 2
                engine.wait_ge(signal.sem, item.at(half, signal.per - parity * half))

        def position_copied(engine, d, unit):
            copied, units = (pos_dve, POS_DVE) if unit in POS_DVE else (pos_act, POS_ACT)
            wait(engine, copied, d, units.index(unit) + 1)

        def copy_positions(copy, d, unit, copied):
            it, q4, par = unit // 6, unit % 6 // 2, unit % 2
            copy(pos_out[0:ROWS[it], it, 4 * q4 + par:4 * q4 + 4:2, :],
                 bank[unit % 4][0:ROWS[it], 0:2 * WIN].rearrange("p (h w) -> p h w", h=2)).then_inc(copied.sem, 1)

        def probabilities_t(engine, copy, e, tr, jt):
            wait(engine, ptj_ps, e, 2 * tr + jt + 1)
            if tr >= 2:
                wait(engine, pvj_ps, e, tr - 1)
            else:
                wait(engine, pvj_ps, e.minus(1), tr + 3)
            if jt == 0:
                copy(pTj[:, tr % 2, :], bank[2 * (tr % 2)][:, 0:3 * S]).then_inc(ptj_sb[jt].sem, 1)
            else:
                copy(pTk[:, tr % 2, :], bank[2 * (tr % 2) + 1][0:3 * KR, 0:S]).then_inc(ptj_sb[jt].sem, 1)

        block = ctx.enter_context(nc.Block())

        @block.sync
        def _(sp):
            sp.dma_start(cst[:, :], consts).then_inc(consts_in.sem, 16)
            sp.dma_start(id_sb[:, :], ids).then_inc(ids_in.sem, 16)
            sp.dma_start(pid_sb[:, :], pos_ids).then_inc(ids_in.sem, 16)
            sp.dma_start(ext[:, :, :].rearrange("p b k -> p (b k)"), mask[0:1, :].broadcast_to([TXT, B * TXT])
                         ).then_inc(mask_in.sem, 16)

            def load_qk(l):
                sp.dma_start(wa[:, 0:A_V], w_a[bass.ds(l, 1), :, 0:A_V].rearrange("l p n -> (l p) n")).then_inc(wa_in.sem, 16)

            def load_v(l):
                sp.dma_start(wa[:, A_V:A_W], w_a[bass.ds(l, 1), :, A_V:A_W].rearrange("l p n -> (l p) n")).then_inc(wv_in.sem, 16)
                sp.dma_start(ra[:, :, :].rearrange("p r d -> p (r d)"),
                             r_a[bass.ds(l, 1), :].broadcast_to([TXT, 2 * D])).then_inc(wv_in.sem, 16)

            def load_b(l):
                sp.dma_start(wb[:, :], w_b[bass.ds(l, 1), :, :].rearrange("l p n -> (l p) n")).then_inc(wb_in.sem, 16)
                sp.dma_start(rb[:, :, :].rearrange("p r d -> p (r d)"),
                             r_b[bass.ds(l, 1), :].broadcast_to([TXT, 3 * D])).then_inc(wb_in.sem, 16)

            def load_up(l):
                sp.dma_start(wc[:, :], w_c[bass.ds(l, 1), :, :].rearrange("l p n -> (l p) n")).then_inc(wc_in.sem, 16)
                sp.dma_start(wc2[:, C2_COL:C2_W], w_c2[bass.ds(l, 1), :, C2_COL:C2_W].rearrange("l p n -> (l p) n")
                             ).then_inc(wc_in.sem, 16)

            def load_down(l):
                sp.dma_start(wc2[:, 0:C2_COL], w_c2[bass.ds(l, 1), :, 0:C2_COL].rearrange("l p n -> (l p) n")
                             ).then_inc(wc2_in.sem, 16)
                sp.dma_start(rc[:, :, :].rearrange("p r d -> p (r d)"),
                             r_c[bass.ds(l, 1), :].broadcast_to([TXT, 2 * D])).then_inc(wc2_in.sem, 16)

            def store_embedding(g):
                sp.wait_ge(emb_done.sem, g + 1)
                for b in range(G):
                    sp.dma_start(h_text[g * G + b, :, :], emb[:, g * G + b, :]).then_inc(emb_stored[min(g, 2)].sem, 16)

            def load_h(a, g):
                wait_alone(sp, hT_ps, a.minus(1), 2)
                for b in range(G):
                    if isinstance(a.base, int) and a.value() < GROUPS:
                        early = a.value() < 2
                        sp.wait_ge(emb_stored[min(a.value(), 2)].sem, 16 * G * (1 if early else GROUPS - 2))
                        break
                    wait_alone(sp, h_stored[b], a.minus(GROUPS), 16)
                sp.dma_start(h_tok[:, :, :], h_text[g * G:(g + 1) * G, :, :].rearrange("b t d -> t b d")
                             ).then_inc(h_in.sem, 16)

            def load_res(a, g, b):
                wait_alone(sp, hb_ok, a.minus(1), b + 1)
                sp.dma_start(h_res[:, b, :], h_text[g * G + b, :, :]).then_inc(res_in[b].sem, 16)

            def step(c, c_group, a_next, a_group, reload=None):
                if a_next is not None:
                    load_h(a_next, a_group)
                for b in range(G):
                    if c is not None:
                        wait_alone(sp, ho_ok, c, b + 1)
                        sp.dma_start(h_text[c_group * G + b, :, :], h_out[:, b, :]).then_inc(h_stored[b].sem, 16)
                    if b == 0 and reload is not None:
                        reload()
                    if a_next is not None and b > 0:
                        load_res(a_next, a_group, b - 1)
                if a_next is not None:
                    load_res(a_next, a_group, G - 1)

            def early_reload(t, g, layer):
                def reload():
                    if g == GROUPS - 1:
                        wait_alone(sp, q_sb, t, 4)
                        wait_alone(sp, k_sb, t, 2)
                        load_qk(layer + 1)
                    if g == 1:
                        wait_alone(sp, gelu_ok, t.minus(2), MH)
                        load_up(layer)
                return reload

            def late_reload(t, g, layer):
                if g == GROUPS - 1:
                    wait_alone(sp, v_sb, t, G)
                    wait_alone(sp, hb_ok, t, G)
                    load_v(layer + 1)
                if g == 0:
                    wait_alone(sp, r1_ok, t.minus(1), G)
                    wait_alone(sp, nb_ok, t.minus(1), G)
                    load_b(layer)
                if g == 1:
                    load_down(layer)

            load_qk(0)
            store_embedding(0)
            load_h(Item(sp, 0), 0)
            for b in range(G):
                load_res(Item(sp, 0), 0, b)
            load_v(0)
            load_b(0)
            load_up(0)
            load_down(0)
            store_embedding(1)

            def fixed_step(t, reload=None):
                c = Item(sp, t - 2) if t >= 2 else None
                a_next = Item(sp, t + 1) if t + 1 < STEPS else None
                step(c, (t - 2) % GROUPS, a_next, (t + 1) % GROUPS, reload)

            def load_joint_weights():
                sp.dma_start(wtok[:, :, :], w_tok).then_inc(jw_in.sem, 16)
                sp.dma_start(wj[:, :], w_joint).then_inc(jw_in.sem, 16)
                sp.dma_start(wk[:, :], w_joint128).then_inc(jw_in.sem, 16)
                sp.dma_start(v_bias[:, :], r_joint[0:1, 4 * D:5 * D].broadcast_to([128, D])).then_inc(jw_in.sem, 16)
                sp.dma_start(rj[0:1, 0, :], r_joint[0:1, 0:D]).then_inc(jw_in.sem, 16)
                sp.dma_start(rj[1:IMG, 0, :], r_joint[0:1, D:2 * D].broadcast_to([IMG - 1, D])).then_inc(jw_in.sem, 16)
                sp.dma_start(rj[:, 1:7, :].rearrange("p r d -> p (r d)"),
                             r_joint[0:1, 2 * D:8 * D].broadcast_to([IMG, 6 * D])).then_inc(jw_in.sem, 16)

            for t in range(GROUPS):
                now = Item(sp, t)
                fixed_step(t, early_reload(now, t, 0) if t == GROUPS - 1 else None)
                if t == 0:
                    for g in range(2, GROUPS):
                        store_embedding(g)
                if t == 2:
                    load_joint_weights()
                if t == GROUPS - 1:
                    late_reload(now, t, 0)
            with sp.Fori(1, LAYERS - 1) as layer:
                t0 = Item(sp, sp.snap(layer * GROUPS))
                for g in range(GROUPS):
                    t = t0.minus(-g)
                    step(t.minus(2), (g - 2) % GROUPS, t.minus(-1), (g + 1) % GROUPS, early_reload(t, g, layer))
                    late_reload(t, g, layer)
            for t in range(STEPS - GROUPS, STEPS + 2):
                now, g = Item(sp, t), t - (STEPS - GROUPS)
                fixed_step(t, early_reload(now, g, LAYERS - 1) if g < 2 else None)
                if g < 2:
                    late_reload(now, g, LAYERS - 1)

            text_over(sp)

            def load_patches(u, p):
                wait_alone(sp, e_ps, u.minus(2), 1)
                sp.dma_start(pat[:, p, :], patches[:, bass.ds(u.value(), 1), :].rearrange("k b n -> k (b n)")
                             ).then_inc(pat_in[p].sem, 16)

            load_patches(Item(sp, 0), 0)

            def jstep(n, d, e, f, p):
                if n is not None:
                    wait_alone(sp, hc_ok, n.minus(1), 2)
                    wait_alone(sp, xq_ok, n.minus(1), 2)
                    sp.dma_start(hj[0:TXT, 1, :], h_text[bass.ds(n.value(), 1), :, :].rearrange("b t d -> (b t) d")
                                 ).then_inc(ht_in.sem, 16)
                if n is not None and not (isinstance(n.base, int) and n.value() == B - 1):
                    load_patches(n.minus(-1), p)
                if d is not None:
                    for it in range(2):
                        m = ROWS[it]
                        wait_alone(sp, pos_dve, d, sum(v // 6 <= it for v in POS_DVE))
                        wait_alone(sp, pos_act, d, sum(v // 6 <= it for v in POS_ACT))
                        wait_alone(sp, pos_back[it], d.minus(1), 16)
                        sp.dma_start(pos_scratch[it, 0:m, :], pos_out[0:m, it, :, :].rearrange("p h w -> p (h w)")
                                     ).then_inc(pos_written[it].sem, 16)
                    for it in range(2):
                        m = ROWS[it]
                        wait_alone(sp, pos_written[it], d, 16)
                        wait_alone(sp, sj_sb, d.minus(1), 12 * (it + 1))
                        skew = bass.AP(pos_scratch.tensor, pos_scratch.offset + it * IMG * NH * WIN + m - 1,
                                       [[NH * WIN - 1, m], [WIN, NH], [1, S]])
                        sp.dma_start(pos_in[0:m, it, :, :], skew).then_inc(pos_back[it].sem, 16)
                if f is not None:
                    for it in range(2):
                        wait_alone(sp, yj_ok, f, it + 1)
                        sp.dma_start(out[bass.ds(f.value(), 1), OFF[it]:OFF[it] + ROWS[it], :].rearrange("b t d -> (b t) d"),
                                     yj[0:ROWS[it], p, it, :]).then_inc(y_stored[p].sem, 16)

            joint_steps(sp, jstep)
            for p in range(2):
                sp.wait_ge(y_stored[p].sem, B // 2 * 32)
            for it in range(2):
                sp.wait_ge(pos_back[it].sem, B * 16)

        @block.gpsimd
        def _(pool):
            pool.memset(v_tok[:, :, :, HD:HA], 1.0).then_inc(ones_set.sem, 1)
            pool.wait_ge(ids_in.sem, 32)
            pool.indirect_dma_start(pos_row[:, :], None, pos_emb,
                                    bass.IndirectOffsetOnAxis(pid_sb[:, 0:1].bitcast(U32), 0)).then_inc(pos_row_in.sem, 16)
            for i in range(B):
                pool.indirect_dma_start(emb[:, i, :], None, tok_emb,
                                        bass.IndirectOffsetOnAxis(id_sb[:, i:i + 1].bitcast(U32), 0)
                                        ).then_inc(emb_in[i // G].sem, 16)
            pool.wait_ge(consts_in.sem, 16)

            def rstd(out_, var, n, ready, item, count, done):
                wait(pool, ready, item, count)
                nc.gpsimd.tensor_tensor(out_, var, power[0:out_.shape[0], 0:n], ALU.pow).then_inc(done.sem, 1)

            def step(a, b_, c):
                def first_scale(item, b):
                    if item is not None:
                        wait(pool, x1_ok, item, b)
                        rstd(rs1[:, :], mv1[:, 1:2], 1, ve1_ok, item, b + 1, rs1_ok)

                def residual(item, b):
                    if item is not None:
                        wait(pool, res_in[b], item, 16)
                        wait(pool, r1_ok, item.minus(1), b + 1)
                        nc.gpsimd.tensor_tensor(h_bias[:, b, :], h_res[:, b, :], ra[:, 1, :], ALU.add).then_inc(hb_ok.sem, 1)

                def first_affine(item, b):
                    if item is not None:
                        wait(pool, bias2_ok, item, 1)
                        wait(pool, x1_ok, item, b + 1)
                        wait(pool, nb_ok, item, b)
                        nc.gpsimd.tensor_tensor(nb_tmp[:, :], x1[:, b, :], rb[:, 0, :], ALU.mult).then_inc(nbt_ok.sem, 1)
                        wait(pool, nbt_ok, item, b + 1)
                        wait(pool, r2_ok, item.minus(1), b + 1)
                        nc.gpsimd.tensor_tensor(n_bias[:, b, :], nb_tmp[:, :], bias2[:, :], ALU.add).then_inc(nb_ok.sem, 1)

                def bias(b):
                    if a is not None and not first_step(a):
                        pool.wait_ge(masked.sem, masked.after(a, 3 * (b + 1)))
                        if isinstance(a.base, int):
                            e = ext[:, (a.value() % GROUPS) * G + b, :].unsqueeze(1)
                        else:
                            e = ext[:, bass.ds((a.value() % GROUPS) * G + b, 1), :]
                        nc.gpsimd.tensor_tensor(sc[:, b, :, :], sc[:, b, :, :], e.broadcast_to([TXT, NH, TXT]),
                                                ALU.add).then_inc(biased.sem, 1)

                def second_scale(b):
                    if c is not None:
                        wait(pool, x2_ok, c, b)
                        rstd(rs2[:, :], mv2[:, 1:2], 1, ve2_ok, c, b + 1, rs2_ok)

                def second_affine(b):
                    if c is not None:
                        pool.wait_ge(x2_ok.sem, x2_ok.after(c, b + 1))
                        wait(pool, ho_ok, c, b)
                        nc.gpsimd.tensor_tensor(ho_tmp[:, :], x2[:, :], rc[:, 0, :], ALU.mult).then_inc(hot_ok.sem, 1)
                        pool.wait_ge(hot_ok.sem, hot_ok.after(c, b + 1))
                        wait(pool, h_stored[b], c.minus(1), 16)
                        nc.gpsimd.tensor_tensor(h_out[:, b, :], ho_tmp[:, :], rc[:, 1, :], ALU.add).then_inc(ho_ok.sem, 1)

                first_scale(c, G - 1)
                first_affine(c, G - 1)
                residual(b_, G - 1)
                bias(0)
                if a is not None:
                    layer_in(pool, wv_in, a)
                if b_ is not None:
                    layer_in(pool, wb_in, b_)
                    wait(pool, nb_ok, b_.minus(1), G)
                    nc.gpsimd.tensor_tensor(bias2[:, :], rb[:, 1, :], rb[:, 2, :], ALU.add).then_inc(bias2_ok.sem, 1)
                if c is not None:
                    layer_in(pool, wc2_in, c)
                for b in range(1, G + 1):
                    if b >= 2:
                        first_scale(b_, b - 2)
                        residual(a, b - 2)
                    if b < G:
                        bias(b)
                    second_scale(b - 1)
                    if b >= 2:
                        first_affine(b_, b - 2)
                    second_affine(b - 1)

            text_steps(pool, step)

            text_over(pool)
            for m in (vj[:], vk[:], scj[:, :, :, S:S + 1], mve[:], mvq[:], mv3[:], mv4[:]):
                pool.memset(m, 0.0).then_inc(pads.sem, 1)
            pool.wait_ge(jw_in.sem, 112)
            pool.wait_ge(pads.sem, 7)

            def jstep(n, d, e, f, p):
                if f is not None:
                    rstd(rs3[:, :], mv3[:, :, 1], 2, ve3_ok, f, 1, rs3_ok)
                    for it in range(2):
                        m = ROWS[it]
                        pool.wait_ge(x3_ok.sem, x3_ok.after(f, it + 1))
                        nc.gpsimd.tensor_tensor(t3[0:m, it, :], x3[0:m, it, :], rj[0:m, 5, :], ALU.mult).then_inc(t3_ok.sem, 1)
                    for it in range(2):
                        m = ROWS[it]
                        pool.wait_ge(t3_ok.sem, t3_ok.after(f, it + 1))
                        nc.gpsimd.tensor_tensor(t4[0:m, it, :], t3[0:m, it, :], rj[0:m, 6, :], ALU.add).then_inc(t4_ok.sem, 1)
                    for it in range(2):
                        m = ROWS[it]
                        pool.wait_ge(t4_ok.sem, t4_ok.after(f, it + 1))
                        wait(pool, yj_ok, f.minus(2), 2)
                        nc.gpsimd.tensor_tensor(h2[0:m, p, it, :], t4[0:m, it, :], hc[0:m, p, it, :], ALU.add).then_inc(h2_ok.sem, 1)

                def normalise(it, half):
                    if e is not None:
                        m, hs = ROWS[it], slice(6 * half, 6 * half + 6)
                        pool.wait_ge(rdj_ok.sem, rdj_ok.after(e, it + 1))
                        inverse = rdj[0:m, it, hs].unsqueeze(2)
                        nc.gpsimd.tensor_tensor(scj[0:m, it, hs, 0:128], scj[0:m, it, hs, 0:128],
                                                inverse.broadcast_to([m, 6, 128]), ALU.mult).then_inc(pn_ok.sem, 1)
                        nc.gpsimd.tensor_tensor(pk[0:m, it, hs, :], scj[0:m, it, hs, 128:128 + KR],
                                                inverse.broadcast_to([m, 6, KR]), ALU.mult).then_inc(pn_ok.sem, 1)

                if f is not None:
                    rstd(rs4[:, :], mv4[:, :, 1], 2, ve4_ok, f, 1, rs4_ok)
                normalise(0, 0)
                normalise(0, 1)
                if n is not None:
                    rstd(rse[:, :], mve[:, 1:2], 1, vee_ok, n, 1, rse_ok)
                normalise(1, 0)
                if n is not None:
                    pool.wait_ge(e1_ok.sem, e1_ok.after(n, 1))
                    nc.gpsimd.tensor_tensor(e2[:, :], e1[:, :], rj[:, 1, :], ALU.mult).then_inc(e2_ok.sem, 1)
                    pool.wait_ge(e2_ok.sem, e2_ok.after(n, 1))
                    wait(pool, hc_ok, n.minus(1), 2)
                    wait(pool, xq_ok, n.minus(1), 2)
                    nc.gpsimd.tensor_tensor(hj[:, 0, :], e2[:, :], rj[:, 2, :], ALU.add).then_inc(e3_ok.sem, 1)
                normalise(1, 1)
                if d is not None:
                    for it in range(2):
                        m = ROWS[it]
                        pool.wait_ge(xq_ok.sem, xq_ok.after(d, it + 1))
                        wait(pool, r3_ok, d.minus(2), 2)
                        nc.gpsimd.tensor_tensor(xqb[0:m, p, it, :], xq[0:m, it, :], rj[0:m, 4, :], ALU.add).then_inc(xqb_ok.sem, 1)
                if n is not None:
                    rstd(rsq[:, :], mvq[:, :, 1], 2, veq_ok, n, 1, rsq_ok)

            joint_steps(pool, jstep)

        @block.scalar
        def _(act):
            act.wait_ge(consts_in.sem, 16)

            def step(a, b_, c):
                if a is not None:
                    for pair in range(2):
                        act.wait_ge(hT_ps.sem, hT_ps.after(a, pair + 1))
                        if pair == 0:
                            wait(act, v_ps, a.minus(1), G)
                        nc.scalar.activation(hT[:, :, pair * 2 * TXT:(pair + 1) * 2 * TXT],
                                             bank[pair][0:HALF, 0:4 * TXT].rearrange("p (c t) -> p c t", c=2),
                                             ACT.Identity).then_inc(hT_sb.sem, 1)

                def gelus(m):
                    if c is not None:
                        act.wait_ge(fc_ps.sem, fc_ps.after(c, m + 1))
                        if m == 0:
                            wait(act, ml_ps, c.minus(1), G)
                        nc.scalar.activation(gel[:, m, :], bank[6 + m % 2][:, 0:GT], ACT.Gelu_apprx_tanh,
                                             bias=wc2[:, C2_COL + m:C2_COL + m + 1]).then_inc(gelu_ok.sem, 1)

                def queries(m):
                    if a is not None:
                        act.wait_ge(qk_ps.sem, qk_ps.after(a, 2 * m + 1))
                        if m == 0:
                            wait(act, s_ps, a.minus(1), G)
                        for par, dst in enumerate((q_even, q_odd)):
                            nc.scalar.activation(dst[:, m, :], bank[2 - m][0:HALF, 0:GT], ACT.Identity,
                                                 bias=wa[:, A_COL + 2 * par + m:A_COL + 2 * par + m + 1],
                                                 scale=cst[0:HALF, CST_EVEN + par:CST_EVEN + par + 1]).then_inc(q_sb.sem, 1)

                def attended(item, b):
                    if item is not None:
                        act.wait_ge(aT_ps.sem, aT_ps.after(item, b + 1))
                        wait(act, pj_ps, item, b)
                        nc.scalar.activation(aT[:, :], bank[5][0:HALF, 0:2 * TXT], ACT.Identity).then_inc(aT_sb.sem, 1)

                def probabilities_t(b, half):
                    if b_ is not None:
                        act.wait_ge(pT_ps.sem, pT_ps.after(b_, 2 * b + half + 1))
                        wait(act, pv_ps, b_, b)
                        nc.scalar.activation(pT[:, half, :], bank[3 + half][0:TXT, 0:6 * TXT], ACT.Identity).then_inc(pT_sb.sem, 1)

                def exponents(item, b):
                    if item is not None:
                        act.wait_ge(shifted.sem, shifted.after(item, b + 1))
                        nc.scalar.activation(sc[:, b, :, :], sc[:, b, :, :], ACT.Exp).then_inc(expd.sem, 1)

                attended(c, G - 1)
                probabilities_t(0, 0)
                probabilities_t(0, 1)
                if a is not None:
                    layer_in(act, wa_in, a)
                queries(0)
                exponents(b_, G - 1)
                queries(1)
                if c is not None:
                    nc.scalar.activation(primer[:, :], cst[0:1, 0:1], ACT.Gelu_apprx_tanh)
                    layer_in(act, wc_in, c)
                for m in range(MH):
                    gelus(m)
                for b in range(1, G):
                    exponents(a, b - 1)
                    probabilities_t(b, 0)
                    probabilities_t(b, 1)
                    attended(b_, b - 1)
            text_steps(act, step)

            text_over(act)
            act.wait_ge(jw_in.sem, 112)
            act.wait_ge(r8_ok.sem, 2)

            def exponents(e, it):
                m = ROWS[it]
                act.wait_ge(nm_ok.sem, nm_ok.after(e, it + 1))
                wait(act, rdj_ok, e.minus(1), it + 1)
                for h in range(NH):
                    nc.scalar.activation(scj[0:m, it, h, 0:S], scj[0:m, it, h, 0:S], ACT.Exp, bias=nmj[0:m, it, h:h + 1],
                                         accum_out=dnj[0:m, it, h:h + 1]).then_inc(ej_ok.sem, 1)

            def jstep(n, d, e, f, p):
                if e is not None:
                    nc.scalar.activation(primer_j[:, :], cst[0:1, 0:1], ACT.Exp)
                    exponents(e, 0)
                    exponents(e, 1)
                if d is not None:
                    for unit in POS_ACT:
                        act.wait_ge(pos_ps.sem, pos_ps.after(d, unit + 1))
                        wait(act, pos_written[unit // 6], d.minus(1), 16)
                        copy_positions(lambda dst, src: nc.scalar.activation(dst, src, ACT.Identity), d, unit, pos_act)
                        if unit == POS_ACT[0]:
                            for it in range(2):
                                m = ROWS[it]
                                act.wait_ge(e3_ok.sem, e3_ok.after(d, 1))
                                act.wait_ge(ht_in.sem, ht_in.after(d, 16))
                                wait(act, h2_ok, d.minus(2), 2)
                                nc.scalar.activation(hc[0:m, p, it, :], hj[0:m, it, :], ACT.Identity).then_inc(hc_ok.sem, 1)
                def hidden(half):
                    for t in range(3 * half, 3 * half + 3):
                        act.wait_ge(fj_ps.sem, fj_ps.after(f, t // 3 + 1))
                        if t == 0:
                            wait(act, mj_ps, f.minus(1), 1)
                        nc.scalar.activation(gj[:, t, :], bank[4 + t // 3][:, (t % 3) * S:(t % 3 + 1) * S], ACT.Gelu,
                                             bias=wk[:, K_INB + t:K_INB + t + 1]).then_inc(gj_ok.sem, 1)

                def probabilities(trs):
                    for tr in trs:
                        probabilities_t(act, lambda dst, src: nc.scalar.activation(dst, src, ACT.Identity), e, tr, 0)

                if e is not None:
                    probabilities((0,))
                if f is not None:
                    hidden(0)
                    hidden(1)
                if e is not None:
                    probabilities((1, 2, 3))
                    act.wait_ge(pvj_ps.sem, pvj_ps.after(e, 4))
                    wait(act, wo_ps, e.minus(1), 1)
                    nc.scalar.activation(aTj[:, :], bank[6][0:HALF, 0:2 * S], ACT.Identity).then_inc(atT_sb.sem, 1)
                if n is not None:
                    act.wait_ge(xqT_ps.sem, xqT_ps.after(n, 1))
                    wait(act, vj_ps, n.minus(1), 1)
                    nc.scalar.activation(xqT[:, :, :], bank[5][0:HALF, 0:2 * S].rearrange("p (c t) -> p c t", c=2),
                                         ACT.Identity).then_inc(xqT_sb.sem, 1)

            joint_steps(act, jstep)

        @block.tensor
        def _(pe):
            pe.wait_ge(consts_in.sem, 16)
            mm = nc.tensor.matmul

            def step(a, b_, c):
                def attended_t(item, b):
                    if item is not None:
                        pe.wait_ge(att_ok.sem, att_ok.after(item, b + 1))
                        for k in range(2):
                            last = nc.tensor.transpose(bank[5][0:HALF, k * TXT:(k + 1) * TXT],
                                                       att[:, k * HALF:(k + 1) * HALF], ident[0:TXT, 0:TXT])
                        last.then_inc(aT_ps.sem, 1)

                def project(item, b):
                    pe.wait_ge(aT_sb.sem, aT_sb.after(item, b + 1))
                    for k in range(2):
                        last = mm(bank[6 + (b + 1) % 2][0:TXT, D:2 * D], aT[:, k * TXT:(k + 1) * TXT], wb[:, k * D:(k + 1) * D],
                                  start=(k == 0), stop=(k == 1))
                    last.then_inc(pj_ps.sem, 1)

                def queries_keys(ms):
                    for m in ms:
                        if m == 3:
                            pe.wait_ge(q_sb.sem, q_sb.after(a, 2))
                        col = (m % 2) * D + (m // 2) * HALF
                        for k in range(2):
                            last = mm(bank[(2, 0, 1, 2)[m]][0:HALF, 0:GT], wa[:, k * 2 * D + col:k * 2 * D + col + HALF],
                                      hT[:, k, :], start=(k == 0), stop=(k == 1))
                        last.then_inc(qk_ps.sem, 1)

                def normed_t(pair):
                    if c is not None:
                        pe.wait_ge(x1_ok.sem, x1_ok.after(c, 2 * pair + 2))
                        for k in range(2):
                            for b in range(2 * pair, 2 * pair + 2):
                                col = (2 * k + b % 2) * TXT
                                last = nc.tensor.transpose(bank[7 - pair][0:HALF, col:col + TXT],
                                                           x1[:, b, k * HALF:(k + 1) * HALF], ident[0:TXT, 0:TXT])
                        last.then_inc(nT_ps.sem, 1)

                def scores(b):
                    if a is not None:
                        if b == 0:
                            pe.wait_ge(q_sb.sem, q_sb.after(a, 4))
                            pe.wait_ge(k_sb.sem, k_sb.after(a, 2))
                        else:
                            pe.wait_ge(masked.sem, masked.after(a, 3 * b))
                        for half in range(2):
                            for par, q in enumerate((q_even, q_odd)):
                                for r in range(3):
                                    col = (2 * half + par) * TXT
                                    last = mm(bank[r][0:TXT, col:col + TXT],
                                              q[32 * r:32 * r + 32, half, b * TXT:(b + 1) * TXT],
                                              kT[32 * r:32 * r + 32, half, b * TXT:(b + 1) * TXT],
                                              start=True, stop=True, tile_position=(32 * r, 0))
                        last.then_inc(s_ps.sem, 1)

                def transposes(b):
                    if b_ is not None:
                        pe.wait_ge(expd.sem, expd.after(b_, b + 1))
                        for half in range(2):
                            if b > 0:
                                pe.wait_ge(pT_sb.sem, pT_sb.after(b_, 2 * b - 1 + half))
                            else:
                                wait(pe, pT_sb, b_.minus(1), 2 * G - 1 + half)
                            for i in range(6):
                                last = nc.tensor.transpose(bank[3 + half][0:TXT, i * TXT:(i + 1) * TXT],
                                                           sc[:, b, 6 * half + i, :], ident[0:TXT, 0:TXT])
                            last.then_inc(pT_ps.sem, 1)

                def weighted(b):
                    if b_ is not None:
                        pe.wait_ge(v_sb.sem, v_sb.after(b_, b + 1))
                        pe.wait_ge(pT_sb.sem, pT_sb.after(b_, 2 * b + 2))
                        wait(pe, aT_sb, b_, b)
                        for h in range(NH):
                            last = mm(bank[5][0:TXT, h * HA:(h + 1) * HA], pT[:, h // 6, (h % 6) * TXT:(h % 6 + 1) * TXT],
                                      v_tok[:, b, h, :], start=True, stop=True)
                        last.then_inc(pv_ps.sem, 1)

                def down(b):
                    if c is not None:
                        pe.wait_ge(gelu_ok.sem, gelu_ok.after(c, MH))
                        if b == 0:
                            layer_in(pe, wc2_in, c)
                        if b > 0 and a is not None:
                            pe.wait_ge(v_sb.sem, v_sb.after(a, b))
                        if b > 0 and b_ is not None:
                            pe.wait_ge(r1_ok.sem, r1_ok.after(b_, b))
                        if b >= 2 and a is None and b_ is None:
                            pe.wait_ge(r2_ok.sem, r2_ok.after(c, b - 1))
                        for m in range(MH):
                            last = mm(bank[6 + b % 2][0:TXT, 0:D], gel[:, m, b * TXT:(b + 1) * TXT],
                                      wc2[:, m * D:(m + 1) * D], start=(m == 0), stop=(m == MH - 1))
                        last.then_inc(ml_ps.sem, 1)

                def values_project(b):
                    if c is not None:
                        if b > 0:
                            pe.wait_ge(r2_ok.sem, r2_ok.after(c, b))
                    elif b >= 2:
                        pe.wait_ge(v_sb.sem, v_sb.after(a, b - 1))
                        if b_ is not None:
                            pe.wait_ge(r1_ok.sem, r1_ok.after(b_, b - 1))
                    else:
                        wait(pe, v_sb, a.minus(1), G)
                    if a is not None:
                        if b == 0:
                            layer_in(pe, wv_in, a)
                        for k in range(2):
                            last = mm(bank[6 + (b + 1) % 2][0:TXT, 0:D], hT[:, k, b * TXT:(b + 1) * TXT],
                                      wa[:, A_V + k * D:A_V + (k + 1) * D], start=(k == 0), stop=(k == 1))
                        last.then_inc(v_ps.sem, 1)
                    if b_ is not None and b < G - 1:
                        if b == 0:
                            layer_in(pe, wb_in, b_)
                        project(b_, b)

                if a is not None:
                    pe.wait_ge(h_in.sem, h_in.after(a, 16))
                    wait(pe, masked, a.minus(1), 3 * G)
                    for pair in range(2):
                        for k in range(2):
                            for b in range(2 * pair, 2 * pair + 2):
                                col = (2 * k + b % 2) * TXT
                                last = nc.tensor.transpose(bank[pair][0:HALF, col:col + TXT],
                                                           h_tok[:, b, k * HALF:(k + 1) * HALF], ident[0:TXT, 0:TXT])
                        last.then_inc(hT_ps.sem, 1)
                attended_t(c, G - 1)
                transposes(0)
                if c is not None:
                    if b_ is not None:
                        pe.wait_ge(v_sb.sem, v_sb.after(b_, G))
                    wait(pe, r2_ok, c.minus(1), G - 1)
                    project(c, G - 1)
                if a is not None:
                    layer_in(pe, wa_in, a)
                    pe.wait_ge(hT_sb.sem, hT_sb.after(a, 2))
                    queries_keys(range(4))
                if c is not None:
                    wait(pe, r2_ok, c.minus(1), G)
                    if isinstance(c.base, int) and c.value() == 0:
                        pe.wait_ge(v_sb.sem, v_sb.after(b_, G))
                        pe.wait_ge(r1_ok.sem, r1_ok.after(c, G - 1))
                    normed_t(0)
                    pe.wait_ge(r1_ok.sem, r1_ok.after(c, G))
                    normed_t(1)
                scores(0)
                if c is not None:
                    layer_in(pe, wc_in, c)
                    pe.wait_ge(nT_sb.sem, nT_sb.after(c, 4))
                    for m in range(MH):
                        if m >= 2:
                            pe.wait_ge(gelu_ok.sem, gelu_ok.after(c, m - 1))
                        for k in range(2):
                            last = mm(bank[6 + m % 2][:, 0:GT], wc[:, k * HID + m * 128:k * HID + (m + 1) * 128],
                                      nT[:, k, :], start=(k == 0), stop=(k == 1))
                        last.then_inc(fc_ps.sem, 1)
                for b in range(1, G):
                    scores(b)
                    transposes(b)
                    weighted(b - 1)
                    down(b - 1)
                    attended_t(b_, b - 1)
                    if a is not None or b_ is not None:
                        values_project(b - 1)
                weighted(G - 1)
                if a is not None:
                    values_project(G - 1)
                down(G - 1)

            text_steps(pe, step)

            pe.wait_ge(jw_in.sem, 112)
            for g in ((v_sb, G), (masked, 3 * G), (pT_sb, 2 * G), (r1_ok, G), (r2_ok, G)):
                pe.wait_ge(g[0].sem, g[0].after(Item(pe, STEPS - 1), g[1]))
            for m in range(6):
                if m >= 2:
                    pe.wait_ge(rel_ok.sem, m - 1)
                for k in range(2):
                    last = mm(bank[m % 2][:, 0:NT], wj[:, J_R + k * 768 + m * 128:J_R + k * 768 + (m + 1) * 128],
                              wj[:, J_POS + k * NT:J_POS + (k + 1) * NT], start=(k == 0), stop=(k == 1))
                last.then_inc(rel_ps.sem, 1)
            pe.wait_ge(rel_ok.sem, 6)
            text_over(pe)

            def jstep(n, d, e, f, p):
                def content(it):
                    m = ROWS[it]
                    for i4 in range(4):
                        half, par = i4 // 2, i4 % 2
                        if it == 1:
                            pe.wait_ge(sj_sb.sem, sj_sb.after(e, 3 * i4 + 3))
                        elif f is not None:
                            wait(pe, ptj_sb[i4 % 2], f, 3 + i4 // 2)
                        else:
                            position_copied(pe, e, 8 + i4)
                        for i in range(3):
                            t = 3 * half + i
                            last = mm(bank[i4][0:m, i * S:(i + 1) * S],
                                      qc[64 * par:64 * par + 64, 1 - p, t, OFF[it]:OFF[it] + m],
                                      kj[64 * par:64 * par + 64, 1 - p, t, :],
                                      start=True, stop=True, tile_position=(64 * par, 0))
                        last.then_inc(sj_ps.sem, 1)

                if e is not None:
                    pe.wait_ge(qc_ok.sem, qc_ok.after(e, 2))
                    pe.wait_ge(kj_ok.sem, kj_ok.after(e, 2))
                    content(0)
                    content(1)
                if n is not None:
                    pair_wait(pe, pat_in[1 - p], n, 1 - p)
                    if f is not None:
                        pe.wait_ge(r3_ok.sem, r3_ok.after(f, 2))
                    for k in range(3):
                        last = mm(bank[6][0:IMG, 0:D], pat[:, 1 - p, k * IMG:(k + 1) * IMG], wtok[:, k, :],
                                  start=(k == 0), stop=(k == 2))
                    last.then_inc(e_ps.sem, 1)
                if d is not None:
                    pe.wait_ge(xqT_sb.sem, xqT_sb.after(d, 1))
                    for half in range(2):
                        if e is not None:
                            pe.wait_ge(sj_sb.sem, sj_sb.after(e, 12 + 3 * half + 3))
                        for i in range(3):
                            t = 3 * half + i
                            last = mm(bank[half][:, i * S:(i + 1) * S], wj[:, J_Q + t * 128:J_Q + (t + 1) * 128],
                                      xqT[:, half, :], start=True, stop=True)
                        last.then_inc(qj_ps.sem, 1)
                    for half in range(2):
                        if e is not None:
                            pe.wait_ge(sj_sb.sem, sj_sb.after(e, 18 + 3 * half + 3))
                        for i in range(3):
                            t = 3 * half + i
                            last = mm(bank[2 + half][:, i * S:(i + 1) * S], wj[:, J_K + t * 128:J_K + (t + 1) * 128],
                                      xqT[:, half, :], start=True, stop=True)
                        last.then_inc(kj_ps.sem, 1)
                    if f is not None:
                        wait(pe, gj_ok, f.minus(1), 6)
                    for jt in range(2):
                        m = KEYS[jt]
                        for k in range(2):
                            last = mm(bank[4][0:m, jt * D + k * HALF:jt * D + (k + 1) * HALF],
                                      xqT[:, k, KOFF[jt]:KOFF[jt] + m], wj[:, J_V + k * HALF:J_V + (k + 1) * HALF],
                                      start=True, stop=True)
                    last.then_inc(vj_ps.sem, 1)

                def positions(units):
                    for unit in units:
                        it, q4, par = unit // 6, unit % 6 // 2, unit % 2
                        m = ROWS[it]
                        if unit < 2:
                            pe.wait_ge(qc_ok.sem, qc_ok.after(d, unit + 1))
                            pe.wait_ge(qr_ok.sem, qr_ok.after(d, 2))
                        elif unit < 4:
                            pe.wait_ge(kj_ok.sem, kj_ok.after(d, unit - 1))
                        else:
                            position_copied(pe, d, unit - 4)
                        first = (S - 1) - (OFF[it] + m - 1)
                        w = S + m - 1
                        for i in range(2):
                            t = 2 * q4 + i
                            last = mm(bank[unit % 4][0:m, i * WIN:i * WIN + w],
                                      qr[64 * par:64 * par + 64, t, OFF[it]:OFF[it] + m],
                                      rel[64 * par:64 * par + 64, t, first:first + w],
                                      start=True, stop=True, tile_position=(64 * par, 0))
                        last.then_inc(pos_ps.sem, 1)

                def triple(tr):
                    if tr == 0 or tr == 2:
                        pe.wait_ge(pn_ok.sem, pn_ok.after(e, 6 + tr))
                    for jt in range(2):
                        if tr >= 2:
                            pe.wait_ge(ptj_sb[jt].sem, ptj_sb[jt].after(e, tr - 1))
                        elif d is not None:
                            position_copied(pe, d, 8 + 2 * tr + jt)
                        for it in range(2):
                            m = ROWS[it]
                            if jt == 0:
                                for i in range(3):
                                    last = nc.tensor.transpose(bank[2 * (tr % 2)][:, i * S + OFF[it]:i * S + OFF[it] + m],
                                                               scj[0:m, it, 3 * tr + i, 0:128], ident[0:m, 0:m])
                            else:
                                last = nc.tensor.transpose(bank[2 * (tr % 2) + 1][0:3 * KR, OFF[it]:OFF[it] + m],
                                                           pk[0:m, it, 3 * tr:3 * tr + 3, :].rearrange("p h k -> p (h k)"), ident[0:m, 0:m])
                        last.then_inc(ptj_ps.sem, 1)

                if d is not None:
                    positions(range(12))
                if f is not None:
                    for it in range(2):
                        pe.wait_ge(x4_ok.sem, x4_ok.after(f, it + 1))
                    wait(pe, yj_ok, f.minus(1), 2)
                    for it in range(2):
                        m = ROWS[it]
                        for k in range(2):
                            last = nc.tensor.transpose(bank[7][0:HALF, k * S + OFF[it]:k * S + OFF[it] + m],
                                                       x4[0:m, it, k * HALF:(k + 1) * HALF], ident[0:m, 0:m])
                    last.then_inc(x4T_ps.sem, 1)
                if e is not None:
                    triple(0)
                if f is not None:
                    pe.wait_ge(x4T_sb.sem, x4T_sb.after(f, 1))
                    if d is not None:
                        pe.wait_ge(vj_ok.sem, vj_ok.after(d, 7))

                def hidden(half):
                    if f is not None:
                        for i in range(3):
                            t = 3 * half + i
                            for k in range(2):
                                last = mm(bank[4 + half][:, i * S:(i + 1) * S],
                                          wj[:, J_IN + k * HID + t * 128:J_IN + k * HID + (t + 1) * 128],
                                          x4T[:, k, :], start=(k == 0), stop=(k == 1))
                        last.then_inc(fj_ps.sem, 1)

                def weighted(tr):
                    for jt in range(2):
                        pe.wait_ge(ptj_sb[jt].sem, ptj_sb[jt].after(e, tr + 1))
                    if tr == 0:
                        pe.wait_ge(vj_ok.sem, vj_ok.after(e, 7))
                        if n is not None:
                            pe.wait_ge(e0_ok.sem, e0_ok.after(n, 1))
                        elif f is not None:
                            pe.wait_ge(r3_ok.sem, r3_ok.after(f, 2))
                    half = tr // 2
                    out_t = bank[6][0:HALF, half * S:(half + 1) * S]
                    for i in range(3):
                        h = 3 * (tr % 2) + i
                        mm(out_t, vj[:, 1 - p, half, h * HALF:(h + 1) * HALF], pTj[:, tr % 2, i * S:(i + 1) * S],
                           start=(h == 0), stop=False)
                    last = mm(out_t, vk[:, 1 - p, tr, :], pTk[:, tr % 2, :], start=False, stop=(tr % 2 == 1))
                    last.then_inc(pvj_ps.sem, 1)

                hidden(0)
                hidden(1)
                if e is not None:
                    for tr in range(1, 4):
                        triple(tr)
                        weighted(tr - 1)
                    weighted(3)
                if f is not None:
                    pe.wait_ge(gj_ok.sem, gj_ok.after(f, 6))
                    for it in range(2):
                        m = ROWS[it]
                        for t in range(MH):
                            last = mm(bank[7][0:m, it * D:(it + 1) * D], gj[:, t, OFF[it]:OFF[it] + m],
                                      wk[:, K_OUT + t * D:K_OUT + (t + 1) * D], start=(t == 0), stop=(t == MH - 1))
                    last.then_inc(mj_ps.sem, 1)
                if n is not None:
                    for it in range(2):
                        pe.wait_ge(xq_ok.sem, xq_ok.after(n, it + 1))
                    for it in range(2):
                        m = ROWS[it]
                        for k in range(2):
                            last = nc.tensor.transpose(bank[5][0:HALF, k * S + OFF[it]:k * S + OFF[it] + m],
                                                       xq[0:m, it, k * HALF:(k + 1) * HALF], ident[0:m, 0:m])
                    last.then_inc(xqT_ps.sem, 1)
                if e is not None:
                    pe.wait_ge(atT_sb.sem, atT_sb.after(e, 1))
                    for it in range(2):
                        m = ROWS[it]
                        for k in range(2):
                            last = mm(bank[6][0:m, it * D:(it + 1) * D], aTj[:, k * S + OFF[it]:k * S + OFF[it] + m],
                                      wj[:, J_O + k * D:J_O + (k + 1) * D], start=(k == 0), stop=(k == 1))
                    last.then_inc(wo_ps.sem, 1)

            joint_steps(pe, jstep)

        @block.vector
        def _(dve):
            V = nc.vector
            def embed(g):
                dve.wait_ge(emb_in[g].sem, 16 * G)
                V.tensor_tensor(emb[:, g * G:(g + 1) * G, :], emb[:, g * G:(g + 1) * G, :],
                                pos_row[:, :].unsqueeze(1).broadcast_to([TXT, G, D]), ALU.add).then_inc(emb_done.sem, 1)

            dve.wait_ge(pos_row_in.sem, 16)
            embed(0)
            dve.wait_ge(mask_in.sem, 16)
            dve.wait_ge(consts_in.sem, 16)
            flat = ext[:, :, :].rearrange("p b k -> p (b k)")
            V.tensor_scalar(flat, flat, -1.0, 1.0, ALU.mult, ALU.add).then_inc(ext_one.sem, 1)
            dve.wait_ge(ext_one.sem, 1)
            V.tensor_scalar(flat, flat, FMIN, None, ALU.mult).then_inc(ext_scaled.sem, 1)
            dve.wait_ge(ext_scaled.sem, 1)
            neg = cst[0:TXT, CST_NEG:CST_NEG + TXT].unsqueeze(1).broadcast_to([TXT, G, TXT])
            for g in range(B // G):
                V.tensor_tensor(ext[:, g * G:(g + 1) * G, :], ext[:, g * G:(g + 1) * G, :], neg, ALU.add).then_inc(ext_ready.sem, 1)

            def step(a, b_, c):
                def keys(m):
                    if a is not None:
                        dve.wait_ge(qk_ps.sem, qk_ps.after(a, 2 * m + 2))
                        if m == 0:
                            wait(dve, s_ps, a.minus(1), G)
                        V.tensor_scalar(kT[:, m, :], bank[(0, 2)[m]][0:HALF, 0:GT],
                                        wa[:, A_COL + 4 + m:A_COL + 5 + m], HD ** -0.5, ALU.add, ALU.mult).then_inc(k_sb.sem, 1)

                def normed_t(pair):
                    dve.wait_ge(nT_ps.sem, nT_ps.after(c, pair + 1))
                    if pair == 0:
                        wait(dve, fc_ps, c.minus(1), MH)
                    for k in range(2):
                        V.tensor_scalar(nT[:, k, pair * 2 * TXT:(pair + 1) * 2 * TXT],
                                        bank[7 - pair][0:HALF, 2 * k * TXT:(2 * k + 2) * TXT],
                                        wc[:, C_COL + k:C_COL + k + 1], wc[:, C_COL + 2 + k:C_COL + 3 + k],
                                        ALU.mult, ALU.add).then_inc(nT_sb.sem, 1)

                def first_norm_stats(item, b):
                    dve.wait_ge(pj_ps.sem, pj_ps.after(item, b + 1))
                    wait(dve, x1_ok, item, b)
                    dve.wait_ge(hb_ok.sem, hb_ok.after(item, b + 1))
                    V.tensor_tensor(r1[:, :], bank[6 + (b + 1) % 2][0:TXT, D:2 * D], h_bias[:, b, :], ALU.add).then_inc(r1_ok.sem, 1)
                    wait(dve, r1_ok, item, b + 1)
                    V.bn_stats(st1[:, :], r1[:, :]).then_inc(st1_ok.sem, 1)
                    wait_alone(dve, st1_ok, item, b + 1)
                    V.bn_aggr(mv1[:, :], st1[:, :]).then_inc(mv1_ok.sem, 1)
                    wait(dve, mv1_ok, item, b + 1)
                    V.tensor_scalar(mv1[:, 1:2], mv1[:, 1:2], EPS, None, ALU.add).then_inc(ve1_ok.sem, 1)

                def first_norm(item, b):
                    wait(dve, rs1_ok, item, b + 1)
                    wait(dve, nT_ps, item.minus(1), b // 2 + 1)
                    wait(dve, nb_ok, item.minus(1), b + 1)
                    V.tensor_scalar(x1[:, b, :], r1[:, :], mv1[:, 0:1], rs1[:, 0:1], ALU.subtract, ALU.mult).then_inc(x1_ok.sem, 1)

                def mask(b):
                    dve.wait_ge(s_ps.sem, s_ps.after(a, b + 1))
                    if b_ is not None:
                        dve.wait_ge(pT_ps.sem, pT_ps.after(b_, 2 * b + 2))
                    for r in range(3):
                        dst = sc[:, b, :, :].rearrange("p (half r par) k -> p half r par k", half=2, r=3)[:, :, r]
                        src = bank[r][0:TXT, 0:4 * TXT].rearrange("p (half par k) -> p half par k", half=2, par=2)
                        msk = cst[0:TXT, CST_CAUSAL:CST_CAUSAL + TXT].unsqueeze(1).unsqueeze(1).broadcast_to([TXT, 2, 2, TXT])
                        V.tensor_tensor(dst, src, msk, ALU.mult).then_inc(masked.sem, 1)

                def bias(b):
                    dve.wait_ge(masked.sem, masked.after(a, 3 * (b + 1)))
                    dve.wait_ge(ext_ready.sem, B // G)
                    V.tensor_tensor(sc[:, b, :, :], sc[:, b, :, :], ext[:, b, :].unsqueeze(1).broadcast_to([TXT, NH, TXT]),
                                    ALU.add).then_inc(biased.sem, 1)

                def shift(b):
                    dve.wait_ge(biased.sem, biased.after(a, b + 1))
                    V.tensor_reduce(mx[:, b, :], sc[:, b, :, :], AX.X, ALU.max).then_inc(maxed.sem, 1)
                    dve.wait_ge(maxed.sem, maxed.after(a, b + 1))
                    V.tensor_tensor(sc[:, b, :, :], sc[:, b, :, :], mx[:, b, :].unsqueeze(2).broadcast_to([TXT, NH, TXT]),
                                    ALU.subtract).then_inc(shifted.sem, 1)

                def second_norm_stats(b):
                    dve.wait_ge(ml_ps.sem, ml_ps.after(c, b + 1))
                    wait(dve, x2_ok, c, b)
                    dve.wait_ge(nb_ok.sem, nb_ok.after(c, b + 1))
                    V.tensor_tensor(r2[:, :], bank[6 + b % 2][0:TXT, 0:D], n_bias[:, b, :], ALU.add).then_inc(r2_ok.sem, 1)
                    dve.wait_ge(r2_ok.sem, r2_ok.after(c, b + 1))
                    V.bn_stats(st2[:, :], r2[:, :]).then_inc(st2_ok.sem, 1)
                    wait_alone(dve, st2_ok, c, b + 1)
                    V.bn_aggr(mv2[:, :], st2[:, :]).then_inc(mv2_ok.sem, 1)
                    dve.wait_ge(mv2_ok.sem, mv2_ok.after(c, b + 1))
                    V.tensor_scalar(mv2[:, 1:2], mv2[:, 1:2], EPS, None, ALU.add).then_inc(ve2_ok.sem, 1)

                def second_norm(b):
                    dve.wait_ge(rs2_ok.sem, rs2_ok.after(c, b + 1))
                    wait(dve, hot_ok, c, b)
                    V.tensor_scalar(x2[:, :], r2[:, :], mv2[:, 0:1], rs2[:, 0:1], ALU.subtract, ALU.mult).then_inc(x2_ok.sem, 1)

                def attend(b):
                    dve.wait_ge(pv_ps.sem, pv_ps.after(b_, b + 1))
                    pv = bank[5][0:TXT, 0:NH * HA].rearrange("p (h e) -> p h e", h=NH)
                    V.reciprocal(rden[:, :], pv[:, :, HD]).then_inc(rden_ok.sem, 1)
                    dve.wait_ge(rden_ok.sem, rden_ok.after(b_, b + 1))
                    wait(dve, aT_ps, b_, b)
                    V.tensor_tensor(att[:, :].rearrange("p (h e) -> p h e", h=NH), pv[:, :, 0:HD],
                                    rden[:, :].unsqueeze(2).broadcast_to([TXT, NH, HD]), ALU.mult).then_inc(att_ok.sem, 1)

                def value(b):
                    dve.wait_ge(v_ps.sem, v_ps.after(a, b + 1))
                    if b_ is not None:
                        dve.wait_ge(pv_ps.sem, pv_ps.after(b_, b + 1))
                        if b < G - 1:
                            dve.wait_ge(pj_ps.sem, pj_ps.after(b_, b + 1))
                    V.tensor_tensor(v_tok[:, b, :, 0:HD], bank[6 + (b + 1) % 2][0:TXT, 0:D].rearrange("p (h e) -> p h e", h=NH),
                                    ra[:, 0, :].rearrange("p (h e) -> p h e", h=NH), ALU.add).then_inc(v_sb.sem, 1)

                if a is not None:
                    layer_in(dve, wa_in, a)
                if c is not None:
                    first_norm_stats(c, G - 1)
                keys(0)
                if c is not None:
                    first_norm(c, G - 1)
                keys(1)
                if c is not None:
                    layer_in(dve, wc_in, c)
                    normed_t(0)
                    normed_t(1)
                if a is not None:
                    mask(0)
                    if first_step(a):
                        embed(1)
                        bias(0)
                    shift(0)
                    layer_in(dve, wv_in, a)
                for b in range(1, G + 1):
                    if b_ is not None and b == G:
                        attend(b - 1)
                    if a is not None and b == G:
                        value(b - 1)
                        shift(b - 1)
                    if a is not None and 2 <= b < G:
                        shift(b - 1)
                    if b_ is not None and b < G:
                        attend(b - 1)
                    if a is not None and b < G:
                        mask(b)
                        if first_step(a):
                            bias(b)
                            embed(2 * b)
                            embed(2 * b + 1)
                    if b_ is not None and b >= 2:
                        first_norm(b_, b - 2)
                    if c is not None:
                        second_norm_stats(b - 1)
                    if a is not None and b < G:
                        value(b - 1)
                    if b_ is not None and b < G:
                        first_norm_stats(b_, b - 1)
                    if c is not None:
                        second_norm(b - 1)

            dve.wait_ge(ones_set.sem, 1)
            text_steps(dve, step)

            dve.wait_ge(jw_in.sem, 112)
            V.tensor_scalar(rw8[:, :], wk[:, K_RW:K_RW + 6], DH ** -0.5, None, ALU.mult).then_inc(r8_ok.sem, 1)
            V.tensor_scalar(rr8[:, :], wk[:, K_RR:K_RR + 6], DH ** -0.5, None, ALU.mult).then_inc(r8_ok.sem, 1)
            dve.wait_ge(r8_ok.sem, 2)
            for m in range(6):
                dve.wait_ge(rel_ps.sem, m + 1)
                V.tensor_copy(rel[:, m, :], bank[m % 2][:, 0:NT]).then_inc(rel_ok.sem, 1)
            text_over(dve)
            dve.wait_ge(pads.sem, 7)

            def norm_stats(src, stats, mv, stats_ok, mv_ok, ve_ok, item, eps, ready):
                for it in range(2):
                    n = ROWS[it]
                    ready(it)
                    V.bn_stats(stats[0:n, it, :], src[0:n, it, :]).then_inc(stats_ok.sem, 1)
                for it in range(2):
                    n = ROWS[it]
                    wait_alone(dve, stats_ok, item, it + 1)
                    V.bn_aggr(mv[0:n, it, :], stats[0:n, it, :]).then_inc(mv_ok.sem, 1)
                wait(dve, mv_ok, item, 2)
                V.tensor_scalar(mv[:, :, 1], mv[:, :, 1], eps, None, ALU.add).then_inc(ve_ok.sem, 1)

            def jstep(n, d, e, f, p):
                def add_positions(it):
                    m = ROWS[it]
                    wait_alone(dve, pos_back[it], e, 16)
                    wait_alone(dve, ptj_ps, e.minus(1), 8)
                    for i4 in range(4):
                        half, par = i4 // 2, i4 % 2
                        wait_alone(dve, sj_ps, e, 4 * it + i4 + 1)
                        for i in range(3):
                            h = 6 * half + 2 * i + par
                            V.tensor_tensor_reduce(scj[0:m, it, h, 0:S], bank[i4][0:m, i * S:(i + 1) * S],
                                                   pos_in[0:m, it, h, :], 1.0, FMIN, ALU.add, ALU.max,
                                                   mxj[0:m, it, h:h + 1]).then_inc(sj_sb.sem, 1)
                    dve.wait_ge(sj_sb.sem, sj_sb.after(e, 12 * (it + 1)))
                    V.tensor_scalar(nmj[0:m, it, :], mxj[0:m, it, :], -1.0, None, ALU.mult).then_inc(nm_ok.sem, 1)

                def positions(*units):
                    if d is not None:
                        for unit in units:
                            dve.wait_ge(pos_ps.sem, pos_ps.after(d, unit + 1))
                            wait(dve, pos_written[unit // 6], d.minus(1), 16)
                            copy_positions(V.tensor_copy, d, unit, pos_dve)

                def inverse_sums(it):
                    m = ROWS[it]
                    dve.wait_ge(ej_ok.sem, ej_ok.after(e, 12 * (it + 1)))
                    wait(dve, pn_ok, e.minus(1), 8)
                    V.reciprocal(rdj[0:m, it, :], dnj[0:m, it, :]).then_inc(rdj_ok.sem, 1)

                if f is not None:
                    dve.wait_ge(wo_ps.sem, wo_ps.after(f, 1))
                    wait(dve, x3_ok, f.minus(1), 2)
                    dve.wait_ge(xqb_ok.sem, xqb_ok.after(f, 2))
                    for it in range(2):
                        m = ROWS[it]
                        V.tensor_tensor(r3[0:m, it, :], bank[6][0:m, it * D:(it + 1) * D], xqb[0:m, p, it, :], ALU.add).then_inc(r3_ok.sem, 1)
                if e is not None:
                    add_positions(0)
                if f is not None:
                    norm_stats(r3, st3, mv3, st3_ok, mv3_ok, ve3_ok, f, ATT_EPS, lambda it: wait(dve, r3_ok, f, it + 1))
                if e is not None:
                    add_positions(1)
                if f is not None:
                    dve.wait_ge(rs3_ok.sem, rs3_ok.after(f, 1))
                    wait(dve, t3_ok, f.minus(1), 2)
                    for it in range(2):
                        m = ROWS[it]
                        V.tensor_scalar(x3[0:m, it, :], r3[0:m, it, :], mv3[0:m, it, 0:1], rs3[0:m, it:it + 1],
                                        ALU.subtract, ALU.mult).then_inc(x3_ok.sem, 1)
                if d is not None:
                    wait(dve, pos_ps, d.minus(1), 12)
                    q_half = [(bank[half][:, 0:3 * S].rearrange("p (m t) -> p m t", m=3), slice(3 * half, 3 * half + 3))
                              for half in range(2)]
                    for half, (src, ms) in enumerate(q_half):
                        dve.wait_ge(qj_ps.sem, qj_ps.after(d, half + 1))
                        V.scalar_tensor_tensor(qr[:, ms, :], src, DH ** -0.5, rr8[:, ms].unsqueeze(2).broadcast_to([128, 3, S]),
                                               ALU.mult, ALU.add).then_inc(qr_ok.sem, 1)
                    for src, ms in q_half:
                        V.scalar_tensor_tensor(qc[:, p, ms, :], src, DH ** -0.5, rw8[:, ms].unsqueeze(2).broadcast_to([128, 3, S]),
                                               ALU.mult, ALU.add).then_inc(qc_ok.sem, 1)
                    for half in range(2):
                        dve.wait_ge(kj_ps.sem, kj_ps.after(d, half + 1))
                        src = bank[2 + half][:, 0:3 * S].rearrange("p (m t) -> p m t", m=3)
                        ms = slice(3 * half, 3 * half + 3)
                        V.tensor_tensor(kj[:, p, ms, :], src, wk[:, K_BK + 3 * half:K_BK + 3 * half + 3].unsqueeze(2).broadcast_to([128, 3, S]),
                                        ALU.add).then_inc(kj_ok.sem, 1)
                if e is not None:
                    inverse_sums(0)
                positions(0)
                if f is not None:
                    norm_stats(h2[:, p], st4, mv4, st4_ok, mv4_ok, ve4_ok, f, EPS, lambda it: wait(dve, h2_ok, f, it + 1))
                positions(1, 2)
                if d is not None:
                    dve.wait_ge(vj_ps.sem, vj_ps.after(d, 1))
                    V.tensor_tensor(vj[:, p, :, :].rearrange("p g (h c) -> p g h c", h=6)[:, :, :, 0:HD],
                                    bank[4][:, 0:D].rearrange("p (g h e) -> p g h e", g=2, h=6),
                                    v_bias[:, :].rearrange("p (g h e) -> p g h e", g=2, h=6), ALU.add).then_inc(vj_ok.sem, 1)
                    for i in range(3):
                        m = KEYS[1]
                        for t in range(2):
                            h = 3 * t + i
                            V.tensor_tensor(vk[KR * i:KR * i + m, p, t:4:2, h * HD:(h + 1) * HD],
                                            bank[4][0:m, D:2 * D].rearrange("p (g f) -> p g f", g=2)[:, :, h * HD:(h + 1) * HD],
                                            v_bias[0:m, :].rearrange("p (g f) -> p g f", g=2)[:, :, h * HD:(h + 1) * HD],
                                            ALU.add).then_inc(vj_ok.sem, 1)
                positions(4)
                if n is not None:
                    dve.wait_ge(e_ps.sem, e_ps.after(n, 1))
                    wait(dve, e1_ok, n.minus(1), 1)
                    V.tensor_tensor(e0[:, :], bank[6][0:IMG, 0:D], rj[:, 0, :], ALU.add).then_inc(e0_ok.sem, 1)
                    dve.wait_ge(e0_ok.sem, e0_ok.after(n, 1))
                    V.bn_stats(ste[:, :], e0[:, :]).then_inc(ste_ok.sem, 1)
                    wait_alone(dve, ste_ok, n, 1)
                    V.bn_aggr(mve[:, :], ste[:, :]).then_inc(mve_ok.sem, 1)
                    dve.wait_ge(mve_ok.sem, mve_ok.after(n, 1))
                    V.tensor_scalar(mve[:, 1:2], mve[:, 1:2], EPS, None, ALU.add).then_inc(vee_ok.sem, 1)

                if e is not None:
                    inverse_sums(1)
                positions(6)
                if f is not None:
                    dve.wait_ge(rs4_ok.sem, rs4_ok.after(f, 1))
                    wait(dve, x4T_ps, f.minus(1), 1)
                    for it in range(2):
                        m = ROWS[it]
                        V.tensor_scalar(x4[0:m, it, :], h2[0:m, p, it, :], mv4[0:m, it, 0:1], rs4[0:m, it:it + 1],
                                        ALU.subtract, ALU.mult).then_inc(x4_ok.sem, 1)
                if n is not None:
                    dve.wait_ge(rse_ok.sem, rse_ok.after(n, 1))
                    wait(dve, e2_ok, n.minus(1), 1)
                    V.tensor_scalar(e1[:, :], e0[:, :], mve[:, 0:1], rse[:, 0:1], ALU.subtract, ALU.mult).then_inc(e1_ok.sem, 1)
                positions(8, 10)
                if f is not None:
                    dve.wait_ge(x4T_ps.sem, x4T_ps.after(f, 1))
                    V.tensor_copy(x4T[:, :, :], bank[7][0:HALF, 0:2 * S].rearrange("p (c t) -> p c t", c=2)).then_inc(x4T_sb.sem, 1)
                if e is not None:
                    probabilities_t(dve, V.tensor_copy, e, 0, 1)
                if n is not None:
                    norm_stats(hj, stq, mvq, stq_ok, mvq_ok, veq_ok, n, EPS,
                               lambda it: wait(dve, (e3_ok, ht_in)[it], n, (1, 16)[it]))
                if e is not None:
                    for tr in range(1, 3):
                        probabilities_t(dve, V.tensor_copy, e, tr, 1)
                if n is not None:
                    dve.wait_ge(rsq_ok.sem, rsq_ok.after(n, 1))
                    wait(dve, xqT_ps, n.minus(1), 1)
                    wait(dve, xqb_ok, n.minus(1), 2)
                    for it in range(2):
                        m = ROWS[it]
                        V.tensor_scalar(xq[0:m, it, :], hj[0:m, it, :], mvq[0:m, it, 0:1], rsq[0:m, it:it + 1],
                                        ALU.subtract, ALU.mult).then_inc(xq_ok.sem, 1)
                if e is not None:
                    probabilities_t(dve, V.tensor_copy, e, 3, 1)
                if f is not None:
                    dve.wait_ge(mj_ps.sem, mj_ps.after(f, 1))
                    pair_wait(dve, y_stored[p], f.minus(2), p)
                    for it in range(2):
                        m = ROWS[it]
                        V.tensor_tensor(yj[0:m, p, it, :], bank[7][0:m, it * D:(it + 1) * D], h2[0:m, p, it, :], ALU.add).then_inc(yj_ok.sem, 1)

            joint_steps(dve, jstep)


def kernel(**inputs):
    import numpy as np
    import concourse.bacc as bacc
    from concourse.bass_utils import run_bass_kernel_spmd

    x = {k: np.asarray(v) for k, v in inputs.items()}

    def chunks(w):
        return np.concatenate([w[0:HALF], w[HALF:D]], axis=1)

    def columns(vec, rows):
        return vec.reshape(-1, rows).T

    img = x["x"][:, :, :90, :90].reshape(B, 3, 9, 10, 9, 10)
    patches = np.zeros((PK, B, 3, IMG), np.float32)
    patches[:, :, :, 1:] = img.transpose(3, 5, 0, 1, 2, 4).reshape(PK, B, 3, 81)

    wa, ra, wb, rb, wc, wc2, rc = [], [], [], [], [], [], []
    for l in range(LAYERS):
        w, bias = x["L0_txt_c_attn_w"][l], x["L0_txt_c_attn_b"][l]
        q_cols = columns(bias[0:D], HALF)
        even = np.zeros((HALF, 2), np.float32)
        odd = np.zeros((HALF, 2), np.float32)
        is_even = (np.arange(HALF) // HD) % 2 == 0
        even[is_even] = q_cols[is_even]
        odd[~is_even] = q_cols[~is_even]
        wa.append(np.concatenate([chunks(w[:, 0:2 * D]), even, odd, columns(bias[D:2 * D], HALF), chunks(w[:, 2 * D:])], axis=1))
        ra.append(np.concatenate([bias[2 * D:], x["L0_txt_c_proj_b"][l]]))
        wb.append(chunks(x["L0_txt_c_proj_w"][l]))
        rb.append(np.concatenate([x["L0_txt_ln1_w"][l], x["L0_txt_ln1_b"][l], x["L0_txt_mlp_proj_b"][l]]))
        wc.append(np.concatenate([chunks(x["L0_txt_c_fc_w"][l]), columns(x["L0_txt_ln1_w"][l], HALF),
                                  columns(x["L0_txt_ln1_b"][l], HALF)], axis=1))
        wc2.append(np.concatenate([x["L0_txt_mlp_proj_w"][l].reshape(MH, 128, D).transpose(1, 0, 2).reshape(128, MH * D),
                                   columns(x["L0_txt_c_fc_b"][l], 128)], axis=1))
        rc.append(np.concatenate([x["L0_txt_ln2_w"][l], x["L0_txt_ln2_b"][l]]))

    def block_diagonal(w):
        n = w.shape[2]
        out = np.zeros((HALF, 2, 2, n), np.float32)
        for g in range(4):
            out[48 * (g % 2):48 * (g % 2) + 48, g // 2, g % 2] = w[g]
        return out.reshape(HALF, 4 * n)

    w_joint = np.concatenate([
        block_diagonal(x["L0_attn_Wq"]), block_diagonal(x["L0_attn_Wk"]), block_diagonal(x["L0_attn_Wv"]),
        chunks(x["L0_attn_Wo"]), chunks(x["L0_ffn_in_weight"].T),
        chunks(x["L0_attn_position_embeds"][1:NT + 1].T), chunks(x["L0_attn_r_kernel"].reshape(D, 768))], axis=1)
    w_joint128 = np.concatenate([
        x["L0_ffn_out_weight"].reshape(MH, 128, D).transpose(1, 0, 2).reshape(128, MH * D),
        columns(x["L0_ffn_in_bias"], 128), columns(x["L0_attn_r_w_bias"].reshape(-1), 128),
        columns(x["L0_attn_r_r_bias"].reshape(-1), 128), columns(x["L0_attn_bk"], 128)], axis=1)
    r_joint = np.concatenate([x["L0_tok_cls"].reshape(-1), x["L0_tok_b"], x["L0_tok_gamma"], x["L0_tok_beta"],
                              x["L0_attn_bv"], x["L0_attn_bo"], x["L0_attn_gamma"], x["L0_attn_beta"]])[None]

    consts = np.zeros((128, CST_W), np.float32)
    consts[:, CST_I:CST_I + 128] = np.eye(128)
    consts[0:TXT, CST_CAUSAL:CST_CAUSAL + TXT] = np.tril(np.ones((TXT, TXT)))
    consts[0:TXT, CST_NEG:CST_NEG + TXT] = NEG * (1 - np.tril(np.ones((TXT, TXT))))
    consts[:, CST_EVEN] = (np.arange(128) // HD) % 2 == 0
    consts[:, CST_ODD] = (np.arange(128) // HD) % 2 == 1
    consts[:, CST_PW:CST_PW + 2] = -0.5

    host = {
        "patches": patches.reshape(PK, B, 3 * IMG), "ids": x["x_txt"].T, "pos_ids": x["pos_S"][:, None],
        "mask": x["mask_BS_f1_0"].reshape(1, B * TXT), "tok_emb": x["L0_txt_tok_emb"], "pos_emb": x["L0_txt_pos_emb"],
        "w_a": np.stack(wa), "r_a": np.stack(ra), "w_b": np.stack(wb), "r_b": np.stack(rb),
        "w_c": np.stack(wc), "w_c2": np.stack(wc2), "r_c": np.stack(rc),
        "w_tok": x["L0_tok_W"].T.reshape(3, PK, D).transpose(1, 0, 2), "r_joint": r_joint,
        "w_joint": w_joint, "w_joint128": w_joint128, "consts": consts,
    }
    nc = bacc.Bacc("TRN2", target_bir_lowering=False, num_devices=1)
    arrays, args = {}, []
    for name, array in host.items():
        array = np.ascontiguousarray(array)
        arrays[f"in_{name}"] = array
        args.append(nc.dram_tensor(f"in_{name}", array.shape, mybir.dt.from_np(array.dtype), kind="ExternalInput").ap())
    args.append(nc.dram_tensor("out_0", (B, S, D), F32, kind="ExternalOutput").ap())
    args.append(nc.dram_tensor("h_text", (B, TXT, D), F32, kind="Internal").ap())
    args.append(nc.dram_tensor("pos_scratch", (2, IMG, NH * WIN), F32, kind="Internal").ap())
    early_fusion(nc, *args)
    result = run_bass_kernel_spmd(nc, [arrays], core_ids=[0])
    return result.results[0]["out_0"]
```
